# Optimizing a Trainium2 kernel written in Bass

```python
import numpy as np
import jax
import jax.numpy as jnp

def _softmax(x, axis=-1):
    return jax.nn.softmax(x, axis=axis)

def _gelu(x):
    return jax.nn.gelu(x, approximate=True)

def _silu(x):
    return jax.nn.silu(x)

def _sigmoid(x):
    return jax.nn.sigmoid(x)

def _layernorm(x, axis=-1, eps=1e-05):
    m = jnp.mean(x, axis=axis, keepdims=True)
    v = jnp.var(x, axis=axis, keepdims=True)
    return (x - m) / jnp.sqrt(v + eps)

def _scatter_add(tgt, idx, src, axis=0):
    return tgt.at[idx].add(src)

def _segment_sum(src, seg, n):
    return jax.ops.segment_sum(src, seg, n)
kernel_name = 'mk_gnn_resnorm_d4_gnn_r32_71d8be'

def setup_inputs(seed: int=0):
    np.random.seed(seed)
    _w = jnp.asarray

    def _rec_inputs():
        import jax
        import jax.numpy as jnp
        _gk = jax.random.key(seed)
        x = -0.000202 + 1 * jax.random.normal(jax.random.fold_in(_gk, 1), (3125, 128), jnp.float32)
        _s = jax.random.randint(jax.random.fold_in(_gk, 2), (25000,), 0, 3125, jnp.int32)
        _d = jax.random.randint(jax.random.fold_in(_gk, 3), (25000,), 0, 3125, jnp.int32)
        _loop = jnp.arange(3125, dtype=jnp.int32)
        src = jnp.concatenate([_s, _d, _loop])
        dst = jnp.concatenate([_d, _s, _loop])
        _o = jnp.argsort(dst, stable=True)
        src = src[_o]
        dst = dst[_o]
        edge_attr_128 = -8.16379e-05 + 0.999858 * jax.random.normal(jax.random.fold_in(_gk, 12), (53125, 128), jnp.float32)
        edge_type_4 = jax.random.randint(jax.random.fold_in(_gk, 14), (53125,), 0, 4, jnp.int32)
        return (x, src, dst, edge_attr_128, edge_type_4)
    x, src, dst, edge_attr_128, edge_type_4 = _rec_inputs()

    def _L0_gnn_setup():
        import jax, jax.numpy as jnp
        import numpy as np
        N_NODES = 50000
        N_EDGES = 25000
        DIM = 128
        N_LAYERS = 3

        def _sage_mean_layer(h, edge_src, edge_dst, deg):
            msg = h[edge_src]
            agg = jax.ops.segment_sum(msg, edge_dst, num_segments=h.shape[0])
            neigh = agg / deg[:, None]
            return h + neigh
        key = jax.random.key(seed)
        k1, k2, k3 = jax.random.split(key, 3)
        h = jax.random.normal(k1, (N_NODES, DIM), dtype=jnp.float32)
        edge_src = jax.random.randint(k2, (N_EDGES,), 0, N_NODES, dtype=jnp.int32)
        edge_dst = jax.random.randint(k3, (N_EDGES,), 0, N_NODES, dtype=jnp.int32)
        return {'h': h, 'edge_src': edge_src, 'edge_dst': edge_dst}
    _L0_gnn_all = _L0_gnn_setup()
    _L0_gnn_in = {k: v for k, v in _L0_gnn_all.items() if k in ()}
    del _L0_gnn_all

    def _L1_gnn_setup():
        import jax, jax.numpy as jnp
        import numpy as np
        EPS = 1e-07
        N_NODES, N_EDGES, D = (10000, 5000, 128)

        def mobius_add(x, y):
            x2 = jnp.sum(x * x, axis=-1, keepdims=True)
            y2 = jnp.sum(y * y, axis=-1, keepdims=True)
            xy = jnp.sum(x * y, axis=-1, keepdims=True)
            num = (1.0 + 2.0 * xy + y2) * x + (1.0 - x2) * y
            den = 1.0 + 2.0 * xy + x2 * y2
            return num / jnp.maximum(den, EPS)

        def mobius_scalar_mul(r, x):
            nrm = jnp.sqrt(jnp.sum(x * x, axis=-1, keepdims=True))
            nrm_c = jnp.clip(nrm, EPS, 1.0 - EPS)
            scaled = jnp.tanh(r * jnp.arctanh(nrm_c)) * (x / nrm_c)
            return jnp.where(nrm > EPS, scaled, jnp.zeros_like(x))
        key = jax.random.key(seed)
        kx, ke = jax.random.split(key)
        raw = jax.random.normal(kx, (N_NODES, D), dtype=jnp.float32)
        x = 0.4 * raw / (1.0 + jnp.linalg.norm(raw, axis=-1, keepdims=True))
        edge_index = jax.random.randint(ke, (2, N_EDGES), 0, N_NODES, dtype=jnp.int64)
        return {'x': x, 'edge_index': edge_index}
    _L1_gnn_all = _L1_gnn_setup()
    _L1_gnn_in = {k: v for k, v in _L1_gnn_all.items() if k in ()}
    del _L1_gnn_all

    def _L2_gnn_setup():
        import jax, jax.numpy as jnp
        import numpy as np
        N_NODES = 50000
        N_EDGES = 25000
        IN_CH = 128
        OUT_CH = 32
        HEADS = 4
        N_TYPES = 4
        N_CONF = 5
        key = jax.random.key(seed)
        ks = jax.random.split(key, 8)
        x = jax.random.normal(ks[0], (N_NODES, IN_CH), dtype=jnp.float32)
        edge_index = jax.random.randint(ks[1], (2, N_EDGES), 0, N_NODES, dtype=jnp.int32)
        edge_types = jax.random.randint(ks[2], (N_EDGES,), 0, N_TYPES, dtype=jnp.int32)
        D = OUT_CH * HEADS
        W = jax.random.normal(ks[3], (N_TYPES, IN_CH, D), dtype=jnp.float32) * (1.0 / np.sqrt(IN_CH))
        att_vectors = jax.random.normal(ks[4], (N_CONF, HEADS, 2 * OUT_CH), dtype=jnp.float32) * 0.1
        confounder_probs = jax.random.uniform(ks[5], (N_CONF,), dtype=jnp.float32)
        edge_importance = jnp.array([2.0, 1.5, 1.0, 0.5], dtype=jnp.float32)
        bias = jnp.zeros((D,), dtype=jnp.float32)
        return {'x': x, 'edge_index': edge_index, 'edge_types': edge_types, 'W': W, 'att_vectors': att_vectors, 'confounder_probs': confounder_probs, 'edge_importance': edge_importance, 'bias': bias}
    _L2_gnn_all = _L2_gnn_setup()
    _L2_gnn_in = {k: v for k, v in _L2_gnn_all.items() if k in ('W', 'att_vectors', 'confounder_probs', 'edge_importance', 'bias')}
    del _L2_gnn_all

    def _L3_gnn_setup():
        import jax, jax.numpy as jnp
        import numpy as np
        N_NODES = 6250
        N_EDGES = 25000
        D = 128
        key = jax.random.key(seed)
        ks = jax.random.split(key, 6)
        x = jax.random.normal(ks[0], (N_NODES, D), dtype=jnp.float32)
        edge_attr = jax.random.normal(ks[1], (N_EDGES, D), dtype=jnp.float32)
        edge_index = jax.random.randint(ks[2], (2, N_EDGES), 0, N_NODES, dtype=jnp.int64)
        W1 = jax.random.normal(ks[3], (2 * D, D), dtype=jnp.float32) * (1.0 / np.sqrt(2 * D))
        b1 = jnp.zeros((D,), dtype=jnp.float32)
        W2 = jax.random.normal(ks[4], (D, D), dtype=jnp.float32) * (1.0 / np.sqrt(D))
        b2 = jnp.zeros((D,), dtype=jnp.float32)
        return {'x': x, 'edge_attr': edge_attr, 'edge_index': edge_index, 'W1': W1, 'b1': b1, 'W2': W2, 'b2': b2}
    _L3_gnn_all = _L3_gnn_setup()
    _L3_gnn_in = {k: v for k, v in _L3_gnn_all.items() if k in ('W1', 'b1', 'W2', 'b2')}
    del _L3_gnn_all
    return {'x': x, 'src': src, 'dst': dst, 'edge_attr_128': edge_attr_128, 'edge_type_4': edge_type_4, 'L2_gnn_W': _L2_gnn_in['W'], 'L2_gnn_att_vectors': _L2_gnn_in['att_vectors'], 'L2_gnn_confounder_probs': _L2_gnn_in['confounder_probs'], 'L2_gnn_edge_importance': _L2_gnn_in['edge_importance'], 'L2_gnn_bias': _L2_gnn_in['bias'], 'L3_gnn_W1': _L3_gnn_in['W1'], 'L3_gnn_b1': _L3_gnn_in['b1'], 'L3_gnn_W2': _L3_gnn_in['W2'], 'L3_gnn_b2': _L3_gnn_in['b2']}

def reference(x, src, dst, edge_attr_128, edge_type_4, L2_gnn_W, L2_gnn_att_vectors, L2_gnn_confounder_probs, L2_gnn_edge_importance, L2_gnn_bias, L3_gnn_W1, L3_gnn_b1, L3_gnn_W2, L3_gnn_b2):
    import jax
    import jax.numpy as jnp

    def _L0_gnn_ref(h, edge_src, edge_dst):
        import jax, jax.numpy as jnp
        import numpy as np
        N_NODES = 50000
        N_EDGES = 25000
        DIM = 128
        N_LAYERS = 3

        def _sage_mean_layer(h, edge_src, edge_dst, deg):
            msg = h[edge_src]
            agg = jax.ops.segment_sum(msg, edge_dst, num_segments=h.shape[0])
            neigh = agg / deg[:, None]
            return h + neigh
        n = h.shape[0]
        deg = jax.ops.segment_sum(jnp.ones((edge_dst.shape[0],), dtype=h.dtype), edge_dst, num_segments=n)
        deg = jnp.maximum(deg, 1.0)
        res = h
        tmp = h
        for i in range(N_LAYERS):
            tmp = _sage_mean_layer(tmp, edge_src, edge_dst, deg)
            res = res + tmp / (1.0 + i)
        return res

    def _L1_gnn_ref(x, edge_index):
        import jax, jax.numpy as jnp
        import numpy as np
        EPS = 1e-07
        N_NODES, N_EDGES, D = (10000, 5000, 128)

        def mobius_add(x, y):
            x2 = jnp.sum(x * x, axis=-1, keepdims=True)
            y2 = jnp.sum(y * y, axis=-1, keepdims=True)
            xy = jnp.sum(x * y, axis=-1, keepdims=True)
            num = (1.0 + 2.0 * xy + y2) * x + (1.0 - x2) * y
            den = 1.0 + 2.0 * xy + x2 * y2
            return num / jnp.maximum(den, EPS)

        def mobius_scalar_mul(r, x):
            nrm = jnp.sqrt(jnp.sum(x * x, axis=-1, keepdims=True))
            nrm_c = jnp.clip(nrm, EPS, 1.0 - EPS)
            scaled = jnp.tanh(r * jnp.arctanh(nrm_c)) * (x / nrm_c)
            return jnp.where(nrm > EPS, scaled, jnp.zeros_like(x))
        src, dst = (edge_index[0], edge_index[1])
        n, d = x.shape
        messages = mobius_add(x[src], -x[dst])

        def body(out, em):
            m, idx = em
            return (out.at[idx].set(mobius_add(out[idx], m)), None)
        out0 = jnp.zeros((n, d), dtype=x.dtype)
        total, _ = jax.lax.scan(body, out0, (messages, dst))
        count = jnp.zeros((n,), dtype=x.dtype).at[dst].add(1.0)
        scale = 1.0 / jnp.maximum(count, 1.0)
        aggr = mobius_scalar_mul(scale[:, None], total)
        return mobius_add(x, aggr)

    def _L2_gnn_ref(x, edge_index, edge_types, W, att_vectors, confounder_probs, edge_importance, bias):
        import jax, jax.numpy as jnp
        import numpy as np
        N_NODES = 50000
        N_EDGES = 25000
        IN_CH = 128
        OUT_CH = 32
        HEADS = 4
        N_TYPES = 4
        N_CONF = 5
        N = x.shape[0]
        T = W.shape[0]
        K, H, C2 = att_vectors.shape
        C = C2 // 2
        src = edge_index[0]
        dst = edge_index[1]
        et = edge_types.astype(jnp.int32)
        xt = jnp.einsum('ni,tio->tno', x, W)
        xj = xt[et, src].reshape(-1, H, C)
        xi = xt[et, dst].reshape(-1, H, C)
        x_cat = jnp.concatenate([xi, xj], axis=-1)
        scores = jnp.einsum('ehd,khd->ehk', x_cat, att_vectors)
        scores = jax.nn.leaky_relu(scores, negative_slope=0.2)
        pk = jax.nn.softmax(confounder_probs)
        alpha = jnp.einsum('ehk,k->eh', scores, pk)
        seg = et * N + dst
        n_seg = T * N
        m = jax.ops.segment_max(alpha, seg, num_segments=n_seg)
        a = jnp.exp(alpha - m[seg])
        denom = jax.ops.segment_sum(a, seg, num_segments=n_seg)
        alpha_n = a / denom[seg]
        msg = (xj * alpha_n[..., None]).reshape(-1, H * C)
        msg = msg * edge_importance[et][:, None]
        out = jax.ops.segment_sum(msg, dst, num_segments=N)
        out = out + x @ W[0] + bias
        return out

    def _L3_gnn_ref(x, edge_attr, edge_index, W1, b1, W2, b2):
        import jax, jax.numpy as jnp
        import numpy as np
        N_NODES = 6250
        N_EDGES = 25000
        D = 128
        receivers = edge_index[1]
        agg = jax.ops.segment_sum(edge_attr, receivers, num_segments=x.shape[0])
        node_inputs = jnp.concatenate([x, agg], axis=-1)
        h = jax.nn.relu(node_inputs @ W1 + b1)
        x_new = h @ W2 + b2
        return x_new
    edge_index = jnp.stack([src, dst])
    x = _layernorm(x + _L0_gnn_ref(x, src, dst), axis=-1)
    x = _layernorm(x + _L1_gnn_ref(x, edge_index), axis=-1)
    x = _layernorm(x + _L2_gnn_ref(x, edge_index, edge_type_4, L2_gnn_W, L2_gnn_att_vectors, L2_gnn_confounder_probs, L2_gnn_edge_importance, L2_gnn_bias), axis=-1)
    x = _layernorm(x + _L3_gnn_ref(x, edge_attr_128, edge_index, L3_gnn_W1, L3_gnn_b1, L3_gnn_W2, L3_gnn_b2), axis=-1)
    return x

_drawn_inputs = setup_inputs


def setup_inputs(seed=0):
    import zlib

    import numpy as np

    out = dict(_drawn_inputs(seed))
    spreads = {'L2_gnn_bias': (0.0, 0.366), 'L3_gnn_b1': (0.0, 0.1), 'L3_gnn_b2': (0.0, 0.1)}
    factors = {'L2_gnn_confounder_probs': 7.951}
    for name, (base, spread) in spreads.items():
        noise = np.random.default_rng([zlib.crc32(name.encode()), seed]).standard_normal(out[name].shape)
        drawn = base * np.exp(spread * noise) if base else spread * noise
        out[name] = jnp.asarray(drawn.astype(out[name].dtype))
    for name, factor in factors.items():
        out[name] = (out[name] * factor).astype(out[name].dtype)
    return out
```

```python
from contextlib import ExitStack

import concourse.bass as bass
from concourse import mybir

F32 = mybir.dt.float32
BF16 = mybir.dt.bfloat16
I32 = mybir.dt.int32
ALU = mybir.AluOpType
ACT = mybir.ActivationFunctionType
AX = mybir.AxisListType

P = 128
LN_EPS = 1e-5
MOB_EPS = 1e-7
NEG = -1e30

G = 5
RB = 4
SLOTS = RB * G
W = 32
UPW = W // RB
AR = 8
HIST_COLS = 25


class Steps:

    def __init__(self, eng, sem):
        self.eng, self.sem, self.n = eng, sem, 0

    def restart(self):
        self.eng.sem_clear(self.sem)
        self.n = 0

    def go(self, ins):
        self.n += 1
        ins.then_inc(self.sem, 1)
        return self.n

    def link(self, ins):
        self.go(ins)
        self.eng.wait_ge(self.sem, self.n)

    def need(self, n):
        self.eng.wait_ge(self.sem, n)


def build_program(nc, x, src, dst, edge_attr, edge_type, W2n, att, conf, importance, bias2,
                  W1m, b1m, W2m, b2m, out):
    N, D = x.shape
    E = src.shape[0]
    NTILE = -(-N // P)
    NP = NTILE * P
    NGRP = NTILE // G
    T, H, K = W2n.shape[0], att.shape[1], att.shape[0]
    C = D // H
    HK = H * K
    LD = E // 125
    assert NTILE % G == 0 and E % 125 == 0 and D == P and NP > N and LD % HIST_COLS == 0
    NCHUNK = LD // HIST_COLS
    deg_max = [E] + [E // (g * G * P) for g in range(1, NGRP)]
    NU = sum(-(-d // RB) + 1 for d in deg_max)
    NWIN = [-(-d // W) + 1 for d in deg_max]
    ATT_TURNS = [-(-d // AR) + 1 for d in deg_max]
    MW = D + 4
    TW = D + HK + T

    def dram(name, shape, dt=F32):
        return nc.dram_tensor(name, shape, dt, kind="Internal").ap()

    node_tab = dram("node_tab", [NP, 4], I32)
    h_tab = [dram(f"h_tab{i}", [NP, D]) for i in range(3)]
    m_tab = dram("m_tab", [NP, MW])
    t_tab = dram("t_tab", [NP, T * TW])
    src_pad = dram("src_pad", [E + W], I32)
    type_pad = dram("type_pad", [E + W], I32)
    unit_hi = [sum(-(-d // RB) + 1 for d in deg_max[:g]) for g in range(NGRP + 1)]
    NLIST = max(unit_hi[g] + NWIN[g] * UPW for g in range(NGRP)) + 1
    slot_node = dram("slot_node", [NLIST, P, SLOTS], I32)
    slot_typed = dram("slot_typed", [NLIST, P, SLOTS], I32)

    def flat(ap):
        names = "abcd"[:len(ap.shape)]
        ap = ap.rearrange(" ".join(names) + " -> (" + " ".join(names) + ")") if len(ap.shape) > 1 else ap
        return ap.rearrange("(n o) -> n o", o=1)

    ctx = ExitStack()
    with ctx:
        made = {}

        def unique(name):
            made[name] = made.get(name, 0) + 1
            return name if made[name] == 1 else f"{name}_{made[name]}"

        def sb(name, shape, dt=F32, c=ctx):
            return c.enter_context(nc.sbuf_tensor(unique(name), shape, dt))

        def psum(name, shape, c):
            return c.enter_context(nc.psum_tensor(unique(name), shape, F32))

        def sem(name, c):
            return c.enter_context(nc.semaphore(unique(name)))

        X = sb("X", [P, NTILE, D])
        RES = sb("RES", [P, NTILE, D])
        O = sb("O", [P, NTILE, D])
        node = sb("node", [P, NTILE, 4], I32)
        nodef = sb("nodef", [P, NTILE, 4])
        rdeg = sb("rdeg", [P, NTILE])
        real = sb("real", [P, NTILE])
        ctl = sb("ctl", [1, 64], I32)
        ident = sb("ident", [P, P])
        zeros = sb("zeros", [P, 4 * P])
        iota_w = sb("iota_w", [P, W])
        d2 = sb("d2", [P, NTILE])
        UB, WB, AB = 0, 8, 16

        def bounds(eng, at, n, lo, hi):
            return [eng.value_load(ctl[0:1, at + i:at + i + 1], min_val=lo[i], max_val=hi[i]) for i in range(n)]

        def unit_bounds(eng):
            return bounds(eng, UB, NGRP + 1, list(range(NGRP + 1)), unit_hi)

        with ExitStack() as c0:
            cnt = sb("cnt", [P, NTILE], F32, c0)
            low = sb("low", [P, P], F32, c0)
            high = sb("high", [P, P], F32, c0)
            ones = sb("ones", [P, P], F32, c0)
            nodeid = sb("nodeid", [P, NTILE], I32, c0)
            dsts = sb("dsts", [125, LD], I32, c0)
            dlo = sb("dlo", [125, LD], I32, c0)
            dhi = sb("dhi", [125, LD], I32, c0)
            dlof = sb("dlof", [125, LD], BF16, c0)
            dhif = sb("dhif", [125, LD], BF16, c0)
            iol = sb("iol", [P, P], BF16, c0)
            zi = sb("zi", [1, W], I32, c0)
            with ExitStack() as c1, nc.Block() as block:
                masked, filled, loaded, copied, split, cleared = (
                    sem(n, c1) for n in ("masked", "filled", "loaded", "copied", "split", "cleared"))

                @block.gpsimd
                def _(pool):
                    pool.memset(ident[:], 0.0).then_inc(filled, 1)
                    pool.memset(low[:], 1.0).then_inc(filled, 1)
                    pool.memset(high[:], 1.0).then_inc(filled, 1)
                    pool.wait_ge(filled, 3)
                    pool.affine_select(out=ident[:], in_=ident[:], compare_op=ALU.not_equal, fill=1.0, base=0,
                                       pattern=[[-1, P]], channel_multiplier=1).then_inc(masked, 1)
                    pool.affine_select(out=low[:], in_=low[:], compare_op=ALU.is_gt, fill=0.0, base=0,
                                       pattern=[[-1, P]], channel_multiplier=1).then_inc(masked, 1)
                    pool.affine_select(out=high[:], in_=high[:], compare_op=ALU.is_gt, fill=0.0, base=0,
                                       pattern=[[1, P]], channel_multiplier=-1).then_inc(masked, 1)
                    pool.iota(nodeid[:], pattern=[[P, NTILE]], base=0, channel_multiplier=1).then_inc(masked, 1)
                    pool.iota(iota_w[:], pattern=[[1, W]], base=0, channel_multiplier=0,
                              allow_small_or_imprecise_dtypes=True).then_inc(masked, 1)
                    pool.iota(iol[:], pattern=[[1, P]], base=0, channel_multiplier=0,
                              allow_small_or_imprecise_dtypes=True).then_inc(masked, 1)

                @block.sync
                def _(sp):
                    sp.dma_start(dsts[:], dst.rearrange("(p n) -> p n", p=125)).then_inc(loaded, 16)
                    sp.dma_start(src_pad[0:E].rearrange("(p n) -> p n", p=125),
                                 src.rearrange("(p n) -> p n", p=125)).then_inc(copied, 16)
                    sp.dma_start(type_pad[0:E].rearrange("(p n) -> p n", p=125),
                                 edge_type.rearrange("(p n) -> p n", p=125)).then_inc(copied, 16)
                    sp.dma_start(h_tab[0][0:N, :], x).then_inc(copied, 16)
                    sp.wait_ge(cleared, 2)
                    sp.dma_start(src_pad[E:E + W].rearrange("(o n) -> o n", o=1), zi[:]).then_inc(copied, 16)
                    sp.dma_start(type_pad[E:E + W].rearrange("(o n) -> o n", o=1), zi[:]).then_inc(copied, 16)
                    sp.dma_start(h_tab[0][N:NP, :], zeros[0:NP - N, 0:D]).then_inc(copied, 16)
                    sp.wait_ge(copied, 96)

                @block.vector
                def _(dve):
                    dve.memset(zeros[:], 0.0).then_inc(cleared, 1)
                    dve.memset(zi[:], 0).then_inc(cleared, 1)
                    dve.memset(ones[:], 1.0).then_inc(split, 1)
                    dve.wait_ge(loaded, 16)
                    dve.tensor_scalar(dlo[:], dsts[:], P - 1, None, ALU.bitwise_and).then_inc(split, 1)
                    dve.tensor_scalar(dhi[:], dsts[:], 7, None, ALU.arith_shift_right).then_inc(split, 1)
                    dve.wait_ge(split, 3)
                    dve.tensor_copy(dlof[:], dlo[:]).then_inc(split, 1)
                    dve.tensor_copy(dhif[:], dhi[:]).then_inc(split, 1)

            with ExitStack() as c1:
                hlo = [sb(f"hlo{i}", [125, HIST_COLS, P], BF16, c1) for i in range(2)]
                hhi = [sb(f"hhi{i}", [125, HIST_COLS, NTILE], BF16, c1) for i in range(2)]
                zb = sb("zb", [P, P], BF16, c1)
                count_ps = psum("count_ps", [P, 512], c1)
                zeroed = sem("zeroed", c1)
                hot = [sem(f"hot{i}", c1) for i in range(2)]
                hot_used = [sem(f"hot_used{i}", c1) for i in range(2)]
                counted, degrees = sem("counted", c1), sem("degrees", c1)
                PAIRS = NCHUNK // 2

                def at(i, b):
                    return bass.ds(i * (2 * HIST_COLS) + b * HIST_COLS, HIST_COLS)

                def last_chunk():
                    return bass.ds(2 * PAIRS * HIST_COLS, HIST_COLS)

                with nc.Block() as block:
                    @block.vector
                    def _(dve):
                        def one_hots(b, cols):
                            dve.tensor_tensor(
                                hlo[b][:], iol[0:125, :].unsqueeze(1).to_broadcast([125, HIST_COLS, P]),
                                dlof[:, cols].unsqueeze(2).to_broadcast([125, HIST_COLS, P]), ALU.is_equal,
                            ).then_inc(hot[b], 1)
                            dve.tensor_tensor(
                                hhi[b][:], iol[0:125, 0:NTILE].unsqueeze(1).to_broadcast([125, HIST_COLS, NTILE]),
                                dhif[:, cols].unsqueeze(2).to_broadcast([125, HIST_COLS, NTILE]), ALU.is_equal,
                            ).then_inc(hot[b], 1)

                        dve.memset(zb[:], 0.0).then_inc(zeroed, 1)
                        with dve.Fori(0, PAIRS) as i:
                            for b in range(2):
                                dve.wait_ge(hot_used[b], i + 1)
                                one_hots(b, at(i, b))
                        dve.wait_ge(hot_used[0], PAIRS + 1)
                        one_hots(0, last_chunk())
                        dve.wait_ge(counted, 1)
                        dve.tensor_copy(cnt[:], count_ps[:, 0:NTILE]).then_inc(degrees, 1)

                    @block.tensor
                    def _(pe):
                        def products(b):
                            for j in range(HIST_COLS):
                                mm = pe.matmul(count_ps[:, 0:NTILE], hlo[b][:, j, :], hhi[b][:, j, :],
                                               start=False, stop=False, skip_group_check=True)
                            return mm

                        for b in range(2):
                            pe.sem_inc(hot_used[b], 1)
                        pe.wait_ge(zeroed, 1)
                        pe.matmul(count_ps[:, :], zb[:], zeros[:].bitcast(BF16)[:, 0:512], start=True, stop=False,
                                  skip_group_check=True)
                        with pe.Fori(0, PAIRS) as i:
                            for b in range(2):
                                pe.wait_ge(hot[b], 2 * i + 2)
                                products(b).then_inc(hot_used[b], 1)
                        pe.wait_ge(hot[0], 2 * PAIRS + 2)
                        products(0).then_inc(counted, 1)

            with ExitStack() as c1:
                diag = sb("diag", [P, NTILE, P], F32, c1)
                drow = sb("drow", [P, NP], F32, c1)
                junk = sb("junk", [P, NP], F32, c1)
                tots = sb("tots", [P, NTILE], F32, c1)
                incl = sb("incl", [P, NTILE], F32, c1)
                onesc = sb("onesc", [P, NTILE], F32, c1)
                firstf = sb("firstf", [P, NTILE], F32, c1)
                part = sb("part", [P, 4, NTILE], F32, c1)
                posf = sb("posf", [P, NTILE], F32, c1)
                pos = sb("pos", [P, NTILE], I32, c1)
                rec = sb("rec", [P, NTILE, 4], I32, c1)
                cf = sb("cf", [1, 64], F32, c1)
                ci = sb("ci", [1, 64], I32, c1)
                row_ps = psum("row_ps", [P, 7 * 512], c1)
                pre_ps = psum("pre_ps", [P, 512], c1)
                diag_made, row_made, row_kept, prefixed, ordered, placed, read_back, own = (
                    sem(n, c1) for n in ("diag_made", "row_made", "row_kept", "prefixed", "ordered",
                                         "placed", "read_back", "own"))
                with nc.Block() as block:
                    @block.tensor
                    def _(pe):
                        pe.matmul(pre_ps[:, 0:NTILE], high[:], cnt[:], start=True, stop=True)
                        pe.matmul(pre_ps[:, 32:32 + NTILE], ones[:], cnt[:], start=True, stop=True).then_inc(prefixed, 1)
                        pe.wait_ge(diag_made, 1)
                        df = diag[:].rearrange("p t j -> p (t j)")
                        for b in range(-(-NP // 512)):
                            e = min(NP, 512 * b + 512)
                            mm = pe.matmul(row_ps[:, 512 * b:e], ones[:], df[:, 512 * b:e], start=True, stop=True)
                            mm.then_inc(row_made, 1)

                    @block.scalar
                    def _(act):
                        for b in range(-(-NP // 512)):
                            e = min(NP, 512 * b + 512)
                            act.wait_ge(row_made, b + 1)
                            act.activation(drow[:, 512 * b:e], row_ps[:, 512 * b:e], ACT.Copy).then_inc(row_kept, 1)

                    @block.vector
                    def _(dve):
                        s = Steps(dve, own)
                        dve.tensor_tensor(diag[:], ident[:].unsqueeze(1).to_broadcast([P, NTILE, P]),
                                          cnt[:].unsqueeze(2).to_broadcast([P, NTILE, P]), ALU.mult).then_inc(diag_made, 1)
                        s.link(dve.memset(onesc[:], 1.0))
                        s.link(dve.memset(part[:], 0.0))
                        dve.wait_ge(prefixed, 1)
                        s.link(dve.tensor_copy(tots[:], pre_ps[:, 32:32 + NTILE]))
                        s.link(dve.tensor_tensor_scan(incl[:], onesc[:], tots[:], 0.0, ALU.mult, ALU.add))
                        s.link(dve.tensor_tensor(incl[:], incl[:], tots[:], ALU.subtract))
                        s.link(dve.tensor_tensor(firstf[:], incl[:], pre_ps[:, 0:NTILE], ALU.add))
                        dve.wait_ge(row_kept, -(-NP // 512))
                        for t in range(NTILE):
                            mine = drow[:, t * P:(t + 1) * P]
                            deg = cnt[:, t:t + 1]
                            if t:
                                s.go(dve.tensor_scalar(junk[:, 0:t * P], drow[:, 0:t * P], deg, 0.0, ALU.is_ge, ALU.add,
                                                       accum_out=part[:, 0, t:t + 1]))
                            if t < NTILE - 1:
                                s.go(dve.tensor_scalar(junk[:, (t + 1) * P:], drow[:, (t + 1) * P:], deg, 0.0,
                                                       ALU.is_gt, ALU.add, accum_out=part[:, 1, t:t + 1]))
                            s.go(dve.scalar_tensor_tensor(out=diag[:, 0, :], in0=mine, scalar=deg, in1=low[:],
                                                          op0=ALU.is_ge, op1=ALU.mult, accum_out=part[:, 2, t:t + 1]))
                            s.link(dve.scalar_tensor_tensor(out=diag[:, 1, :], in0=mine, scalar=deg, in1=high[:],
                                                            op0=ALU.is_gt, op1=ALU.mult, accum_out=part[:, 3, t:t + 1]))
                        s.link(dve.tensor_reduce(posf[:], part[:].rearrange("p a t -> p t a"), AX.X, ALU.add))
                        s.go(dve.tensor_copy(pos[:], posf[:]))
                        s.go(dve.memset(rec[:], 0))
                        s.need(s.n)
                        s.go(dve.tensor_copy(rec[:, :, 0], firstf[:]))
                        s.go(dve.tensor_copy(rec[:, :, 1], cnt[:]))
                        s.go(dve.tensor_copy(rec[:, :, 2], nodeid[:]))
                        s.need(s.n)
                        dve.sem_inc(ordered, 1)
                        dve.wait_ge(read_back, 16)
                        s.link(dve.tensor_copy(nodef[:], node[:]))
                        s.link(dve.tensor_scalar(rdeg[:], nodef[:, :, 1], 1.0, None, ALU.max))
                        s.link(dve.reciprocal(rdeg[:], rdeg[:]))
                        s.link(dve.tensor_scalar(real[:], nodef[:, :, 2], float(N), None, ALU.is_lt))
                        top = node[0:1, 0:NTILE:G, 1]
                        for at0, span in ((UB, RB), (AB, AR), (24, W)):
                            raw = ci[:, at0:at0 + NGRP]
                            s.link(dve.tensor_copy(raw, top))
                            s.link(dve.tensor_scalar(raw, raw, span - 1, None, ALU.add))
                            s.link(dve.tensor_scalar(raw, raw, span.bit_length() - 1, None, ALU.arith_shift_right))
                            s.link(dve.tensor_scalar(raw, raw, 1, None, ALU.max))
                        s.link(dve.memset(ctl[:], 0))
                        s.link(dve.tensor_copy(ctl[:, WB:WB + NGRP], ci[:, 24:24 + NGRP]))
                        for at0 in (UB, AB):
                            s.link(dve.tensor_copy(cf[:, at0:at0 + NGRP], ci[:, at0:at0 + NGRP]))
                            s.link(dve.tensor_tensor_scan(cf[:, 32 + at0:32 + at0 + NGRP], onesc[0:1, 0:NGRP],
                                                          cf[:, at0:at0 + NGRP], 0.0, ALU.mult, ALU.add))
                            s.link(dve.tensor_copy(ctl[:, at0 + 1:at0 + 1 + NGRP], cf[:, 32 + at0:32 + at0 + NGRP]))

                    @block.gpsimd
                    def _(pool):
                        pool.wait_ge(ordered, 1)
                        for t in range(NTILE):
                            pool.indirect_dma_start(node_tab, bass.IndirectOffsetOnAxis(ap=pos[:, t:t + 1], axis=0),
                                                    rec[:, t, :], None).then_inc(placed, 16)

                    @block.sync
                    def _(sp):
                        sp.wait_ge(placed, 16 * NTILE)
                        sp.dma_start(node[:], node_tab.rearrange("(t p) c -> p t c", p=P)).then_inc(read_back, 16)
                        sp.wait_ge(read_back, 16)

        with ExitStack() as c1:
            offi = sb("offi", [P, G], I32, c1)
            off = sb("off", [P, G], F32, c1)
            wsrc = sb("wsrc", [P, G, W], I32, c1)
            wtyp = sb("wtyp", [P, G, W], I32, c1)
            end = sb("end", [P, NTILE], F32, c1)
            start_of = sb("start_of", [P, NTILE], F32, c1)
            val = sb("val", [P, G, W], F32, c1)
            tf = sb("tf", [P, G, W], F32, c1)
            sf = sb("sf", [P, G, W], F32, c1)
            pn = sb("pn", [P, UPW, RB, G], I32, c1)
            pt = sb("pt", [P, UPW, RB, G], I32, c1)
            offsets, windows, listed, written, list_free, own, gone, features, marker = (
                sem(n, c1) for n in ("offsets", "windows", "listed", "written", "list_free", "own", "gone",
                                     "features", "marker"))
            with nc.Block() as block:
                def each_turn(eng, body):
                    wn = bounds(eng, WB, NGRP, [1] * NGRP, NWIN)
                    ub = unit_bounds(eng)
                    first = 0
                    for g in range(NGRP):
                        with eng.Fori(0, wn[g]) as w:
                            body(g, w, first + w, ub[g])
                        first = first + wn[g]
                    return first

                @block.gpsimd
                def _(pool):
                    for t in range(NTILE):
                        pool.indirect_dma_start(X[:, t, :], None, h_tab[0],
                                                bass.IndirectOffsetOnAxis(ap=node[:, t, 2:3], axis=0)).then_inc(features, 16)

                    def body(g, w, turn, u0):
                        pool.wait_ge(offsets, turn + 1)
                        pool.sem_inc(marker, 1)
                        for k in range(G):
                            pool.indirect_dma_start(wsrc[:, k, :], None, flat(src_pad),
                                                    bass.IndirectOffsetOnAxis(ap=offi[:, k:k + 1], axis=0)).then_inc(windows, 16)
                            pool.indirect_dma_start(wtyp[:, k, :], None, flat(type_pad),
                                                    bass.IndirectOffsetOnAxis(ap=offi[:, k:k + 1], axis=0)).then_inc(windows, 16)

                    each_turn(pool, body)
                    pool.wait_ge(features, 16 * NTILE)

                @block.vector
                def _(dve):
                    s = Steps(dve, own)
                    dve.tensor_tensor(end[:], nodef[:, :, 0], nodef[:, :, 1], ALU.add).then_inc(gone, 1)
                    dve.wait_ge(gone, 1)

                    def body(g, w, turn, u0):
                        s.restart()
                        cols = slice(g * G, (g + 1) * G)
                        s.link(dve.tensor_scalar(off[:], start_of[:, cols], float(E), None, ALU.min))
                        dve.tensor_copy(offi[:], off[:]).then_inc(offsets, 1)
                        s.link(dve.tensor_tensor(val[:], iota_w[:].unsqueeze(1).to_broadcast([P, G, W]),
                                                 off[:].unsqueeze(2).to_broadcast([P, G, W]), ALU.add))
                        s.link(dve.tensor_tensor(val[:], val[:], end[:, cols].unsqueeze(2).to_broadcast([P, G, W]), ALU.is_lt))
                        s.link(dve.tensor_scalar(start_of[:, cols], start_of[:, cols], float(W), None, ALU.add))
                        dve.wait_ge(windows, (turn + 1) * (2 * G * 16))
                        dve.wait_ge(list_free, turn + 1)
                        s.link(dve.tensor_copy(sf[:], wsrc[:]))
                        s.link(dve.tensor_copy(tf[:], wtyp[:]))
                        s.link(dve.scalar_tensor_tensor(out=tf[:], in0=sf[:], scalar=float(T), in1=tf[:], op0=ALU.mult, op1=ALU.add))
                        s.link(dve.tensor_scalar(sf[:], sf[:], float(-N), None, ALU.add))
                        s.link(dve.tensor_scalar(tf[:], tf[:], float(-N * T), None, ALU.add))
                        s.link(dve.tensor_tensor(sf[:], sf[:], val[:], ALU.mult))
                        s.link(dve.tensor_tensor(tf[:], tf[:], val[:], ALU.mult))
                        for a, b, plus in ((pn, sf, N), (pt, tf, N * T)):
                            s.link(dve.tensor_scalar(a[:].rearrange("p u r k -> p (u r) k"), b[:].rearrange("p k w -> p w k"),
                                                     float(plus), None, ALU.add))
                        dve.sem_inc(listed, 1)

                    dve.tensor_copy(start_of[:], nodef[:, :, 0]).then_inc(gone, 1)
                    dve.wait_ge(gone, 2)
                    each_turn(dve, body)

                @block.sync
                def _(sp):
                    def body(g, w, turn, u0):
                        sp.wait_ge(listed, turn + 1)
                        at = bass.ds(u0 + w * UPW, UPW)
                        sp.dma_start(slot_node[at].rearrange("u p s -> p u s"),
                                     pn[:].rearrange("p u r k -> p u (r k)")).then_inc(written, 16)
                        sp.dma_start(slot_typed[at].rearrange("u p s -> p u s"),
                                     pt[:].rearrange("p u r k -> p u (r k)")).then_inc(written, 16)
                        sp.wait_ge(written, (turn + 1) * 32)
                        sp.sem_inc(list_free, 1)

                    sp.sem_inc(list_free, 1)
                    turns = each_turn(sp, body)
                    past = bass.ds(bounds(sp, UB + NGRP, 1, [NGRP], [unit_hi[NGRP]])[0], 1)
                    for lists, mine in ((slot_node, pn), (slot_typed, pt)):
                        sp.dma_start(lists[past].rearrange("u p s -> p (u s)"),
                                     mine[:, 0].rearrange("p r k -> p (r k)")).then_inc(written, 16)
                    sp.wait_ge(written, turns * 32 + 32)
                    sp.sem_inc(marker, 1)

        def load_slots(sp, lists, slot, slots_in, rows_in):
            units = bounds(sp, UB + NGRP, 1, [NGRP], [unit_hi[NGRP]])[0]

            def load(u, q):
                sp.dma_start(slot[q][:], lists[bass.ds(u, 1), :, q * G:(q + 1) * G]
                             .rearrange("o p k -> (o p) k")).then_inc(slots_in[q], 16)

            for q in range(RB):
                load(0, q)
            with sp.Fori(0, units) as u:
                for q in range(RB):
                    sp.wait_ge(rows_in[q], (16 * G) * u + 16 * G)
                    load(u + 1, q)
            for q in range(RB):
                sp.wait_ge(slots_in[q], 16 * units + 16)
                sp.sem_inc(pass_marker, 1)

        def gather_unit(pool, u, table, slot, rows, slots_in, rows_in, rows_free, marker):
            for q in range(RB):
                pool.wait_ge(slots_in[q], 16 * u + 16)
                pool.wait_ge(rows_free[q], u + 1)
                pool.sem_inc(marker, 1)
                for k in range(G):
                    pool.indirect_dma_start(rows[q][:, k, :], None, table,
                                            bass.IndirectOffsetOnAxis(ap=slot[q][:, k:k + 1], axis=0)
                                            ).then_inc(rows_in[q], 16)

        def scatter_group(pool, g, table, rows_of, stored):
            for k in range(G):
                t = g * G + k
                pool.indirect_dma_start(table, bass.IndirectOffsetOnAxis(ap=node[:, t, 2:3], axis=0),
                                        rows_of(t), None).then_inc(stored, 16)

        pass_sems = [[sem(f"{name}{q}", ctx) for q in range(RB)] for name in ("slots_in", "rows_free")]
        pass_marker = sem("pass_marker", ctx)
        passes = [0]

        def pass_memory(c, width):
            if passes[0]:
                with nc.Block() as block:
                    @block.sync
                    def _(sp):
                        for one in (*pass_sems[0], *pass_sems[1], pass_marker):
                            sp.sem_clear(one)
            passes[0] += 1
            rows = [sb(f"rows{q}", [P, G, width], F32, c) for q in range(RB)]
            slot = [sb(f"slot{q}", [P, G], I32, c) for q in range(RB)]
            rows_in = [sem(f"rows_in{q}", ctx) for q in range(RB)]
            return rows, slot, pass_sems[0], rows_in, pass_sems[1], pass_marker

        def add_rows(pe, acc, rows, start=False):
            pe.matmul(acc[:, 0:4 * P].rearrange("p (k d) -> p k d", k=4), ident[:], rows[:, 0:4, 0:D],
                      start=start, stop=False, skip_group_check=True)
            return pe.matmul(acc[:, 4 * P:5 * P], ident[:], rows[:, 4, 0:D], start=start, stop=False,
                             skip_group_check=True)

        def clear_sums(pe, acc):
            pe.matmul(acc[:, 0:4 * P], ident[:], zeros[:], start=True, stop=False, skip_group_check=True)
            pe.matmul(acc[:, 4 * P:5 * P], ident[:], zeros[:, 0:P], start=True, stop=False, skip_group_check=True)

        def cols(g):
            return slice(g * G, (g + 1) * G)

        def wide(ap, n=D):
            return ap.unsqueeze(2).to_broadcast([P, G, n])

        def normalise(s, dve, act_std, g, A, B, st, std_in, std_out, turn):
            a, b = A[:, cols(g), :], B[:]
            s.link(dve.tensor_reduce(st[:, 0, :], a, AX.X, ALU.add))
            s.link(dve.tensor_scalar(st[:, 0, :], st[:, 0, :], 1.0 / D, None, ALU.mult))
            s.link(dve.tensor_tensor(a, a, wide(st[:, 0, :]), ALU.subtract))
            s.link(dve.tensor_tensor(b, a, a, ALU.mult))
            s.link(dve.tensor_reduce(st[:, 1, :], b, AX.X, ALU.add))
            dve.tensor_scalar(st[:, 1, :], st[:, 1, :], 1.0 / D, LN_EPS, ALU.mult, ALU.add).then_inc(std_in, 1)
            dve.wait_ge(std_out, turn + 1)
            s.link(dve.reciprocal(st[:, 3, :], st[:, 2, :]))
            s.link(dve.tensor_tensor(a, a, wide(st[:, 3, :]), ALU.mult))

        def roots(act, st, std_in, std_out, turn):
            act.wait_ge(std_in, turn + 1)
            act.activation(st[:, 2, :], st[:, 1, :], ACT.Sqrt).then_inc(std_out, 1)

        for layer in range(3):
            with ExitStack() as c1:
                rows, slot, slots_in, rows_in, rows_free, marker = pass_memory(c1, D)
                acc = psum("acc", [P, 2, 1024], c1)
                own, summed, stored = sem("own", c1), sem("summed", c1), sem("stored", c1)
                with nc.Block() as block:
                    @block.sync
                    def _(sp):
                        load_slots(sp, slot_node, slot, slots_in, rows_in)

                    @block.gpsimd
                    def _(pool):
                        ub = unit_bounds(pool)

                        def store(g):
                            pool.wait_ge(summed, g + 1)
                            scatter_group(pool, g, h_tab[layer + 1], lambda t: X[:, t, :], stored)

                        for g in range(NGRP):
                            with pool.Fori(ub[g], ub[g + 1]) as u:
                                gather_unit(pool, u, h_tab[layer], slot, rows, slots_in, rows_in, rows_free, marker)
                            if g and layer < 2:
                                store(g - 1)
                        if layer < 2:
                            store(NGRP - 1)
                            pool.wait_ge(stored, 16 * NTILE)

                    @block.tensor
                    def _(pe):
                        ub = unit_bounds(pe)
                        for q in range(RB):
                            pe.sem_inc(rows_free[q], 1)
                        for g in range(NGRP):
                            if g >= 2:
                                pe.wait_ge(summed, g - 1)
                            clear_sums(pe, acc[:, g % 2, :])
                            with pe.Fori(ub[g], ub[g + 1]) as u:
                                for q in range(RB):
                                    pe.wait_ge(rows_in[q], (16 * G) * u + 16 * G)
                                    add_rows(pe, acc[:, g % 2, :], rows[q]).then_inc(rows_free[q], 1)

                    @block.vector
                    def _(dve):
                        ub = unit_bounds(dve)
                        s = Steps(dve, own)
                        for g in range(NGRP):
                            if layer == 0:
                                s.link(dve.tensor_scalar(RES[:, cols(g), :], X[:, cols(g), :], 2.0, None, ALU.mult))
                            dve.wait_ge(rows_free[RB - 1], ub[g + 1] + 1)
                            for k in range(G):
                                t = g * G + k
                                s.go(dve.scalar_tensor_tensor(
                                    out=X[:, t, :], in0=acc[:, g % 2, k * P:(k + 1) * P], scalar=rdeg[:, t:t + 1],
                                    in1=X[:, t, :], op0=ALU.mult, op1=ALU.add))
                            s.need(s.n)
                            dve.sem_inc(summed, 1)
                            for k in range(G):
                                t = g * G + k
                                s.go(dve.scalar_tensor_tensor(
                                    out=RES[:, t, :], in0=X[:, t, :], scalar=1.0 / (1.0 + layer),
                                    in1=RES[:, t, :], op0=ALU.mult, op1=ALU.add))
                        s.need(s.n)

        with ExitStack() as c1:
            stage = [sb(f"stage{i}", [P, G, MW], F32, c1) for i in range(2)]
            sq = sb("sq", [P, G, D], F32, c1)
            st = sb("st", [P, 4, G], F32, c1)
            own, std_in, std_out, staged = (sem(n, c1) for n in ("own", "std_in", "std_out", "staged"))
            stored = [sem(f"stored{i}", c1) for i in range(2)]
            with nc.Block() as block:
                @block.vector
                def _(dve):
                    s = Steps(dve, own)
                    for i in range(2):
                        s.go(dve.memset(stage[i][:], 0.0))
                    for g in range(NGRP):
                        normalise(s, dve, None, g, RES, sq, st, std_in, std_out, g)
                        x1 = RES[:, cols(g), :]
                        s.link(dve.tensor_copy(X[:, cols(g), :], x1))
                        s.link(dve.tensor_tensor(sq[:], x1, x1, ALU.mult))
                        s.link(dve.tensor_reduce(d2[:, cols(g)], sq[:], AX.X, ALU.add))
                        if g >= 2:
                            dve.wait_ge(stored[g % 2], 16 * G * (g // 2))
                        b = stage[g % 2]
                        s.go(dve.tensor_copy(b[:, :, 0:D], x1))
                        s.go(dve.tensor_copy(b[:, :, D], d2[:, cols(g)]))
                        s.go(dve.tensor_copy(b[:, :, D + 1], real[:, cols(g)]))
                        s.need(s.n)
                        dve.sem_inc(staged, 1)

                @block.scalar
                def _(act):
                    for g in range(NGRP):
                        roots(act, st, std_in, std_out, g)

                @block.gpsimd
                def _(pool):
                    for g in range(NGRP):
                        pool.wait_ge(staged, g + 1)
                        scatter_group(pool, g, m_tab, lambda t: stage[g % 2][:, t - g * G, :], stored[g % 2])
                    pool.wait_ge(stored[0], 16 * G * ((NGRP + 1) // 2))
                    pool.wait_ge(stored[1], 16 * G * (NGRP // 2))

        with ExitStack() as c1:
            gam = sb("gam", [P, NTILE], F32, c1)
            with ExitStack() as c2:
                rows, slot, slots_in, rows_in, rows_free, marker = pass_memory(c2, MW)
                junk = sb("junk", [P, 2 * G, D], F32, c2)
                us = sb("us", [P, G, D], F32, c2)
                px = sb("px", [P, NTILE], F32, c2)
                o2 = sb("o2", [P, NTILE], F32, c2)
                names = ("dot a sd den al be ms mb y2 y2p mp ad bd ux g1 pb xy xx dn A B Ba Bb t1 t2 t3".split())
                v = {n: sb("v_" + n, [P, G], F32, c2) for n in names}
                own, scaled, scale_in = sem("own", c2), sem("scaled", c2), sem("scale_in", c2)
                with nc.Block() as block:
                    @block.sync
                    def _(sp):
                        load_slots(sp, slot_node, slot, slots_in, rows_in)

                    @block.gpsimd
                    def _(pool):
                        ub = unit_bounds(pool)
                        for g in range(NGRP):
                            with pool.Fori(ub[g], ub[g + 1]) as u:
                                gather_unit(pool, u, m_tab, slot, rows, slots_in, rows_in, rows_free, marker)

                    @block.scalar
                    def _(act):
                        ub = unit_bounds(act)
                        for g in range(NGRP):
                            with act.Fori(ub[g], ub[g + 1]) as u:
                                for q in range(RB):
                                    act.wait_ge(scale_in, u * RB + (q + 1))
                                    for k in range(G):
                                        a = act.activation(us[:, k, :], O[:, g * G + k, :], ACT.Copy,
                                                           scale=v["A"][:, k:k + 1])
                                    a.then_inc(scaled, 1)

                    @block.vector
                    def _(dve):
                        ub = unit_bounds(dve)
                        s = Steps(dve, own)
                        TT, TS, STT = dve.tensor_tensor, dve.tensor_scalar, dve.scalar_tensor_tensor

                        def mul(o, a, b):
                            s.link(TT(v[o][:], a, b, ALU.mult))

                        def add(o, a, b):
                            s.link(TT(v[o][:], a, b, ALU.add))

                        for a in (O, gam, px, o2):
                            s.go(dve.memset(a[:], 0.0))
                        s.need(s.n)
                        for q in range(RB):
                            dve.sem_inc(rows_free[q], 1)

                        def rank(g, u, q):
                            R, c = rows[q], cols(g)
                            s2, valid = R[:, :, D], R[:, :, D + 1]
                            V = {n: v[n][:] for n in v}
                            dve.wait_ge(rows_in[q], (16 * G) * u + 16 * G)
                            for k in range(G):
                                s.go(dve.tensor_tensor_reduce(junk[:, k, :], R[:, k, 0:D], X[:, g * G + k, :], 1.0, 0.0,
                                                              ALU.mult, ALU.add, v["dot"][:, k:k + 1]))
                                s.go(dve.tensor_tensor_reduce(junk[:, G + k, :], R[:, k, 0:D], O[:, g * G + k, :], 1.0, 0.0,
                                                              ALU.mult, ALU.add, v["ux"][:, k:k + 1]))
                            s.need(s.n)
                            s.link(TS(V["a"], V["dot"], -2.0, 1.0, ALU.mult, ALU.add))
                            mul("sd", s2, d2[:, c])
                            add("den", V["a"], V["sd"])
                            s.link(TS(V["den"], V["den"], MOB_EPS, None, ALU.max))
                            s.link(dve.reciprocal(V["den"], V["den"]))
                            mul("den", V["den"], valid)
                            add("al", V["a"], d2[:, c])
                            mul("al", V["al"], V["den"])
                            s.link(TS(V["be"], s2, -1.0, None, ALU.add))
                            mul("be", V["be"], V["den"])
                            mul("ad", V["al"], V["dot"])
                            mul("bd", V["be"], V["dot"])
                            mul("ms", V["al"], s2)
                            mul("mb", V["be"], d2[:, c])
                            add("ms", V["ms"], V["bd"])
                            add("mp", V["ad"], V["mb"])
                            mul("t1", V["al"], V["ms"])
                            mul("t2", V["be"], V["mp"])
                            add("y2", V["t1"], V["t2"])
                            s.link(TS(V["y2p"], V["y2"], 1.0, None, ALU.add))
                            mul("g1", gam[:, c], V["dot"])
                            add("g1", V["g1"], V["ux"])
                            mul("g1", V["g1"], V["al"])
                            mul("pb", px[:, c], V["be"])
                            add("xy", V["g1"], V["pb"])
                            mul("xx", o2[:, c], V["y2"])
                            s.link(STT(out=V["dn"], in0=V["xy"], scalar=2.0, in1=V["xx"], op0=ALU.mult, op1=ALU.add))
                            s.link(TS(V["dn"], V["dn"], 1.0, MOB_EPS, ALU.add, ALU.max))
                            s.link(dve.reciprocal(V["dn"], V["dn"]))
                            s.link(STT(out=V["A"], in0=V["xy"], scalar=2.0, in1=V["y2p"], op0=ALU.mult, op1=ALU.add))
                            s.link(TT(V["A"], V["A"], V["dn"], ALU.mult))
                            dve.sem_inc(scale_in, 1)
                            s.link(TS(V["B"], o2[:, c], -1.0, 1.0, ALU.mult, ALU.add))
                            mul("B", V["B"], V["dn"])
                            mul("Ba", V["B"], V["al"])
                            mul("Bb", V["B"], V["be"])
                            mul("t1", V["B"], V["xy"])
                            mul("t2", V["A"], o2[:, c])
                            add("t1", V["t1"], V["t2"])
                            mul("t1", V["t1"], V["A"])
                            mul("t2", V["A"], V["xy"])
                            mul("t3", V["B"], V["y2"])
                            add("t2", V["t2"], V["t3"])
                            mul("t2", V["t2"], V["B"])
                            s.link(TT(o2[:, c], V["t1"], V["t2"], ALU.add))
                            mul("t1", V["A"], gam[:, c])
                            s.link(TT(gam[:, c], V["t1"], V["Bb"], ALU.add))
                            mul("t1", V["A"], px[:, c])
                            mul("t2", V["B"], V["mp"])
                            s.link(TT(px[:, c], V["t1"], V["t2"], ALU.add))
                            dve.wait_ge(scaled, u * RB + (q + 1))
                            for k in range(G):
                                s.go(STT(out=O[:, g * G + k, :], in0=R[:, k, 0:D], scalar=v["Ba"][:, k:k + 1],
                                         in1=us[:, k, :], op0=ALU.mult, op1=ALU.add))
                            s.need(s.n)
                            dve.sem_inc(rows_free[q], 1)

                        for g in range(NGRP):
                            with dve.Fori(ub[g], ub[g + 1]) as u:
                                s.restart()
                                for q in range(RB):
                                    rank(g, u, q)

            with ExitStack() as c2:
                junk = sb("junk", [P, NTILE, D], F32, c2)
                st = sb("st", [P, 4, G], F32, c2)
                sq = sb("sq", [P, G, D], F32, c2)
                names = "n2 xo nrm nc lp lm z th f ok y2 xy den c1 c2 t".split()
                v = {n: sb("w_" + n, [P, NTILE], F32, c2) for n in names}
                V = {n: v[n][:] for n in names}
                own, roots_in, roots_out, std_in, std_out = (
                    sem(n, c2) for n in ("own", "roots_in", "roots_out", "std_in", "std_out"))
                with nc.Block() as block:
                    @block.scalar
                    def _(act):
                        act.wait_ge(roots_in, 1)
                        act.activation(V["nrm"], V["n2"], ACT.Sqrt).then_inc(roots_out, 1)
                        act.wait_ge(roots_in, 2)
                        act.activation(V["lp"], V["lp"], ACT.Ln).then_inc(roots_out, 1)
                        act.activation(V["lm"], V["lm"], ACT.Ln).then_inc(roots_out, 1)
                        act.wait_ge(roots_in, 3)
                        act.activation(V["th"], V["z"], ACT.Tanh).then_inc(roots_out, 1)
                        for g in range(NGRP):
                            roots(act, st, std_in, std_out, g)

                    @block.vector
                    def _(dve):
                        s = Steps(dve, own)
                        TT, TS, STT = dve.tensor_tensor, dve.tensor_scalar, dve.scalar_tensor_tensor

                        def tt(o, a, b, op=ALU.mult):
                            s.link(TT(V[o], a, b, op))

                        for t in range(NTILE):
                            s.go(STT(out=O[:, t, :], in0=X[:, t, :], scalar=gam[:, t:t + 1], in1=O[:, t, :],
                                     op0=ALU.mult, op1=ALU.add))
                        s.need(s.n)
                        for t in range(NTILE):
                            s.go(dve.tensor_tensor_reduce(junk[:, t, :], O[:, t, :], O[:, t, :], 1.0, 0.0,
                                                          ALU.mult, ALU.add, v["n2"][:, t:t + 1]))
                        s.need(s.n)
                        dve.sem_inc(roots_in, 1)
                        for t in range(NTILE):
                            s.go(dve.tensor_tensor_reduce(junk[:, t, :], O[:, t, :], X[:, t, :], 1.0, 0.0,
                                                          ALU.mult, ALU.add, v["xo"][:, t:t + 1]))
                        s.need(s.n)
                        dve.wait_ge(roots_out, 1)
                        s.link(TS(V["nc"], V["nrm"], MOB_EPS, 1.0 - MOB_EPS, ALU.max, ALU.min))
                        s.link(TS(V["lp"], V["nc"], 1.0, 1.0, ALU.mult, ALU.add))
                        s.link(TS(V["lm"], V["nc"], -1.0, 1.0, ALU.mult, ALU.add))
                        dve.sem_inc(roots_in, 1)
                        dve.wait_ge(roots_out, 3)
                        tt("z", V["lp"], V["lm"], ALU.subtract)
                        tt("z", V["z"], rdeg[:])
                        s.link(TS(V["z"], V["z"], 0.5, None, ALU.mult))
                        dve.sem_inc(roots_in, 1)
                        s.link(dve.reciprocal(V["f"], V["nc"]))
                        s.link(TS(V["ok"], V["nrm"], MOB_EPS, None, ALU.is_gt))
                        dve.wait_ge(roots_out, 4)
                        tt("f", V["f"], V["th"])
                        tt("f", V["f"], V["ok"])
                        tt("xy", V["f"], V["xo"])
                        tt("t", V["f"], V["f"])
                        tt("y2", V["t"], V["n2"])
                        tt("t", d2[:], V["y2"])
                        s.link(TS(V["xy"], V["xy"], 2.0, 1.0, ALU.mult, ALU.add))
                        tt("den", V["xy"], V["t"], ALU.add)
                        s.link(TS(V["den"], V["den"], MOB_EPS, None, ALU.max))
                        s.link(dve.reciprocal(V["den"], V["den"]))
                        tt("c1", V["xy"], V["y2"], ALU.add)
                        tt("c1", V["c1"], V["den"])
                        s.link(TS(V["c1"], V["c1"], 1.0, None, ALU.add))
                        s.link(TS(V["c2"], d2[:], -1.0, 1.0, ALU.mult, ALU.add))
                        tt("c2", V["c2"], V["f"])
                        tt("c2", V["c2"], V["den"])
                        for t in range(NTILE):
                            s.go(TS(O[:, t, :], O[:, t, :], v["c2"][:, t:t + 1], None, ALU.mult))
                        s.need(s.n)
                        for t in range(NTILE):
                            s.go(STT(out=X[:, t, :], in0=X[:, t, :], scalar=v["c1"][:, t:t + 1], in1=O[:, t, :],
                                     op0=ALU.mult, op1=ALU.add))
                        s.need(s.n)
                        for g in range(NGRP):
                            normalise(s, dve, None, g, X, sq, st, std_in, std_out, g)

        l2 = ctx.enter_context(ExitStack())
        XA = l2.enter_context(nc.sbuf_tensor("XA", [P, NTILE, T * HK], F32))
        pk = sb("pk", [P, HK])
        imp = sb("imp", [P, T])
        with ExitStack() as c1:
            Wt = sb("Wt", [P, T, D], F32, c1)
            WT = sb("WT", [P, T, D], F32, c1)
            A2 = sb("A2", [P, 2, H, K], F32, c1)
            Wj = sb("Wj", [P, T, D + HK], F32, c1)
            Wi = sb("Wi", [P, T * HK], F32, c1)
            cf = sb("cf", [P, K], F32, c1)
            cs = sb("cs", [P, 4], F32, c1)
            bias = sb("bias", [P, D], F32, c1)
            hot = sb("hot", [P, T, T], F32, c1)
            xT = [sb(f"xT{i}", [P, D], F32, c1) for i in range(2)]
            stage = [sb(f"tstage{i}", [P, T, TW], F32, c1) for i in range(2)]
            turn_ps = psum("turn_ps", [P, 2, 512], c1)
            prod_ps = psum("prod_ps", [P, 2, 1024], c1)
            loaded, zeroed, own, turned, kept, vecs, vkept, exp_in, exp_out, staged = (
                sem(n, c1) for n in ("loaded", "zeroed", "own", "turned", "kept", "vecs", "vkept", "exp_in",
                                     "exp_out", "staged"))
            x_turned, x_kept, multiplied = (sem(n, c1) for n in ("x_turned", "x_kept", "multiplied"))
            stored = [sem(f"stored{i}", c1) for i in range(2)]
            with nc.Block() as block:
                @block.sync
                def _(sp):
                    sp.dma_start(Wt[:], W2n.rearrange("t i o -> i t o")).then_inc(loaded, 16)
                    sp.dma_start(cf[:], conf.rearrange("(o k) -> o k", o=1).to_broadcast([P, K])).then_inc(loaded, 16)
                    sp.dma_start(imp[:], importance.rearrange("(o k) -> o k", o=1).to_broadcast([P, T])).then_inc(loaded, 16)
                    sp.dma_start(bias[:], bias2.rearrange("(o k) -> o k", o=1).to_broadcast([P, D])).then_inc(loaded, 16)
                    sp.wait_ge(zeroed, 1)
                    with nc.allow_non_contiguous_dma("1280 values, once"):
                        for h in range(H):
                            for side, at in ((0, C), (1, 0)):
                                for k in range(K):
                                    sp.dma_start(A2[h * C:(h + 1) * C, side, h, k:k + 1],
                                                 att[k, h, at:at + C].rearrange("(c o) -> c o", o=1)).then_inc(loaded, 16)

                LOADS = 16 * (4 + 2 * H * K)

                @block.tensor
                def _(pe):
                    pe.wait_ge(loaded, LOADS)
                    for t in range(T):
                        pe.transpose(turn_ps[:, 0, t * D:(t + 1) * D], Wt[:, t, :], ident[:]).then_inc(turned, 1)
                    pe.wait_ge(kept, 1)
                    for t in range(T):
                        pe.matmul(turn_ps[:, 1, t * 64:t * 64 + 2 * HK], WT[:, t, :],
                                  A2[:].rearrange("p s h k -> p (s h k)"), start=True, stop=True).then_inc(vecs, 1)
                    pe.wait_ge(vkept, 1)
                    wj = Wj[:].rearrange("p t n -> p (t n)")
                    CUT = 3 * (D + HK)
                    for t in range(NTILE):
                        b = t % 2
                        pe.transpose(turn_ps[:, b, 0:D], X[:, t, :], ident[:]).then_inc(x_turned, 1)
                        pe.wait_ge(x_kept, t + 1)
                        if t >= 2:
                            pe.wait_ge(staged, t - 1)
                        pe.matmul(prod_ps[:, b, 0:CUT], xT[b][:], wj[:, 0:CUT], start=True, stop=True)
                        pe.matmul(prod_ps[:, b, 512:512 + D + HK], xT[b][:], wj[:, CUT:], start=True, stop=True)
                        pe.matmul(prod_ps[:, b, 512 + D + HK:512 + D + HK + T * HK], xT[b][:], Wi[:],
                                  start=True, stop=True).then_inc(multiplied, 1)

                @block.scalar
                def _(act):
                    act.wait_ge(exp_in, 1)
                    act.activation(cf[:], cf[:], ACT.Exp, accum_out=cs[:, 1:2]).then_inc(exp_out, 1)
                    for t in range(NTILE):
                        act.wait_ge(x_turned, t + 1)
                        if t >= 2:
                            act.wait_ge(multiplied, t - 1)
                        act.activation(xT[t % 2][:], turn_ps[:, t % 2, 0:D], ACT.Copy).then_inc(x_kept, 1)

                @block.vector
                def _(dve):
                    s = Steps(dve, own)
                    dve.memset(A2[:], 0.0).then_inc(zeroed, 1)
                    for i in range(2):
                        s.go(dve.memset(stage[i][:], 0.0))
                    s.need(s.n)
                    s.link(dve.memset(hot[:], 0.0))
                    for t in range(T):
                        s.go(dve.memset(hot[:, t, t:t + 1], 1.0))
                    dve.wait_ge(loaded, LOADS)
                    s.link(dve.tensor_reduce(cs[:, 0:1], cf[:], AX.X, ALU.max))
                    s.link(dve.tensor_scalar(cf[:], cf[:], cs[:, 0:1], None, ALU.subtract))
                    dve.sem_inc(exp_in, 1)
                    dve.wait_ge(exp_out, 1)
                    s.link(dve.reciprocal(cs[:, 2:3], cs[:, 1:2]))
                    s.link(dve.tensor_scalar(cf[:], cf[:], cs[:, 2:3], None, ALU.mult))
                    s.link(dve.tensor_copy(pk[:].rearrange("p (h k) -> p h k", h=H),
                                           cf[:].unsqueeze(1).to_broadcast([P, H, K])))
                    dve.wait_ge(turned, T)
                    s.go(dve.tensor_copy(Wj[:, :, 0:D], Wt[:]))
                    s.link(dve.tensor_copy(WT[:].rearrange("p t d -> p (t d)"), turn_ps[:, 0, :]))
                    dve.sem_inc(kept, 1)
                    dve.wait_ge(vecs, T)
                    vps = turn_ps[:, 1, 0:T * 64].rearrange("p (t n) -> p t n", n=64)
                    s.link(dve.tensor_copy(Wj[:, :, D:D + HK], vps[:, :, 0:HK]))
                    s.link(dve.tensor_copy(Wi[:].rearrange("p (t n) -> p t n", t=T), vps[:, :, HK:2 * HK]))
                    dve.sem_inc(vkept, 1)
                    for t in range(NTILE):
                        b = stage[t % 2]
                        dve.wait_ge(multiplied, t + 1)
                        if t >= 2:
                            dve.wait_ge(stored[t % 2], 16 * (t // 2))
                        s.go(dve.tensor_copy(b[:, 0:3, 0:D + HK],
                                             prod_ps[:, t % 2, 0:3 * (D + HK)].rearrange("p (t n) -> p t n", t=3)))
                        s.go(dve.tensor_copy(b[:, 3, 0:D + HK], prod_ps[:, t % 2, 512:512 + D + HK]))
                        s.go(dve.tensor_scalar(b[:, :, D + HK:TW], hot[:], real[:, t:t + 1], None, ALU.mult))
                        s.go(dve.tensor_copy(XA[:, t, :], prod_ps[:, t % 2, 512 + D + HK:512 + D + HK + T * HK]))
                        s.link(dve.tensor_tensor(RES[:, t, :], X[:, t, :], prod_ps[:, t % 2, 0:D], ALU.add))
                        dve.sem_inc(staged, 1)
                        s.link(dve.tensor_tensor(RES[:, t, :], RES[:, t, :], bias[:], ALU.add))

                @block.gpsimd
                def _(pool):
                    for t in range(NTILE):
                        pool.wait_ge(staged, t + 1)
                        pool.indirect_dma_start(t_tab, bass.IndirectOffsetOnAxis(ap=node[:, t, 2:3], axis=0),
                                                stage[t % 2][:].rearrange("p t n -> p (t n)"), None
                                                ).then_inc(stored[t % 2], 16)
                    pool.wait_ge(stored[0], 16 * ((NTILE + 1) // 2))
                    pool.wait_ge(stored[1], 16 * (NTILE // 2))

        MX = sb("MX", [P, NTILE, T, 2, H])
        t_rows = t_tab.rearrange("n (t w) -> (n t) w", t=T)

        def scores(s, dve, R, g, tmp):
            prod, sc, al = tmp
            oh = R[:, :, D + HK:TW]
            xa = XA[:, cols(g), :].rearrange("p k (t n) -> p k t n", t=T)
            s.link(dve.tensor_tensor(prod[:, :, :, 0:HK], xa, oh.unsqueeze(3).to_broadcast([P, G, T, HK]), ALU.mult))
            s.link(dve.tensor_reduce(sc[:], prod[:, :, :, 0:HK].rearrange("p k t n -> p k n t"), AX.X, ALU.add))
            s.link(dve.tensor_tensor(sc[:], sc[:], R[:, :, D:D + HK], ALU.add))
            s.link(dve.scalar_tensor_tensor(out=sc[:], in0=sc[:], scalar=0.2, in1=sc[:], op0=ALU.mult, op1=ALU.max))
            s.link(dve.tensor_tensor(sc[:], sc[:], pk[:].unsqueeze(1).to_broadcast([P, G, HK]), ALU.mult))
            s.link(dve.tensor_reduce(al[:], sc[:].rearrange("p k (h c) -> p k h c", h=H), AX.X, ALU.add))

        with ExitStack() as c1:
            rows, slot, slots_in, rows_in, rows_free, marker = pass_memory(c1, TW)
            prod = sb("prod", [P, G, T, HK], F32, c1)
            sc = sb("sc", [P, G, HK], F32, c1)
            al = sb("al", [P, G, H], F32, c1)
            pen = sb("pen", [P, G, T], F32, c1)
            cand = sb("cand", [P, G, T, H], F32, c1)
            mnew = sb("mnew", [P, G, T, H], F32, c1)
            ex = sb("ex", [P, 2, G, T, H], F32, c1)
            MAX = sb("MAX", [P, NTILE, T, H], F32, c1)
            DEN = sb("DEN", [P, NTILE, T, H], F32, c1)
            own, exp_in, exp_out = sem("own", c1), sem("exp_in", c1), sem("exp_out", c1)
            with nc.Block() as block:
                @block.sync
                def _(sp):
                    load_slots(sp, slot_typed, slot, slots_in, rows_in)

                @block.gpsimd
                def _(pool):
                    ub = unit_bounds(pool)
                    for g in range(NGRP):
                        with pool.Fori(ub[g], ub[g + 1]) as u:
                            gather_unit(pool, u, t_rows, slot, rows, slots_in, rows_in, rows_free, marker)

                @block.scalar
                def _(act):
                    ub = unit_bounds(act)
                    for g in range(NGRP):
                        with act.Fori(ub[g], ub[g + 1]) as u:
                            for q in range(RB):
                                act.wait_ge(exp_in, u * RB + (q + 1))
                                act.activation(ex[:], ex[:], ACT.Exp).then_inc(exp_out, 1)

                @block.vector
                def _(dve):
                    ub = unit_bounds(dve)
                    s = Steps(dve, own)
                    TT = dve.tensor_tensor
                    s.go(dve.memset(MAX[:], NEG))
                    s.go(dve.memset(DEN[:], 0.0))
                    s.need(s.n)
                    for q in range(RB):
                        dve.sem_inc(rows_free[q], 1)

                    def rank(g, u, q):
                        R = rows[q]
                        oh = R[:, :, D + HK:TW]
                        by_type = oh.unsqueeze(3).to_broadcast([P, G, T, H])
                        dve.wait_ge(rows_in[q], (16 * G) * u + 16 * G)
                        scores(s, dve, R, g, (prod, sc, al))
                        s.link(dve.tensor_scalar(pen[:], oh, -1.0, -NEG, ALU.add, ALU.mult))
                        s.link(TT(cand[:], al[:].unsqueeze(2).to_broadcast([P, G, T, H]), by_type, ALU.mult))
                        s.link(TT(cand[:], cand[:], pen[:].unsqueeze(3).to_broadcast([P, G, T, H]), ALU.add))
                        M, S = MAX[:, cols(g)], DEN[:, cols(g)]
                        s.link(TT(mnew[:], M, cand[:], ALU.max))
                        s.link(TT(ex[:, 0], cand[:], mnew[:], ALU.subtract))
                        s.link(TT(ex[:, 1], M, mnew[:], ALU.subtract))
                        dve.sem_inc(exp_in, 1)
                        s.link(dve.tensor_copy(M, mnew[:]))
                        dve.wait_ge(exp_out, u * RB + (q + 1))
                        s.link(TT(ex[:, 0], ex[:, 0], by_type, ALU.mult))
                        s.link(TT(S, S, ex[:, 1], ALU.mult))
                        s.link(TT(S, S, ex[:, 0], ALU.add))
                        dve.sem_inc(rows_free[q], 1)

                    for g in range(NGRP):
                        with dve.Fori(ub[g], ub[g + 1]) as u:
                            s.restart()
                            for q in range(RB):
                                rank(g, u, q)
                    s.restart()
                    s.link(dve.tensor_copy(MX[:, :, :, 0, :], MAX[:]))
                    s.link(dve.tensor_scalar(MAX[:], DEN[:], 0.0, None, ALU.is_equal))
                    s.link(TT(DEN[:], DEN[:], MAX[:], ALU.add))
                    s.link(dve.reciprocal(DEN[:], DEN[:]))
                    s.link(TT(MX[:, :, :, 1, :], DEN[:],
                              imp[:].unsqueeze(1).unsqueeze(3).to_broadcast([P, NTILE, T, H]), ALU.mult))

        with ExitStack() as c1:
            rows, slot, slots_in, rows_in, rows_free, marker = pass_memory(c1, TW)
            prod = sb("prod", [P, G, T, HK], F32, c1)
            sc = sb("sc", [P, G, HK], F32, c1)
            al = sb("al", [P, G, H], F32, c1)
            sel = sb("sel", [P, G, 2 * H], F32, c1)
            wgt = sb("wgt", [P, G, H], F32, c1)
            wrow = [sb(f"wrow{i}", [P, G, D], F32, c1) for i in range(2)]
            sq = sb("sq", [P, G, D], F32, c1)
            st = sb("st", [P, 4, G], F32, c1)
            acc = psum("acc", [P, 2, 1024], c1)
            own, exp_in, exp_out, std_in, std_out, weighted, added, summed = (
                sem(n, c1) for n in ("own", "exp_in", "exp_out", "std_in", "std_out", "weighted", "added", "summed"))
            with nc.Block() as block:
                @block.sync
                def _(sp):
                    load_slots(sp, slot_typed, slot, slots_in, rows_in)

                @block.gpsimd
                def _(pool):
                    ub = unit_bounds(pool)
                    for g in range(NGRP):
                        with pool.Fori(ub[g], ub[g + 1]) as u:
                            gather_unit(pool, u, t_rows, slot, rows, slots_in, rows_in, rows_free, marker)

                @block.scalar
                def _(act):
                    ub = unit_bounds(act)
                    for g in range(NGRP):
                        with act.Fori(ub[g], ub[g + 1]) as u:
                            for q in range(RB):
                                act.wait_ge(exp_in, u * RB + (q + 1))
                                act.activation(wgt[:], wgt[:], ACT.Exp).then_inc(exp_out, 1)
                    for g in range(NGRP):
                        roots(act, st, std_in, std_out, g)

                @block.tensor
                def _(pe):
                    ub = unit_bounds(pe)
                    for g in range(NGRP):
                        if g >= 2:
                            pe.wait_ge(summed, g - 1)
                        clear_sums(pe, acc[:, g % 2, :])
                        with pe.Fori(ub[g], ub[g + 1]) as u:
                            for q in range(RB):
                                pe.wait_ge(weighted, u * RB + (q + 1))
                                add_rows(pe, acc[:, g % 2, :], wrow[q % 2]).then_inc(added, 1)

                @block.vector
                def _(dve):
                    ub = unit_bounds(dve)
                    s = Steps(dve, own)
                    TT = dve.tensor_tensor
                    for q in range(RB):
                        dve.sem_inc(rows_free[q], 1)
                    dve.sem_inc(added, 2)

                    def rank(g, u, q):
                        R = rows[q]
                        oh = R[:, :, D + HK:TW]
                        dve.wait_ge(rows_in[q], (16 * G) * u + 16 * G)
                        scores(s, dve, R, g, (prod, sc, al))
                        mx = MX[:, cols(g)].rearrange("p k t a h -> p k t (a h)")
                        s.link(TT(prod[:, :, :, 0:2 * H], mx, oh.unsqueeze(3).to_broadcast([P, G, T, 2 * H]), ALU.mult))
                        s.link(dve.tensor_reduce(sel[:], prod[:, :, :, 0:2 * H].rearrange("p k t n -> p k n t"), AX.X, ALU.add))
                        s.link(TT(wgt[:], al[:], sel[:, :, 0:H], ALU.subtract))
                        dve.sem_inc(exp_in, 1)
                        dve.wait_ge(exp_out, u * RB + (q + 1))
                        s.link(TT(wgt[:], wgt[:], sel[:, :, H:2 * H], ALU.mult))
                        dve.wait_ge(added, u * RB + (q + 1))
                        s.link(TT(wrow[q % 2][:].rearrange("p k (h c) -> p k h c", h=H),
                                  R[:, :, 0:D].rearrange("p k (h c) -> p k h c", h=H),
                                  wgt[:].unsqueeze(3).to_broadcast([P, G, H, C]), ALU.mult))
                        dve.sem_inc(weighted, 1)
                        dve.sem_inc(rows_free[q], 1)

                    for g in range(NGRP):
                        with dve.Fori(ub[g], ub[g + 1]) as u:
                            s.restart()
                            for q in range(RB):
                                rank(g, u, q)
                        s.restart()
                        dve.wait_ge(added, ub[g + 1] * RB + 2)
                        s.link(TT(X[:, cols(g), :], RES[:, cols(g), :],
                                  acc[:, g % 2, 0:5 * P].rearrange("p (k d) -> p k d", k=G), ALU.add))
                        dve.sem_inc(summed, 1)
                    for g in range(NGRP):
                        normalise(s, dve, None, g, X, sq, st, std_in, std_out, g)

        with ExitStack() as c1:
            attr = [sb(f"attr{k}", [P, AR, D], F32, c1) for k in range(G)]
            offs = [sb(f"offs{k}", [P, 1], I32, c1) for k in range(G)]
            off = sb("off", [P, G], F32, c1)
            at0 = sb("at0", [P, NTILE], F32, c1)
            end = sb("end", [P, NTILE], F32, c1)
            eid = sb("eid", [P, G, AR], F32, c1)
            val = sb("val", [P, G, AR], F32, c1)
            val2 = sb("val2", [P, G, AR], F32, c1)
            acc = psum("acc", [P, 2, 1024], c1)
            own, offsets, masked, added, summed, marker = (
                sem(n, c1) for n in ("own", "offsets", "masked", "added", "summed", "marker"))
            attr_in = [sem(f"attr_in{k}", c1) for k in range(G)]
            with nc.Block() as block:
                def turn_bounds(eng):
                    hi = [sum(ATT_TURNS[:g]) for g in range(NGRP + 1)]
                    return bounds(eng, AB, NGRP + 1, list(range(NGRP + 1)), hi)

                @block.gpsimd
                def _(pool):
                    tb = turn_bounds(pool)
                    for g in range(NGRP):
                        with pool.Fori(tb[g], tb[g + 1]) as i:
                            pool.wait_ge(offsets, i + 1)
                            pool.sem_inc(marker, 1)
                            for k in range(G):
                                pool.wait_ge(added, i * G + (k + 1))
                                pool.sem_inc(marker, 1)
                                pool.indirect_dma_start(attr[k][:].rearrange("p r d -> p (r d)"), None, flat(edge_attr),
                                                        bass.IndirectOffsetOnAxis(ap=offs[k][:], axis=0)
                                                        ).then_inc(attr_in[k], 16)

                @block.vector
                def _(dve):
                    tb = turn_bounds(dve)
                    s = Steps(dve, own)
                    TT, TS = dve.tensor_tensor, dve.tensor_scalar
                    s.link(TT(end[:], nodef[:, :, 0], nodef[:, :, 1], ALU.add))
                    s.link(dve.tensor_copy(at0[:], nodef[:, :, 0]))
                    for g in range(NGRP):
                        c = cols(g)
                        with dve.Fori(tb[g], tb[g + 1]) as i:
                            s.restart()
                            s.link(TS(off[:], at0[:, c], float(E - AR), None, ALU.min))
                            for k in range(G):
                                s.go(TS(offs[k][:], off[:, k:k + 1], float(D), None, ALU.mult))
                            s.need(s.n)
                            dve.sem_inc(offsets, 1)
                            s.link(TT(eid[:], iota_w[:, 0:AR].unsqueeze(1).to_broadcast([P, G, AR]), wide(off[:], AR), ALU.add))
                            s.link(TT(val[:], eid[:], wide(at0[:, c], AR), ALU.is_ge))
                            s.link(TT(val2[:], eid[:], wide(end[:, c], AR), ALU.is_lt))
                            s.link(TT(val[:], val[:], val2[:], ALU.mult))
                            s.link(TS(at0[:, c], at0[:, c], float(AR), None, ALU.add))
                            for k in range(G):
                                dve.wait_ge(attr_in[k], 16 * i + 16)
                                s.link(TT(attr[k][:], attr[k][:], val[:, k, :].unsqueeze(2).to_broadcast([P, AR, D]), ALU.mult))
                                dve.sem_inc(masked, 1)
                        s.restart()
                        dve.wait_ge(added, tb[g + 1] * G + G)
                        s.link(dve.tensor_copy(O[:, c, :], acc[:, g % 2, 0:5 * P].rearrange("p (k d) -> p k d", k=G)))
                        dve.sem_inc(summed, 1)

                @block.tensor
                def _(pe):
                    tb = turn_bounds(pe)
                    pe.sem_inc(added, G)
                    for g in range(NGRP):
                        if g >= 2:
                            pe.wait_ge(summed, g - 1)
                        clear_sums(pe, acc[:, g % 2, :])
                        with pe.Fori(tb[g], tb[g + 1]) as i:
                            for k in range(G):
                                pe.wait_ge(masked, i * G + (k + 1))
                                for r in range(AR):
                                    mm = pe.matmul(acc[:, g % 2, k * P:(k + 1) * P], ident[:], attr[k][:, r, :],
                                                   start=False, stop=False, skip_group_check=True)
                                mm.then_inc(added, 1)

        with ExitStack() as c1:
            Wa = sb("Wa", [P, 2, D], F32, c1)
            Wb = sb("Wb", [P, D], F32, c1)
            b1 = sb("b1", [P, 1], F32, c1)
            b2 = sb("b2", [P, D], F32, c1)
            inT = [sb(f"inT{i}", [P, 2 * D], F32, c1) for i in range(2)]
            hT = [sb(f"hT{i}", [P, D], F32, c1) for i in range(2)]
            sq = sb("sq", [P, G, D], F32, c1)
            st = sb("st", [P, 4, G], F32, c1)
            in_ps = psum("in_ps", [P, 2, 512], c1)
            h_ps = psum("h_ps", [P, 2, 512], c1)
            y_ps = psum("y_ps", [P, 2, 512], c1)
            loaded, own, turned, kept, hidden, active, outed, taken, std_in, std_out, normed, stored = (
                sem(n, c1) for n in ("loaded", "own", "turned", "kept", "hidden", "active", "outed", "taken",
                                     "std_in", "std_out", "normed", "stored"))
            with nc.Block() as block:
                @block.sync
                def _(sp):
                    sp.dma_start(Wa[:], W1m.rearrange("(a i) o -> i a o", a=2)).then_inc(loaded, 16)
                    sp.dma_start(Wb[:], W2m).then_inc(loaded, 16)
                    sp.dma_start(b1[:], b1m.rearrange("(d o) -> d o", o=1)).then_inc(loaded, 16)
                    sp.dma_start(b2[:], b2m.rearrange("(o d) -> o d", o=1).to_broadcast([P, D])).then_inc(loaded, 16)

                @block.tensor
                def _(pe):
                    pe.wait_ge(loaded, 64)
                    for t in range(NTILE):
                        b = t % 2
                        if t >= 2:
                            pe.wait_ge(kept, t - 1)
                        pe.transpose(in_ps[:, b, 0:D], X[:, t, :], ident[:])
                        pe.transpose(in_ps[:, b, D:2 * D], O[:, t, :], ident[:]).then_inc(turned, 1)
                        pe.wait_ge(kept, t + 1)
                        pe.matmul(h_ps[:, b, 0:D], Wa[:, 0, :], inT[b][:, 0:D], start=True, stop=False)
                        pe.matmul(h_ps[:, b, 0:D], Wa[:, 1, :], inT[b][:, D:2 * D], start=False, stop=True).then_inc(hidden, 1)
                        pe.wait_ge(active, t + 1)
                        if t >= 2:
                            pe.wait_ge(taken, t - 1)
                        pe.matmul(y_ps[:, b, 0:D], hT[b][:], Wb[:], start=True, stop=True).then_inc(outed, 1)

                @block.scalar
                def _(act):
                    act.wait_ge(loaded, 64)
                    for t in range(NTILE):
                        b = t % 2
                        act.wait_ge(turned, t + 1)
                        act.activation(inT[b][:], in_ps[:, b, 0:2 * D], ACT.Copy).then_inc(kept, 1)
                        act.wait_ge(hidden, t + 1)
                        act.activation(hT[b][:], h_ps[:, b, 0:D], ACT.Relu, bias=b1[:, 0:1]).then_inc(active, 1)
                    for g in range(NGRP):
                        roots(act, st, std_in, std_out, g)

                @block.vector
                def _(dve):
                    s = Steps(dve, own)
                    dve.wait_ge(loaded, 64)
                    for t in range(NTILE):
                        s.link(dve.tensor_tensor(RES[:, t, :], X[:, t, :], b2[:], ALU.add))
                        dve.wait_ge(outed, t + 1)
                        s.link(dve.tensor_tensor(RES[:, t, :], RES[:, t, :], y_ps[:, t % 2, 0:D], ALU.add))
                        dve.sem_inc(taken, 1)
                    for g in range(NGRP):
                        normalise(s, dve, None, g, RES, sq, st, std_in, std_out, g)
                        dve.sem_inc(normed, 1)

                @block.gpsimd
                def _(pool):
                    for g in range(NGRP):
                        pool.wait_ge(normed, g + 1)
                        for k in range(G):
                            t = g * G + k
                            pool.indirect_dma_start(out, bass.IndirectOffsetOnAxis(ap=node[:, t, 2:3], axis=0),
                                                    RES[:, t, :], None, bounds_check=N - 1, oob_is_err=False
                                                    ).then_inc(stored, 16)
                    pool.wait_ge(stored, 16 * NTILE)


_INS = ['x', 'src', 'dst', 'edge_attr_128', 'edge_type_4', 'L2_gnn_W', 'L2_gnn_att_vectors',
        'L2_gnn_confounder_probs', 'L2_gnn_edge_importance', 'L2_gnn_bias', 'L3_gnn_W1', 'L3_gnn_b1',
        'L3_gnn_W2', 'L3_gnn_b2']
_OUTS = [((3125, 128), 'float32')]


def kernel(**inputs):
    import numpy as _np
    import concourse.bacc as _bacc
    from concourse import mybir as _mybir
    from concourse.bass_utils import run_bass_kernel_spmd as _run

    nc = _bacc.Bacc("TRN2", target_bir_lowering=False, num_devices=1)
    arrays, args = {}, []
    for name in _INS:
        a = _np.ascontiguousarray(inputs[name])
        arrays[f"in_{name}_dram"] = a
        args.append(nc.dram_tensor(f"in_{name}_dram", a.shape, _mybir.dt.from_np(a.dtype), kind="ExternalInput").ap())
    for i, (shape, dtype) in enumerate(_OUTS):
        dt = _mybir.dt.from_np(_np.dtype(dtype))
        args.append(nc.dram_tensor(f"out_{i}_dram", shape, dt, kind="ExternalOutput").ap())
    build_program(nc, *args)
    r = _run(nc, [arrays], core_ids=[0])
    got = tuple(r.results[0][f"out_{i}_dram"] for i in range(len(_OUTS)))
    return got[0]
```

```python
from contextlib import ExitStack
from itertools import zip_longest

import concourse.bass as bass
from concourse import mybir

F32 = mybir.dt.float32
BF16 = mybir.dt.bfloat16
I32 = mybir.dt.int32
ALU = mybir.AluOpType
ACT = mybir.ActivationFunctionType
AX = mybir.AxisListType

P = 128
LN_EPS = 1e-5
MOB_EPS = 1e-7
NEG = -1e30

G = 5
RB = 4
SLOTS = RB * G
W = 32
UPW = W // RB
CAP = 64
HIST_COLS = 25


class Steps:

    def __init__(self, eng, sem):
        self.eng, self.sem, self.n, self.seen = eng, sem, 0, 0

    def restart(self):
        self.eng.sem_clear(self.sem)
        self.n = self.seen = 0

    def go(self, ins):
        self.n += 1
        ins.then_inc(self.sem, 1)
        return self.n

    def link(self, ins):
        self.need(self.go(ins))

    def need(self, n):
        if n > self.seen:
            self.eng.wait_ge(self.sem, n)
            self.seen = n


def build_program(nc, x, src, dst, edge_attr, edge_type, W2n, att, conf, importance, bias2,
                  W1m, b1m, W2m, b2m, out):
    N, D = x.shape
    E = src.shape[0]
    NTILE = -(-N // P)
    NP = NTILE * P
    NGRP = NTILE // G
    T, H, K = W2n.shape[0], att.shape[1], att.shape[0]
    C = D // H
    HK = H * K
    LD = E // 125
    assert T & (T - 1) == 0 and NTILE % G == 0 and E % 125 == 0 and D == P and NP > N and LD % HIST_COLS == 0
    NCHUNK = LD // HIST_COLS
    deg_max = [E] + [E // (g * G * P) for g in range(1, NGRP)]
    NU = sum(-(-d // RB) + 1 for d in deg_max)
    NWIN = [-(-d // W) + 1 for d in deg_max]
    MW = D + 4
    TW = D + HK + T

    def dram(name, shape, dt=F32):
        return nc.dram_tensor(name, shape, dt, kind="Internal").ap()

    node_tab = dram("node_tab", [NP, 4], I32)
    h_tab = [dram(f"h_tab{i}", [NP, D]) for i in range(3)]
    m_tab = dram("m_tab", [NP, MW])
    t_tab = dram("t_tab", [NP, T * TW])
    edge_pad = dram("edge_pad", [E + W], I32)
    unit_hi = [sum(-(-d // RB) + 1 for d in deg_max[:g]) for g in range(NGRP + 1)]
    NLIST = max(unit_hi[g] + NWIN[g] * UPW for g in range(NGRP)) + 1
    slot_node = dram("slot_node", [NLIST, P, SLOTS], I32)
    slot_typed = dram("slot_typed", [NLIST, P, SLOTS], I32)

    def flat(ap):
        names = "abcd"[:len(ap.shape)]
        ap = ap.rearrange(" ".join(names) + " -> (" + " ".join(names) + ")") if len(ap.shape) > 1 else ap
        return ap.rearrange("(n o) -> n o", o=1)

    ctx = ExitStack()
    with ctx:
        made = {}

        def unique(name):
            made[name] = made.get(name, 0) + 1
            return name if made[name] == 1 else f"{name}_{made[name]}"

        def sb(name, shape, dt=F32, c=ctx):
            return c.enter_context(nc.sbuf_tensor(unique(name), shape, dt))

        def psum(name, shape, c):
            return c.enter_context(nc.psum_tensor(unique(name), shape, F32))

        def sem(name, c):
            return c.enter_context(nc.semaphore(unique(name)))

        X = sb("X", [P, NTILE, D])
        RES = sb("RES", [P, NTILE, D])
        O = sb("O", [P, NTILE, D])
        ATT = sb("ATT", [P, NTILE, D])
        node = sb("node", [P, NTILE, 4], I32)
        nodef = sb("nodef", [P, NTILE, 4])
        rdeg = sb("rdeg", [P, NTILE])
        real = sb("real", [P, NTILE])
        ctl = sb("ctl", [1, 64], I32)
        ident = sb("ident", [P, P])
        zeros = sb("zeros", [P, 4 * P])
        iota_w = sb("iota_w", [P, W])
        d2 = sb("d2", [P, NTILE])
        UB, WB, BB, CB = 0, 8, 24, 32

        def bounds(eng, at, n, lo, hi):
            return [eng.value_load(ctl[0:1, at + i:at + i + 1], min_val=lo[i], max_val=hi[i]) for i in range(n)]

        def unit_bounds(eng):
            return bounds(eng, UB, NGRP + 1, list(range(NGRP + 1)), unit_hi)

        with ExitStack() as c0:
            cnt = sb("cnt", [P, NTILE], F32, c0)
            low = sb("low", [P, P], F32, c0)
            high = sb("high", [P, P], F32, c0)
            ones = sb("ones", [P, P], F32, c0)
            nodeid = sb("nodeid", [P, NTILE], I32, c0)
            dsts = sb("dsts", [125, LD], I32, c0)
            dlo = sb("dlo", [125, LD], I32, c0)
            dhi = sb("dhi", [125, LD], I32, c0)
            dlof = sb("dlof", [125, LD], BF16, c0)
            dhif = sb("dhif", [125, LD], BF16, c0)
            iol = sb("iol", [P, P], BF16, c0)
            zi = sb("zi", [1, W], I32, c0)
            with ExitStack() as c1, nc.Block() as block:
                srcs = sb("srcs", [125, LD], I32, c1)
                types = sb("types", [125, LD], I32, c1)
                masked, filled, loaded, ends_in, joined, copied, split, cleared = (
                    sem(n, c1) for n in ("masked", "filled", "loaded", "ends_in", "joined", "copied", "split", "cleared"))

                @block.gpsimd
                def _(pool):
                    pool.memset(ident[:], 0.0).then_inc(filled, 1)
                    pool.memset(low[:], 1.0).then_inc(filled, 1)
                    pool.memset(high[:], 1.0).then_inc(filled, 1)
                    pool.wait_ge(filled, 3)
                    pool.affine_select(out=ident[:], in_=ident[:], compare_op=ALU.not_equal, fill=1.0, base=0,
                                       pattern=[[-1, P]], channel_multiplier=1).then_inc(masked, 1)
                    pool.affine_select(out=low[:], in_=low[:], compare_op=ALU.is_gt, fill=0.0, base=0,
                                       pattern=[[-1, P]], channel_multiplier=1).then_inc(masked, 1)
                    pool.affine_select(out=high[:], in_=high[:], compare_op=ALU.is_gt, fill=0.0, base=0,
                                       pattern=[[1, P]], channel_multiplier=-1).then_inc(masked, 1)
                    pool.iota(nodeid[:], pattern=[[P, NTILE]], base=0, channel_multiplier=1).then_inc(masked, 1)
                    pool.iota(iota_w[:], pattern=[[1, W]], base=0, channel_multiplier=0,
                              allow_small_or_imprecise_dtypes=True).then_inc(masked, 1)
                    pool.iota(iol[:], pattern=[[1, P]], base=0, channel_multiplier=0,
                              allow_small_or_imprecise_dtypes=True).then_inc(masked, 1)

                @block.sync
                def _(sp):
                    sp.dma_start(dsts[:], dst.rearrange("(p n) -> p n", p=125)).then_inc(loaded, 16)
                    sp.dma_start(srcs[:], src.rearrange("(p n) -> p n", p=125)).then_inc(ends_in, 16)
                    sp.dma_start(types[:], edge_type.rearrange("(p n) -> p n", p=125)).then_inc(ends_in, 16)
                    sp.dma_start(h_tab[0][0:N, :], x).then_inc(copied, 16)
                    sp.wait_ge(cleared, 2)
                    sp.dma_start(edge_pad[E:E + W].rearrange("(o n) -> o n", o=1), zi[:]).then_inc(copied, 16)
                    sp.dma_start(h_tab[0][N:NP, :], zeros[0:NP - N, 0:D]).then_inc(copied, 16)
                    sp.wait_ge(joined, 1)
                    sp.dma_start(edge_pad[0:E].rearrange("(p n) -> p n", p=125), types[:]).then_inc(copied, 16)
                    sp.wait_ge(copied, 64)

                @block.vector
                def _(dve):
                    dve.memset(zeros[:], 0.0).then_inc(cleared, 1)
                    dve.memset(zi[:], 0).then_inc(cleared, 1)
                    dve.memset(ones[:], 1.0).then_inc(split, 1)
                    dve.wait_ge(loaded, 16)
                    dve.tensor_scalar(dlo[:], dsts[:], P - 1, None, ALU.bitwise_and).then_inc(split, 1)
                    dve.tensor_scalar(dhi[:], dsts[:], 7, None, ALU.arith_shift_right).then_inc(split, 1)
                    dve.wait_ge(split, 3)
                    dve.tensor_copy(dlof[:], dlo[:]).then_inc(split, 1)
                    dve.tensor_copy(dhif[:], dhi[:]).then_inc(split, 1)
                    dve.wait_ge(ends_in, 32)
                    dve.scalar_tensor_tensor(out=types[:], in0=srcs[:], scalar=float(T), in1=types[:],
                                             op0=ALU.mult, op1=ALU.add).then_inc(joined, 1)

            with ExitStack() as c1:
                hlo = [sb(f"hlo{i}", [125, HIST_COLS, P], BF16, c1) for i in range(2)]
                hhi = [sb(f"hhi{i}", [125, HIST_COLS, NTILE], BF16, c1) for i in range(2)]
                zb = sb("zb", [P, P], BF16, c1)
                count_ps = psum("count_ps", [P, 512], c1)
                zeroed = sem("zeroed", c1)
                hot = [sem(f"hot{i}", c1) for i in range(2)]
                hot_used = [sem(f"hot_used{i}", c1) for i in range(2)]
                counted, degrees = sem("counted", c1), sem("degrees", c1)
                PAIRS = NCHUNK // 2

                def at(i, b):
                    return bass.ds(i * (2 * HIST_COLS) + b * HIST_COLS, HIST_COLS)

                def last_chunk():
                    return bass.ds(2 * PAIRS * HIST_COLS, HIST_COLS)

                with nc.Block() as block:
                    @block.vector
                    def _(dve):
                        def one_hots(b, cols):
                            dve.tensor_tensor(
                                hlo[b][:], iol[0:125, :].unsqueeze(1).to_broadcast([125, HIST_COLS, P]),
                                dlof[:, cols].unsqueeze(2).to_broadcast([125, HIST_COLS, P]), ALU.is_equal,
                            ).then_inc(hot[b], 1)
                            dve.tensor_tensor(
                                hhi[b][:], iol[0:125, 0:NTILE].unsqueeze(1).to_broadcast([125, HIST_COLS, NTILE]),
                                dhif[:, cols].unsqueeze(2).to_broadcast([125, HIST_COLS, NTILE]), ALU.is_equal,
                            ).then_inc(hot[b], 1)

                        dve.memset(zb[:], 0.0).then_inc(zeroed, 1)
                        with dve.Fori(0, PAIRS) as i:
                            for b in range(2):
                                dve.wait_ge(hot_used[b], i + 1)
                                one_hots(b, at(i, b))
                        dve.wait_ge(hot_used[0], PAIRS + 1)
                        one_hots(0, last_chunk())
                        dve.wait_ge(counted, 1)
                        dve.tensor_copy(cnt[:], count_ps[:, 0:NTILE]).then_inc(degrees, 1)

                    @block.tensor
                    def _(pe):
                        def products(b):
                            for j in range(HIST_COLS):
                                mm = pe.matmul(count_ps[:, 0:NTILE], hlo[b][:, j, :], hhi[b][:, j, :],
                                               start=False, stop=False, skip_group_check=True)
                            return mm

                        for b in range(2):
                            pe.sem_inc(hot_used[b], 1)
                        pe.wait_ge(zeroed, 1)
                        pe.matmul(count_ps[:, :], zb[:], zeros[:].bitcast(BF16)[:, 0:512], start=True, stop=False,
                                  skip_group_check=True)
                        with pe.Fori(0, PAIRS) as i:
                            for b in range(2):
                                pe.wait_ge(hot[b], 2 * i + 2)
                                products(b).then_inc(hot_used[b], 1)
                        pe.wait_ge(hot[0], 2 * PAIRS + 2)
                        products(0).then_inc(counted, 1)

            with ExitStack() as c1:
                diag = sb("diag", [P, NTILE, P], F32, c1)
                drow = sb("drow", [P, NP], F32, c1)
                junk = sb("junk", [P, NP], F32, c1)
                signs = sb("signs", [P, 2, NP], BF16, c1)
                below = sb("below", [P, NTILE], F32, c1)
                later = sb("later", [P, NTILE], F32, c1)
                tots = sb("tots", [P, NTILE], F32, c1)
                incl = sb("incl", [P, NTILE], F32, c1)
                onesc = sb("onesc", [P, NTILE], F32, c1)
                firstf = sb("firstf", [P, NTILE], F32, c1)
                part = sb("part", [P, 4, NTILE], F32, c1)
                posf = sb("posf", [P, NTILE], F32, c1)
                pos = sb("pos", [P, NTILE], I32, c1)
                rec = sb("rec", [P, NTILE, 4], I32, c1)
                cf = sb("cf", [1, 64], F32, c1)
                ci = sb("ci", [1, 64], I32, c1)
                row_ps = psum("row_ps", [P, 7 * 512], c1)
                pre_ps = psum("pre_ps", [P, 512], c1)
                diag_made, row_made, row_kept, prefixed, below_made, compared, ordered, placed, read_back, own = (
                    sem(n, c1) for n in ("diag_made", "row_made", "row_kept", "prefixed", "below_made", "compared",
                                         "ordered", "placed", "read_back", "own"))
                with nc.Block() as block:
                    @block.tensor
                    def _(pe):
                        pe.matmul(pre_ps[:, 0:NTILE], high[:], cnt[:], start=True, stop=True)
                        pe.matmul(pre_ps[:, 32:32 + NTILE], ones[:], cnt[:], start=True, stop=True).then_inc(prefixed, 1)
                        pe.wait_ge(diag_made, 1)
                        df = diag[:].rearrange("p t j -> p (t j)")
                        for b in range(-(-NP // 512)):
                            e = min(NP, 512 * b + 512)
                            mm = pe.matmul(row_ps[:, 512 * b:e], ones[:], df[:, 512 * b:e], start=True, stop=True)
                            mm.then_inc(row_made, 1)

                    @block.scalar
                    def _(act):
                        for b in range(-(-NP // 512)):
                            e = min(NP, 512 * b + 512)
                            act.wait_ge(row_made, b + 1)
                            act.activation(drow[:, 512 * b:e], row_ps[:, 512 * b:e], ACT.Copy).then_inc(row_kept, 1)
                        act.wait_ge(row_kept, -(-NP // 512))
                        act.wait_ge(below_made, 1)
                        for t in range(NTILE - 1):
                            if t >= 2:
                                act.wait_ge(compared, t - 1)
                            act.activation(signs[:, t % 2, (t + 1) * P:], drow[:, (t + 1) * P:], ACT.Sign, bias=below[:, t:t + 1],
                                           accum_out=part[:, 1, t:t + 1]).then_inc(compared, 1)

                    @block.vector
                    def _(dve):
                        s = Steps(dve, own)
                        dve.tensor_tensor(diag[:], ident[:].unsqueeze(1).to_broadcast([P, NTILE, P]),
                                          cnt[:].unsqueeze(2).to_broadcast([P, NTILE, P]), ALU.mult).then_inc(diag_made, 1)
                        s.link(dve.memset(onesc[:], 1.0))
                        s.link(dve.memset(part[:], 0.0))
                        s.link(dve.tensor_scalar(below[:], cnt[:], -1.0, -0.5, ALU.mult, ALU.add))
                        dve.sem_inc(below_made, 1)
                        for t in range(NTILE):
                            s.go(dve.memset(later[:, t:t + 1], float((NTILE - 1 - t) * P)))
                        s.need(s.n)
                        dve.wait_ge(prefixed, 1)
                        s.link(dve.tensor_copy(tots[:], pre_ps[:, 32:32 + NTILE]))
                        s.link(dve.tensor_tensor_scan(incl[:], onesc[:], tots[:], 0.0, ALU.mult, ALU.add))
                        s.link(dve.tensor_tensor(incl[:], incl[:], tots[:], ALU.subtract))
                        s.link(dve.tensor_tensor(firstf[:], incl[:], pre_ps[:, 0:NTILE], ALU.add))
                        dve.wait_ge(row_kept, -(-NP // 512))
                        for t in range(NTILE):
                            mine = drow[:, t * P:(t + 1) * P]
                            deg = cnt[:, t:t + 1]
                            if t:
                                s.go(dve.tensor_scalar(junk[:, 0:t * P], drow[:, 0:t * P], deg, 0.0, ALU.is_ge, ALU.add,
                                                       accum_out=part[:, 0, t:t + 1]))
                            s.go(dve.scalar_tensor_tensor(out=diag[:, 0, :], in0=mine, scalar=deg, in1=low[:],
                                                          op0=ALU.is_ge, op1=ALU.mult, accum_out=part[:, 2, t:t + 1]))
                            s.link(dve.scalar_tensor_tensor(out=diag[:, 1, :], in0=mine, scalar=deg, in1=high[:],
                                                            op0=ALU.is_gt, op1=ALU.mult, accum_out=part[:, 3, t:t + 1]))
                        dve.wait_ge(compared, NTILE - 1)
                        s.link(dve.tensor_tensor(part[:, 1, :], part[:, 1, :], later[:], ALU.add))
                        s.link(dve.tensor_scalar(part[:, 1, :], part[:, 1, :], 0.5, None, ALU.mult))
                        s.link(dve.tensor_reduce(posf[:], part[:].rearrange("p a t -> p t a"), AX.X, ALU.add))
                        s.go(dve.tensor_copy(pos[:], posf[:]))
                        s.go(dve.memset(rec[:], 0))
                        s.need(s.n)
                        s.go(dve.tensor_copy(rec[:, :, 0], firstf[:]))
                        s.go(dve.tensor_copy(rec[:, :, 1], cnt[:]))
                        s.go(dve.tensor_copy(rec[:, :, 2], nodeid[:]))
                        s.need(s.n)
                        dve.sem_inc(ordered, 1)
                        dve.wait_ge(read_back, 16)
                        s.link(dve.tensor_copy(nodef[:], node[:]))
                        s.link(dve.tensor_scalar(rdeg[:], nodef[:, :, 1], 1.0, None, ALU.max))
                        s.link(dve.reciprocal(rdeg[:], rdeg[:]))
                        s.link(dve.tensor_scalar(real[:], nodef[:, :, 2], float(N), None, ALU.is_lt))
                        top = node[0:1, 0:NTILE:G, 1]
                        for at0, span in ((UB, RB), (24, W)):
                            raw = ci[:, at0:at0 + NGRP]
                            s.link(dve.tensor_copy(raw, top))
                            s.link(dve.tensor_scalar(raw, raw, span - 1, None, ALU.add))
                            s.link(dve.tensor_scalar(raw, raw, span.bit_length() - 1, None, ALU.arith_shift_right))
                            s.link(dve.tensor_scalar(raw, raw, 1, None, ALU.max))
                        s.link(dve.memset(ctl[:], 0))
                        s.link(dve.tensor_copy(ctl[:, WB:WB + NGRP], ci[:, 24:24 + NGRP]))
                        s.link(dve.tensor_copy(cf[:, UB:UB + NGRP], ci[:, UB:UB + NGRP]))
                        s.link(dve.tensor_tensor_scan(cf[:, 32 + UB:32 + UB + NGRP], onesc[0:1, 0:NGRP],
                                                      cf[:, UB:UB + NGRP], 0.0, ALU.mult, ALU.add))
                        s.link(dve.tensor_copy(ctl[:, UB + 1:UB + 1 + NGRP], cf[:, 32 + UB:32 + UB + NGRP]))
                        s.link(dve.tensor_scalar(ctl[:, BB:BB + NGRP + 1], ctl[:, UB:UB + NGRP + 1], CAP, None, ALU.min))
                        s.link(dve.tensor_scalar(ctl[:, CB:CB + NGRP + 1], ctl[:, UB:UB + NGRP + 1], CAP, None, ALU.max))
                        s.link(dve.tensor_scalar(ctl[:, CB:CB + NGRP + 1], ctl[:, CB:CB + NGRP + 1], -CAP, None, ALU.add))

                    @block.gpsimd
                    def _(pool):
                        pool.wait_ge(ordered, 1)
                        for t in range(NTILE):
                            pool.indirect_dma_start(node_tab, bass.IndirectOffsetOnAxis(ap=pos[:, t:t + 1], axis=0),
                                                    rec[:, t, :], None).then_inc(placed, 16)

                    @block.sync
                    def _(sp):
                        sp.wait_ge(placed, 16 * NTILE)
                        sp.dma_start(node[:], node_tab.rearrange("(t p) c -> p t c", p=P)).then_inc(read_back, 16)
                        sp.wait_ge(read_back, 16)

        pk = sb("pk", [P, HK])
        imp = sb("imp", [P, T])
        Wj = sb("Wj", [P, T, D + HK])
        Wi = sb("Wi", [P, T * HK])
        bias = sb("bias", [P, D])
        hot = sb("hot", [P, T, T])
        with ExitStack() as c1:
            offi = sb("offi", [P, G], I32, c1)
            off = sb("off", [P, G], F32, c1)
            window = sb("window", [P, G, W], I32, c1)
            end = sb("end", [P, NTILE], F32, c1)
            start_of = sb("start_of", [P, NTILE], F32, c1)
            val = sb("val", [P, G, W], F32, c1)
            tf = sb("tf", [P, G, W], F32, c1)
            pn = sb("pn", [P, UPW, RB, G], I32, c1)
            pt = sb("pt", [P, UPW, RB, G], I32, c1)
            Wt = sb("Wt", [P, T, D], F32, c1)
            WT = sb("WT", [P, T, D], F32, c1)
            A2 = sb("A2", [P, 2, H, K], F32, c1)
            cf = sb("cf", [P, K], F32, c1)
            cs = sb("cs", [P, 4], F32, c1)
            turn_ps = psum("wturn_ps", [P, 2, 512], c1)
            loaded, zeroed, turned, kept, vecs, vkept, exp_in, exp_out = (
                sem(n, c1) for n in ("loaded", "zeroed", "turned", "kept", "vecs", "vkept", "exp_in", "exp_out"))
            LOADS = 16 * (4 + 2 * H * K)
            offsets, windows, listed, written, list_free, own, gone, features, marker = (
                sem(n, c1) for n in ("offsets", "windows", "listed", "written", "list_free", "own", "gone",
                                     "features", "marker"))
            with nc.Block() as block:
                def each_turn(eng, body, after=None):
                    wn = bounds(eng, WB, NGRP, [1] * NGRP, NWIN)
                    ub = unit_bounds(eng)
                    first = 0
                    for g in range(NGRP):
                        with eng.Fori(0, wn[g]) as w:
                            body(g, w, first + w, ub[g])
                        if after:
                            after(g)
                        first = first + wn[g]
                    return first

                @block.tensor
                def _(pe):
                    pe.wait_ge(loaded, LOADS)
                    for t in range(T):
                        pe.transpose(turn_ps[:, 0, t * D:(t + 1) * D], Wt[:, t, :], ident[:]).then_inc(turned, 1)
                    pe.wait_ge(kept, 1)
                    for t in range(T):
                        pe.matmul(turn_ps[:, 1, t * 64:t * 64 + 2 * HK], WT[:, t, :],
                                  A2[:].rearrange("p s h k -> p (s h k)"), start=True, stop=True).then_inc(vecs, 1)
                    pe.wait_ge(vkept, 1)

                @block.scalar
                def _(act):
                    act.dma_start(Wt[:], W2n.rearrange("t i o -> i t o")).then_inc(loaded, 16)
                    act.dma_start(cf[:], conf.rearrange("(o k) -> o k", o=1).to_broadcast([P, K])).then_inc(loaded, 16)
                    act.dma_start(imp[:], importance.rearrange("(o k) -> o k", o=1).to_broadcast([P, T])).then_inc(loaded, 16)
                    act.dma_start(bias[:], bias2.rearrange("(o k) -> o k", o=1).to_broadcast([P, D])).then_inc(loaded, 16)
                    act.wait_ge(zeroed, 1)
                    with nc.allow_non_contiguous_dma("1280 values, once"):
                        for h in range(H):
                            for side, at in ((0, C), (1, 0)):
                                for k in range(K):
                                    act.dma_start(A2[h * C:(h + 1) * C, side, h, k:k + 1],
                                                 att[k, h, at:at + C].rearrange("(c o) -> c o", o=1)).then_inc(loaded, 16)
                    act.wait_ge(exp_in, 1)
                    act.activation(cf[:], cf[:], ACT.Exp, accum_out=cs[:, 1:2]).then_inc(exp_out, 1)

                @block.gpsimd
                def _(pool):
                    def own_features(g):
                        for t in range(g * G, g * G + G):
                            pool.indirect_dma_start(X[:, t, :], None, h_tab[0],
                                                    bass.IndirectOffsetOnAxis(ap=node[:, t, 2:3], axis=0)
                                                    ).then_inc(features, 16)

                    def body(g, w, turn, u0):
                        pool.wait_ge(offsets, turn + 1)
                        pool.sem_inc(marker, 1)
                        for k in range(G):
                            pool.indirect_dma_start(window[:, k, :], None, flat(edge_pad),
                                                    bass.IndirectOffsetOnAxis(ap=offi[:, k:k + 1], axis=0)).then_inc(windows, 16)

                    each_turn(pool, body, after=own_features)
                    pool.wait_ge(features, 16 * NTILE)

                @block.vector
                def _(dve):
                    s = Steps(dve, own)
                    dve.tensor_tensor(end[:], nodef[:, :, 0], nodef[:, :, 1], ALU.add).then_inc(gone, 1)
                    dve.wait_ge(gone, 1)

                    def body(g, w, turn, u0):
                        s.restart()
                        cols = slice(g * G, (g + 1) * G)
                        s.link(dve.tensor_scalar(off[:], start_of[:, cols], float(E), None, ALU.min))
                        dve.tensor_copy(offi[:], off[:]).then_inc(offsets, 1)
                        s.link(dve.tensor_tensor(val[:], iota_w[:].unsqueeze(1).to_broadcast([P, G, W]),
                                                 off[:].unsqueeze(2).to_broadcast([P, G, W]), ALU.add))
                        s.link(dve.tensor_tensor(val[:], val[:], end[:, cols].unsqueeze(2).to_broadcast([P, G, W]), ALU.is_lt))
                        s.link(dve.tensor_scalar(start_of[:, cols], start_of[:, cols], float(W), None, ALU.add))
                        dve.wait_ge(windows, (turn + 1) * (G * 16))
                        dve.wait_ge(list_free, turn + 1)
                        s.link(dve.scalar_tensor_tensor(out=tf[:], in0=window[:], scalar=float(-N * T), in1=val[:],
                                                        op0=ALU.add, op1=ALU.mult))
                        s.link(dve.tensor_scalar(pt[:].rearrange("p u r k -> p (u r) k"), tf[:].rearrange("p k w -> p w k"),
                                                 float(N * T), None, ALU.add))
                        s.link(dve.tensor_scalar(pn[:], pt[:], T.bit_length() - 1, None, ALU.arith_shift_right))
                        dve.sem_inc(listed, 1)

                    dve.tensor_copy(start_of[:], nodef[:, :, 0]).then_inc(gone, 1)
                    dve.wait_ge(gone, 2)
                    dve.memset(A2[:], 0.0).then_inc(zeroed, 1)
                    each_turn(dve, body)
                    s.restart()
                    s.link(dve.memset(hot[:], 0.0))
                    for t in range(T):
                        s.go(dve.memset(hot[:, t, t:t + 1], 1.0))
                    dve.wait_ge(loaded, LOADS)
                    s.link(dve.tensor_reduce(cs[:, 0:1], cf[:], AX.X, ALU.max))
                    s.link(dve.tensor_scalar(cf[:], cf[:], cs[:, 0:1], None, ALU.subtract))
                    dve.sem_inc(exp_in, 1)
                    dve.wait_ge(exp_out, 1)
                    s.link(dve.reciprocal(cs[:, 2:3], cs[:, 1:2]))
                    s.link(dve.tensor_scalar(cf[:], cf[:], cs[:, 2:3], None, ALU.mult))
                    s.link(dve.tensor_copy(pk[:].rearrange("p (h k) -> p h k", h=H),
                                           cf[:].unsqueeze(1).to_broadcast([P, H, K])))
                    dve.wait_ge(turned, T)
                    s.go(dve.tensor_copy(Wj[:, :, 0:D], Wt[:]))
                    s.link(dve.tensor_copy(WT[:].rearrange("p t d -> p (t d)"), turn_ps[:, 0, :]))
                    dve.sem_inc(kept, 1)
                    dve.wait_ge(vecs, T)
                    vps = turn_ps[:, 1, 0:T * 64].rearrange("p (t n) -> p t n", n=64)
                    s.link(dve.tensor_copy(Wj[:, :, D:D + HK], vps[:, :, 0:HK]))
                    s.link(dve.tensor_copy(Wi[:].rearrange("p (t n) -> p t n", t=T), vps[:, :, HK:2 * HK]))
                    dve.sem_inc(vkept, 1)

                @block.sync
                def _(sp):
                    def body(g, w, turn, u0):
                        sp.wait_ge(listed, turn + 1)
                        at = bass.ds(u0 + w * UPW, UPW)
                        sp.dma_start(slot_node[at].rearrange("u p s -> p u s"),
                                     pn[:].rearrange("p u r k -> p u (r k)")).then_inc(written, 16)
                        sp.dma_start(slot_typed[at].rearrange("u p s -> p u s"),
                                     pt[:].rearrange("p u r k -> p u (r k)")).then_inc(written, 16)
                        sp.wait_ge(written, (turn + 1) * 32)
                        sp.sem_inc(list_free, 1)

                    sp.sem_inc(list_free, 1)
                    turns = each_turn(sp, body)
                    past = bass.ds(bounds(sp, UB + NGRP, 1, [NGRP], [unit_hi[NGRP]])[0], 1)
                    for lists, mine in ((slot_node, pn), (slot_typed, pt)):
                        sp.dma_start(lists[past].rearrange("u p s -> p (u s)"),
                                     mine[:, 0].rearrange("p r k -> p (r k)")).then_inc(written, 16)
                    sp.wait_ge(written, turns * 32 + 32)
                    sp.sem_inc(marker, 1)

        def load_slots(sp, lists, slot, slots_in, rows_in, units=None, first=0):
            if units is None:
                units = bounds(sp, UB + NGRP, 1, [NGRP], [unit_hi[NGRP]])[0]

            def load(u, q):
                sp.dma_start(slot[q][:], lists[bass.ds(u + first, 1), :, q * G:(q + 1) * G]
                             .rearrange("o p k -> (o p) k")).then_inc(slots_in[q], 16)

            for q in range(RB):
                load(0, q)
            with sp.Fori(0, units) as u:
                for q in range(RB):
                    sp.wait_ge(rows_in[q], (16 * G) * u + 16 * G)
                    load(u + 1, q)
            for q in range(RB):
                sp.wait_ge(slots_in[q], 16 * units + 16)
                sp.sem_inc(pass_marker, 1)

        def gather_rank(pool, u, q, table, slot, rows, slots_in, rows_in, rows_free, marker):
            pool.wait_ge(slots_in[q], 16 * u + 16)
            pool.wait_ge(rows_free[q], u + 1)
            pool.sem_inc(marker, 1)
            for k in range(G):
                pool.indirect_dma_start(rows[q][:, k, :], None, table,
                                        bass.IndirectOffsetOnAxis(ap=slot[q][:, k:k + 1], axis=0)
                                        ).then_inc(rows_in[q], 16)

        def gather_unit(pool, u, table, slot, rows, slots_in, rows_in, rows_free, marker):
            for q in range(RB):
                gather_rank(pool, u, q, table, slot, rows, slots_in, rows_in, rows_free, marker)

        def scatter_group(pool, g, table, rows_of, stored):
            for k in range(G):
                t = g * G + k
                pool.indirect_dma_start(table, bass.IndirectOffsetOnAxis(ap=node[:, t, 2:3], axis=0),
                                        rows_of(t), None).then_inc(stored, 16)

        pass_sems = [[sem(f"{name}{q}", ctx) for q in range(RB)] for name in ("slots_in", "rows_free")]
        pass_marker = sem("pass_marker", ctx)
        out_stored = sem("out_stored", ctx)
        passes = [0]

        def pass_memory(c, width, pairs=False):
            if passes[0]:
                with nc.Block() as block:
                    @block.sync
                    def _(sp):
                        for one in (*pass_sems[0], *pass_sems[1], pass_marker):
                            sp.sem_clear(one)
            passes[0] += 1
            if pairs:
                rows = [sb(f"pair{p}", [P, 2, G, width], F32, c) for p in range(RB // 2)]
            else:
                rows = [sb(f"rows{q}", [P, G, width], F32, c) for q in range(RB)]
            slot = [sb(f"slot{q}", [P, G], I32, c) for q in range(RB)]
            rows_in = [sem(f"rows_in{q}", ctx) for q in range(RB)]
            return rows, slot, pass_sems[0], rows_in, pass_sems[1], pass_marker

        def add_rows(pe, acc, rows, start=False):
            pe.matmul(acc[:, 0:4 * P].rearrange("p (k d) -> p k d", k=4), ident[:], rows[:, 0:4, 0:D],
                      start=start, stop=False, skip_group_check=True)
            return pe.matmul(acc[:, 4 * P:5 * P], ident[:], rows[:, 4, 0:D], start=start, stop=False,
                             skip_group_check=True)

        def clear_sums(pe, acc):
            pe.matmul(acc[:, 0:4 * P], ident[:], zeros[:], start=True, stop=False, skip_group_check=True)
            pe.matmul(acc[:, 4 * P:5 * P], ident[:], zeros[:, 0:P], start=True, stop=False, skip_group_check=True)

        def cols(g):
            return slice(g * G, (g + 1) * G)

        def wide(ap, n=D):
            return ap.unsqueeze(2).to_broadcast([P, G, n])

        def normalise(s, dve, act_std, g, A, B, st, std_in, std_out, turn):
            a, b = A[:, cols(g), :], B[:]
            s.link(dve.tensor_reduce(st[:, 0, :], a, AX.X, ALU.add))
            s.link(dve.tensor_scalar(st[:, 0, :], st[:, 0, :], 1.0 / D, None, ALU.mult))
            s.link(dve.tensor_tensor(a, a, wide(st[:, 0, :]), ALU.subtract))
            s.link(dve.tensor_tensor(b, a, a, ALU.mult))
            s.link(dve.tensor_reduce(st[:, 1, :], b, AX.X, ALU.add))
            dve.tensor_scalar(st[:, 1, :], st[:, 1, :], 1.0 / D, LN_EPS, ALU.mult, ALU.add).then_inc(std_in, 1)
            dve.wait_ge(std_out, turn + 1)
            s.link(dve.reciprocal(st[:, 3, :], st[:, 2, :]))
            s.link(dve.tensor_tensor(a, a, wide(st[:, 3, :]), ALU.mult))

        def roots(act, st, std_in, std_out, turn):
            act.wait_ge(std_in, turn + 1)
            act.activation(st[:, 2, :], st[:, 1, :], ACT.Sqrt).then_inc(std_out, 1)

        for layer in range(3):
            with ExitStack() as c1:
                rows, slot, slots_in, rows_in, rows_free, marker = pass_memory(c1, D)
                acc = psum("acc", [P, 2, 1024], c1)
                own, summed, stored = sem("own", c1), sem("summed", c1), sem("stored", c1)
                with nc.Block() as block:
                    @block.sync
                    def _(sp):
                        load_slots(sp, slot_node, slot, slots_in, rows_in)

                    @block.gpsimd
                    def _(pool):
                        ub = unit_bounds(pool)

                        def store(g):
                            pool.wait_ge(summed, g + 1)
                            scatter_group(pool, g, h_tab[layer + 1], lambda t: X[:, t, :], stored)

                        for g in range(NGRP):
                            with pool.Fori(ub[g], ub[g + 1]) as u:
                                gather_unit(pool, u, h_tab[layer], slot, rows, slots_in, rows_in, rows_free, marker)
                            if g and layer < 2:
                                store(g - 1)
                        if layer < 2:
                            store(NGRP - 1)
                            pool.wait_ge(stored, 16 * NTILE)

                    @block.tensor
                    def _(pe):
                        ub = unit_bounds(pe)
                        for q in range(RB):
                            pe.sem_inc(rows_free[q], 1)
                        for g in range(NGRP):
                            if g >= 2:
                                pe.wait_ge(summed, g - 1)
                            clear_sums(pe, acc[:, g % 2, :])
                            with pe.Fori(ub[g], ub[g + 1]) as u:
                                for q in range(RB):
                                    pe.wait_ge(rows_in[q], (16 * G) * u + 16 * G)
                                    add_rows(pe, acc[:, g % 2, :], rows[q]).then_inc(rows_free[q], 1)

                    @block.vector
                    def _(dve):
                        ub = unit_bounds(dve)
                        s = Steps(dve, own)
                        for g in range(NGRP):
                            if layer == 0:
                                s.link(dve.tensor_scalar(RES[:, cols(g), :], X[:, cols(g), :], 2.0, None, ALU.mult))
                            dve.wait_ge(rows_free[RB - 1], ub[g + 1] + 1)
                            for k in range(G):
                                t = g * G + k
                                s.go(dve.scalar_tensor_tensor(
                                    out=X[:, t, :], in0=acc[:, g % 2, k * P:(k + 1) * P], scalar=rdeg[:, t:t + 1],
                                    in1=X[:, t, :], op0=ALU.mult, op1=ALU.add))
                            s.need(s.n)
                            dve.sem_inc(summed, 1)
                            for k in range(G):
                                t = g * G + k
                                s.go(dve.scalar_tensor_tensor(
                                    out=RES[:, t, :], in0=X[:, t, :], scalar=1.0 / (1.0 + layer),
                                    in1=RES[:, t, :], op0=ALU.mult, op1=ALU.add))
                        s.need(s.n)

        with ExitStack() as c1:
            stage = [sb(f"stage{i}", [P, G, MW], F32, c1) for i in range(2)]
            sq = sb("sq", [P, G, D], F32, c1)
            st = sb("st", [P, 4, G], F32, c1)
            own, std_in, std_out, staged = (sem(n, c1) for n in ("own", "std_in", "std_out", "staged"))
            stored = [sem(f"stored{i}", c1) for i in range(2)]
            with nc.Block() as block:
                @block.vector
                def _(dve):
                    s = Steps(dve, own)
                    for i in range(2):
                        s.go(dve.memset(stage[i][:], 0.0))
                    for g in range(NGRP):
                        normalise(s, dve, None, g, RES, sq, st, std_in, std_out, g)
                        x1 = RES[:, cols(g), :]
                        s.link(dve.tensor_copy(X[:, cols(g), :], x1))
                        s.link(dve.tensor_tensor(sq[:], x1, x1, ALU.mult))
                        s.link(dve.tensor_reduce(d2[:, cols(g)], sq[:], AX.X, ALU.add))
                        if g >= 2:
                            dve.wait_ge(stored[g % 2], 16 * G * (g // 2))
                        b = stage[g % 2]
                        s.go(dve.tensor_copy(b[:, :, 0:D], x1))
                        s.go(dve.tensor_copy(b[:, :, D], d2[:, cols(g)]))
                        s.go(dve.tensor_copy(b[:, :, D + 1], real[:, cols(g)]))
                        s.need(s.n)
                        dve.sem_inc(staged, 1)

                @block.scalar
                def _(act):
                    for g in range(NGRP):
                        roots(act, st, std_in, std_out, g)

                @block.gpsimd
                def _(pool):
                    for g in range(NGRP):
                        pool.wait_ge(staged, g + 1)
                        scatter_group(pool, g, m_tab, lambda t: stage[g % 2][:, t - g * G, :], stored[g % 2])
                    pool.wait_ge(stored[0], 16 * G * ((NGRP + 1) // 2))
                    pool.wait_ge(stored[1], 16 * G * (NGRP // 2))

        with ExitStack() as c1:
            gam = sb("gam", [P, NTILE], F32, c1)
            with ExitStack() as c2:
                rows, slot, slots_in, rows_in, rows_free, marker = pass_memory(c2, MW)
                junk = sb("junk", [P, 2 * G, D], F32, c2)
                us = sb("us", [P, G, D], F32, c2)
                gp = sb("gp", [P, NGRP, 2, G], F32, c2)
                o2 = sb("o2", [P, NGRP, G], F32, c2)
                two = lambda name, n: [sb(f"{name}{i}", [P, n, G], F32, c2) for i in range(2)]
                sdd, den, nn, mix, mm = two("sdd", 3), two("den", 2), two("nn", 2), two("mix", 3), two("mm", 4)
                tmp, one = two("tmp", 4), two("one", 2)
                s3 = sb("s3", [P, 3, G], F32, c2)
                p3 = sb("p3", [P, 3, G], F32, c2)
                quad = sb("quad", [P, 4, G], F32, c2)
                ab = sb("ab", [P, 2, G], F32, c2)
                nb = sb("nb", [P, 2, G], F32, c2)
                bab = sb("bab", [P, 2, G], F32, c2)
                dn = sb("dn", [P, G], F32, c2)
                z4 = sb("z4", [P, 4, G], F32, c2)
                z2 = sb("z2", [P, 2, G], F32, c2)
                w2 = sb("w2", [P, 2, G], F32, c2)
                g2 = sb("g2", [P, 2, G], F32, c2)
                own, scaled, scale_in = sem("own", c2), sem("scaled", c2), sem("scale_in", c2)
                attr = [sb(f"attr{k}", [P, RB, D], F32, c2) for k in range(G)]
                offs = sb("offs", [P, G], I32, c2)
                off = sb("off", [P, G], F32, c2)
                at0 = sb("at0", [P, NTILE], F32, c2)
                end = sb("end", [P, NTILE], F32, c2)
                eid = sb("eid", [P, G, RB], F32, c2)
                val = sb("val", [P, G, RB], F32, c2)
                val2 = sb("val2", [P, G, RB], F32, c2)
                acc = psum("acc", [P, 2, 1024], c2)
                offsets, masked, added, summed = (sem(n, c2) for n in ("offsets", "masked", "added", "summed"))
                attr_in = [sem(f"attr_in{k}", c2) for k in range(G)]
                mask_after = {1: (0, 1), 2: (2, 3), 3: (4,)}
                with nc.Block() as block:
                    @block.sync
                    def _(sp):
                        load_slots(sp, slot_node, slot, slots_in, rows_in)

                    @block.gpsimd
                    def _(pool):
                        ub = unit_bounds(pool)
                        for g in range(NGRP):
                            with pool.Fori(ub[g], ub[g + 1]) as u:
                                gather_unit(pool, u, m_tab, slot, rows, slots_in, rows_in, rows_free, marker)
                                pool.wait_ge(offsets, u + 1)
                                pool.wait_ge(added, u + 1)
                                pool.sem_inc(marker, 1)
                                for k in range(G):
                                    pool.indirect_dma_start(attr[k][:].rearrange("p r d -> p (r d)"), None, flat(edge_attr),
                                                            bass.IndirectOffsetOnAxis(ap=offs[:, k:k + 1], axis=0)
                                                            ).then_inc(attr_in[k], 16)
                        for q in range(2):
                            gather_rank(pool, ub[NGRP], q, m_tab, slot, rows, slots_in, rows_in, rows_free, marker)

                    @block.tensor
                    def _(pe):
                        ub = unit_bounds(pe)
                        pe.sem_inc(added, 1)
                        for g in range(NGRP):
                            if g >= 2:
                                pe.wait_ge(summed, g - 1)
                            clear_sums(pe, acc[:, g % 2, :])
                            with pe.Fori(ub[g], ub[g + 1]) as u:
                                for k in range(G):
                                    pe.wait_ge(masked, u * G + (G + k + 1))
                                    for r in range(RB):
                                        mm = pe.matmul(acc[:, g % 2, k * P:(k + 1) * P], ident[:], attr[k][:, r, :],
                                                       start=False, stop=False, skip_group_check=True)
                                mm.then_inc(added, 1)

                    @block.scalar
                    def _(act):
                        ub = unit_bounds(act)
                        for g in range(NGRP):
                            with act.Fori(ub[g], ub[g + 1]) as u:
                                for q in range(RB):
                                    act.wait_ge(scale_in, u * RB + (q + 1))
                                    for k in range(G):
                                        a = act.activation(us[:, k, :], O[:, g * G + k, :], ACT.Copy,
                                                           scale=ab[:, 0, k:k + 1])
                                    a.then_inc(scaled, 1)
                                    for k in mask_after.get(q, ()):
                                        act.wait_ge(attr_in[k], 16 * u + 16)
                                        for r in range(RB):
                                            a = act.activation(attr[k][:, r, :], attr[k][:, r, :], ACT.Copy,
                                                               scale=val[:, k, r:r + 1])
                                        a.then_inc(masked, 1)
                            act.wait_ge(added, ub[g + 1] + 1)
                            act.activation(ATT[:, cols(g), :], acc[:, g % 2, 0:5 * P].rearrange("p (k d) -> p k d", k=G),
                                           ACT.Copy).then_inc(summed, 1)
                        act.wait_ge(summed, NGRP)

                    @block.vector
                    def _(dve):
                        ub = unit_bounds(dve)
                        s = Steps(dve, own)
                        TT, TS, STT = dve.tensor_tensor, dve.tensor_scalar, dve.scalar_tensor_tensor

                        for a in (O, gp, o2):
                            s.go(dve.memset(a[:], 0.0))
                        s.go(TT(end[:], nodef[:, :, 0], nodef[:, :, 1], ALU.add))
                        s.go(dve.tensor_copy(at0[:], nodef[:, :, 0]))
                        dve.sem_inc(masked, G)
                        s.need(s.n)
                        for q in range(RB):
                            dve.sem_inc(rows_free[q], 1)

                        def each(ap, n):
                            return ap.unsqueeze(1).to_broadcast([P, n, G])

                        def dots(g, u, q):
                            dve.wait_ge(rows_in[q], (16 * G) * u + 16 * G)
                            for k in range(G):
                                dotted[q % 2] = s.go(dve.tensor_tensor_reduce(
                                    junk[:, k, :], rows[q][:, k, 0:D], X[:, g * G + k, :], 1.0, 0.0,
                                    ALU.mult, ALU.add, sdd[q % 2][:, 1, k:k + 1]))

                        def message(g, u, q):
                            R, c, i = rows[q], cols(g), q % 2
                            s2, valid = R[:, :, D], R[:, :, D + 1]
                            sd, dot, dd = sdd[i], sdd[i][:, 1, :], d2[:, c]
                            c0 = s.go(dve.tensor_copy(sd[:, 0, :], s2))
                            c2_ = s.go(dve.tensor_copy(sd[:, 2, :], dd))
                            s.go(TT(den[i][:, 0, :], s2, dd, ALU.mult))
                            e1 = s.go(TS(nn[i][:, 1, :], s2, -1.0, None, ALU.add))
                            yield
                            s.need(dotted[i])
                            t = s.go(TS(tmp[i][:, 0, :], dot, -2.0, 1.0, ALU.mult, ALU.add))
                            yield
                            s.need(t)
                            t1 = s.go(TT(den[i][:, 0, :], den[i][:, 0, :], tmp[i][:, 0, :], ALU.add))
                            e0 = s.go(TT(nn[i][:, 0, :], tmp[i][:, 0, :], dd, ALU.add))
                            yield
                            s.need(t1)
                            t = s.go(TS(den[i][:, 0, :], den[i][:, 0, :], MOB_EPS, None, ALU.max))
                            yield
                            s.need(t)
                            t = s.go(dve.reciprocal(den[i][:, 0, :], den[i][:, 0, :]))
                            yield
                            s.need(t)
                            t = s.go(TT(den[i][:, 0, :], den[i][:, 0, :], valid, ALU.mult))
                            yield
                            s.need(t)
                            t = s.go(TT(mix[i][:, 0:3:2, :], nn[i][:], each(den[i][:, 0, :], 2), ALU.mult))
                            yield
                            s.need(t)
                            al, be = mix[i][:, 0, :], mix[i][:, 2, :]
                            s.go(TT(tmp[i][:, 0:2, :], sd[:, 0:2, :], each(al, 2), ALU.mult))
                            t1 = s.go(TT(tmp[i][:, 2:4, :], sd[:, 1:3, :], each(be, 2), ALU.mult))
                            yield
                            s.need(t1)
                            s.go(dve.tensor_copy(mix[i][:, 1, :], tmp[i][:, 1, :]))
                            t = s.go(TT(mm[i][:, 0:2, :], tmp[i][:, 0:2, :], tmp[i][:, 2:4, :], ALU.add))
                            yield
                            s.need(t)
                            t = s.go(TT(tmp[i][:, 0:2, :], mm[i][:, 0:2, :], mix[i][:, 0:3:2, :], ALU.mult))
                            yield
                            s.need(t)
                            t = s.go(TT(mm[i][:, 2, :], tmp[i][:, 0, :], tmp[i][:, 1, :], ALU.add))
                            yield
                            s.need(t)
                            t = s.go(TS(mm[i][:, 3, :], mm[i][:, 2, :], 1.0, None, ALU.add))
                            ready[i] = t
                            yield

                        def add_message(g, u, q, side, after_next):
                            R, i = rows[q], q % 2
                            G2, S2 = gp[:, g], o2[:, g, :]
                            y2, mp = mm[i][:, 2, :], mm[i][:, 1, :]
                            for k in range(G):
                                ux = s.go(dve.tensor_tensor_reduce(junk[:, G + k, :], R[:, k, 0:D], O[:, g * G + k, :], 1.0, 0.0,
                                                                   ALU.mult, ALU.add, s3[:, 0, k:k + 1]))
                            s.need(ready[i])
                            s.go(dve.tensor_copy(s3[:, 1:3, :], G2))
                            s.go(dve.tensor_copy(quad[:, 0, :], S2))
                            s.go(dve.tensor_copy(quad[:, 3, :], y2))
                            s.go(TS(nb[:, 1, :], S2, -1.0, 1.0, ALU.mult, ALU.add))
                            xx = s.go(TT(tmp[i][:, 0, :], S2, y2, ALU.mult))
                            s.need(xx)
                            t = s.go(TT(p3[:], s3[:], mix[i][:], ALU.mult))
                            next(side, None)
                            s.need(t)
                            t = s.go(TT(dn[:], p3[:, 0, :], p3[:, 1, :], ALU.add))
                            next(side, None)
                            s.need(t)
                            xy = quad[:, 1, :]
                            t = s.go(TT(xy, dn[:], p3[:, 2, :], ALU.add))
                            next(side, None)
                            s.need(t)
                            t = s.go(STT(out=dn[:], in0=xy, scalar=2.0, in1=tmp[i][:, 0, :], op0=ALU.mult, op1=ALU.add))
                            s.go(STT(out=nb[:, 0, :], in0=xy, scalar=2.0, in1=mm[i][:, 3, :], op0=ALU.mult, op1=ALU.add))
                            s.go(dve.tensor_copy(quad[:, 2, :], xy))
                            next(side, None)
                            s.need(t)
                            t = s.go(TS(dn[:], dn[:], 1.0, MOB_EPS, ALU.add, ALU.max))
                            next(side, None)
                            s.need(t)
                            t = s.go(dve.reciprocal(dn[:], dn[:]))
                            next(side, None)
                            s.need(t)
                            s.link(TT(ab[:], nb[:], each(dn[:], 2), ALU.mult))
                            dve.sem_inc(scale_in, 1)
                            A, B = each(ab[:, 0, :], 2), each(ab[:, 1, :], 2)
                            s.go(TT(bab[:], mix[i][:, 0:3:2, :], B, ALU.mult))
                            s.go(TT(w2[:], G2, A, ALU.mult))
                            t1 = s.go(TT(z4[:].rearrange("p (a b) k -> p a b k", a=2), quad[:].rearrange("p (a b) k -> p a b k", a=2),
                                         ab[:].unsqueeze(1).to_broadcast([P, 2, 2, G]), ALU.mult))
                            t2 = s.go(TT(g2[:, 1, :], mp, ab[:, 1, :], ALU.mult))
                            next(side, None)
                            s.need(t2)
                            s.go(dve.tensor_copy(g2[:, 0, :], bab[:, 1, :]))
                            t = s.go(TT(z2[:], z4[:, 0:4:2, :], z4[:, 1:4:2, :], ALU.add))
                            next(side, None)
                            s.need(t)
                            s.go(TT(G2, w2[:], g2[:], ALU.add))
                            t = s.go(TT(z2[:], z2[:], ab[:], ALU.mult))
                            next(side, None)
                            s.need(t)
                            t = s.go(TT(S2, z2[:, 0, :], z2[:, 1, :], ALU.add))
                            next(side, None)
                            dots(g, *after_next)
                            dve.wait_ge(scaled, u * RB + (q + 1))
                            for k in range(G):
                                t = s.go(STT(out=O[:, g * G + k, :], in0=R[:, k, 0:D], scalar=bab[:, 0, k:k + 1],
                                             in1=us[:, k, :], op0=ALU.mult, op1=ALU.add))
                                next(side, None)
                            s.need(t)
                            dve.sem_inc(rows_free[q], 1)
                            for _ in side:
                                pass

                        def reads(g, u):
                            c = cols(g)
                            dve.wait_ge(masked, u * G + G)
                            t = s.go(TS(off[:], at0[:, c], float(E - RB), None, ALU.min))
                            yield
                            s.need(t)
                            s.go(TS(offs[:], off[:], float(D), None, ALU.mult))
                            t = s.go(TT(eid[:], iota_w[:, 0:RB].unsqueeze(1).to_broadcast([P, G, RB]), wide(off[:], RB),
                                        ALU.add))
                            yield
                            s.need(t)
                            s.go(TT(val[:], eid[:], wide(at0[:, c], RB), ALU.is_ge))
                            t = s.go(TT(val2[:], eid[:], wide(end[:, c], RB), ALU.is_lt))
                            yield
                            s.need(t)
                            s.go(TS(at0[:, c], at0[:, c], float(RB), None, ALU.add))
                            t = s.go(TT(val[:], val[:], val2[:], ALU.mult))
                            yield
                            s.need(t)
                            dve.sem_inc(offsets, 1)

                        def both(a, b):
                            for _ in a:
                                next(b, None)
                                yield
                            for _ in b:
                                yield

                        ready, dotted = [0, 0], [0, 0]
                        for g in range(NGRP):
                            s.restart()
                            dots(g, ub[g], 0)
                            for _ in message(g, ub[g], 0):
                                pass
                            dots(g, ub[g], 1)
                            s.need(s.n)
                            with dve.Fori(ub[g], ub[g + 1]) as u:
                                s.restart()
                                ready[0] = dotted[1] = 0
                                add_message(g, u, 0, both(message(g, u, 1), reads(g, u)), (u, 2))
                                for q in range(1, RB - 1):
                                    add_message(g, u, q, message(g, u, q + 1), (u, q + 2) if q + 2 < RB else (u + 1, 0))
                                add_message(g, u, RB - 1, message(g, u + 1, 0), (u + 1, 1))
                                s.need(s.n)
                        s.restart()
                        s.link(dve.tensor_copy(gam[:].rearrange("p (g k) -> p g k", g=NGRP), gp[:, :, 0, :]))

            with ExitStack() as c2:
                junk = sb("junk", [P, NTILE, D], F32, c2)
                st = sb("st", [P, 4, G], F32, c2)
                sq = sb("sq", [P, G, D], F32, c2)
                names = "n2 xo nrm nc lp lm z th f ok y2 xy den c1 c2 t".split()
                v = {n: sb("w_" + n, [P, NTILE], F32, c2) for n in names}
                V = {n: v[n][:] for n in names}
                own, roots_in, roots_out, std_in, std_out = (
                    sem(n, c2) for n in ("own", "roots_in", "roots_out", "std_in", "std_out"))
                with nc.Block() as block:
                    @block.scalar
                    def _(act):
                        act.wait_ge(roots_in, 1)
                        act.activation(V["nrm"], V["n2"], ACT.Sqrt).then_inc(roots_out, 1)
                        act.wait_ge(roots_in, 2)
                        act.activation(V["lp"], V["lp"], ACT.Ln).then_inc(roots_out, 1)
                        act.activation(V["lm"], V["lm"], ACT.Ln).then_inc(roots_out, 1)
                        act.wait_ge(roots_in, 3)
                        act.activation(V["th"], V["z"], ACT.Tanh).then_inc(roots_out, 1)
                        for g in range(NGRP):
                            roots(act, st, std_in, std_out, g)

                    @block.vector
                    def _(dve):
                        s = Steps(dve, own)
                        TT, TS, STT = dve.tensor_tensor, dve.tensor_scalar, dve.scalar_tensor_tensor

                        def tt(o, a, b, op=ALU.mult):
                            s.link(TT(V[o], a, b, op))

                        for t in range(NTILE):
                            s.go(STT(out=O[:, t, :], in0=X[:, t, :], scalar=gam[:, t:t + 1], in1=O[:, t, :],
                                     op0=ALU.mult, op1=ALU.add))
                        s.need(s.n)
                        for t in range(NTILE):
                            s.go(dve.tensor_tensor_reduce(junk[:, t, :], O[:, t, :], O[:, t, :], 1.0, 0.0,
                                                          ALU.mult, ALU.add, v["n2"][:, t:t + 1]))
                        s.need(s.n)
                        dve.sem_inc(roots_in, 1)
                        for t in range(NTILE):
                            s.go(dve.tensor_tensor_reduce(junk[:, t, :], O[:, t, :], X[:, t, :], 1.0, 0.0,
                                                          ALU.mult, ALU.add, v["xo"][:, t:t + 1]))
                        s.need(s.n)
                        dve.wait_ge(roots_out, 1)
                        s.link(TS(V["nc"], V["nrm"], MOB_EPS, 1.0 - MOB_EPS, ALU.max, ALU.min))
                        s.link(TS(V["lp"], V["nc"], 1.0, 1.0, ALU.mult, ALU.add))
                        s.link(TS(V["lm"], V["nc"], -1.0, 1.0, ALU.mult, ALU.add))
                        dve.sem_inc(roots_in, 1)
                        dve.wait_ge(roots_out, 3)
                        tt("z", V["lp"], V["lm"], ALU.subtract)
                        tt("z", V["z"], rdeg[:])
                        s.link(TS(V["z"], V["z"], 0.5, None, ALU.mult))
                        dve.sem_inc(roots_in, 1)
                        s.link(dve.reciprocal(V["f"], V["nc"]))
                        s.link(TS(V["ok"], V["nrm"], MOB_EPS, None, ALU.is_gt))
                        dve.wait_ge(roots_out, 4)
                        tt("f", V["f"], V["th"])
                        tt("f", V["f"], V["ok"])
                        tt("xy", V["f"], V["xo"])
                        tt("t", V["f"], V["f"])
                        tt("y2", V["t"], V["n2"])
                        tt("t", d2[:], V["y2"])
                        s.link(TS(V["xy"], V["xy"], 2.0, 1.0, ALU.mult, ALU.add))
                        tt("den", V["xy"], V["t"], ALU.add)
                        s.link(TS(V["den"], V["den"], MOB_EPS, None, ALU.max))
                        s.link(dve.reciprocal(V["den"], V["den"]))
                        tt("c1", V["xy"], V["y2"], ALU.add)
                        tt("c1", V["c1"], V["den"])
                        s.link(TS(V["c1"], V["c1"], 1.0, None, ALU.add))
                        s.link(TS(V["c2"], d2[:], -1.0, 1.0, ALU.mult, ALU.add))
                        tt("c2", V["c2"], V["f"])
                        tt("c2", V["c2"], V["den"])
                        for t in range(NTILE):
                            s.go(TS(O[:, t, :], O[:, t, :], v["c2"][:, t:t + 1], None, ALU.mult))
                        s.need(s.n)
                        for t in range(NTILE):
                            s.go(STT(out=X[:, t, :], in0=X[:, t, :], scalar=v["c1"][:, t:t + 1], in1=O[:, t, :],
                                     op0=ALU.mult, op1=ALU.add))
                        s.need(s.n)
                        for g in range(NGRP):
                            normalise(s, dve, None, g, X, sq, st, std_in, std_out, g)

        l2 = ctx.enter_context(ExitStack())
        XA = l2.enter_context(nc.sbuf_tensor("XA", [P, NTILE, T * HK], F32))
        with ExitStack() as c1:
            xT = [sb(f"xT{i}", [P, D], F32, c1) for i in range(2)]
            stage = [sb(f"tstage{i}", [P, T, TW], F32, c1) for i in range(2)]
            turn_ps = psum("turn_ps", [P, 2, 512], c1)
            prod_ps = psum("prod_ps", [P, 2, 1024], c1)
            own, staged = sem("own", c1), sem("staged", c1)
            x_turned, x_kept, multiplied = (sem(n, c1) for n in ("x_turned", "x_kept", "multiplied"))
            stored = [sem(f"stored{i}", c1) for i in range(2)]
            with nc.Block() as block:
                @block.tensor
                def _(pe):
                    wj = Wj[:].rearrange("p t n -> p (t n)")
                    CUT = 3 * (D + HK)
                    for t in range(NTILE):
                        b = t % 2
                        if t == 0:
                            pe.transpose(turn_ps[:, 0, 0:D], X[:, 0, :], ident[:]).then_inc(x_turned, 1)
                        if t + 1 < NTILE:
                            pe.transpose(turn_ps[:, 1 - b, 0:D], X[:, t + 1, :], ident[:]).then_inc(x_turned, 1)
                        pe.wait_ge(x_kept, t + 1)
                        if t >= 2:
                            pe.wait_ge(staged, t - 1)
                        pe.matmul(prod_ps[:, b, 0:CUT], xT[b][:], wj[:, 0:CUT], start=True, stop=True)
                        pe.matmul(prod_ps[:, b, 512:512 + D + HK], xT[b][:], wj[:, CUT:], start=True, stop=True)
                        pe.matmul(prod_ps[:, b, 512 + D + HK:512 + D + HK + T * HK], xT[b][:], Wi[:],
                                  start=True, stop=True).then_inc(multiplied, 1)

                @block.scalar
                def _(act):
                    for t in range(NTILE):
                        act.wait_ge(x_turned, t + 1)
                        if t >= 2:
                            act.wait_ge(multiplied, t - 1)
                        act.activation(xT[t % 2][:], turn_ps[:, t % 2, 0:D], ACT.Copy).then_inc(x_kept, 1)

                @block.vector
                def _(dve):
                    s = Steps(dve, own)
                    for i in range(2):
                        s.go(dve.memset(stage[i][:], 0.0))
                    s.need(s.n)
                    for t in range(NTILE):
                        b = stage[t % 2]
                        dve.wait_ge(multiplied, t + 1)
                        if t >= 2:
                            dve.wait_ge(stored[t % 2], 16 * (t // 2))
                        s.go(dve.tensor_copy(b[:, 0:3, 0:D + HK],
                                             prod_ps[:, t % 2, 0:3 * (D + HK)].rearrange("p (t n) -> p t n", t=3)))
                        s.go(dve.tensor_copy(b[:, 3, 0:D + HK], prod_ps[:, t % 2, 512:512 + D + HK]))
                        s.go(dve.tensor_scalar(b[:, :, D + HK:TW], hot[:], real[:, t:t + 1], None, ALU.mult))
                        s.go(dve.tensor_copy(XA[:, t, :], prod_ps[:, t % 2, 512 + D + HK:512 + D + HK + T * HK]))
                        s.link(dve.tensor_tensor(RES[:, t, :], X[:, t, :], prod_ps[:, t % 2, 0:D], ALU.add))
                        dve.sem_inc(staged, 1)
                        s.link(dve.tensor_tensor(RES[:, t, :], RES[:, t, :], bias[:], ALU.add))

                @block.gpsimd
                def _(pool):
                    for t in range(NTILE):
                        pool.wait_ge(staged, t + 1)
                        pool.indirect_dma_start(t_tab, bass.IndirectOffsetOnAxis(ap=node[:, t, 2:3], axis=0),
                                                stage[t % 2][:].rearrange("p t n -> p (t n)"), None
                                                ).then_inc(stored[t % 2], 16)
                    pool.wait_ge(stored[0], 16 * ((NTILE + 1) // 2))
                    pool.wait_ge(stored[1], 16 * (NTILE // 2))

        MX = sb("MX", [P, NTILE, T, 2, H])
        t_rows = t_tab.rearrange("n (t w) -> (n t) w", t=T)
        NPAIR = RB // 2
        G2 = 2 * G
        SW = H + T
        kept_rows = dram("kept_rows", [CAP + 1, NPAIR, P, G2 * D])
        kept_scores = dram("kept_scores", [CAP + 1, NPAIR, P, G2 * SW])

        def scores(s, dve, R, g, prod, sc, al):
            xa = XA[:, cols(g), :].rearrange("p k (t n) -> p k t n", t=T)
            for j in range(2):
                t = s.go(dve.tensor_tensor(prod[:, j * G:(j + 1) * G, :, 0:HK], xa,
                                           R[:, j, :, D + HK:TW].unsqueeze(3).to_broadcast([P, G, T, HK]), ALU.mult))
                yield
            s.need(t)
            t = s.go(dve.tensor_reduce(sc[:], prod[:, :, :, 0:HK].rearrange("p k t n -> p k n t"), AX.X, ALU.add))
            yield
            s.need(t)
            t = s.go(dve.tensor_tensor(sc[:], sc[:], R.rearrange("p j k w -> p (j k) w")[:, :, D:D + HK], ALU.add))
            yield
            s.need(t)
            t = s.go(dve.scalar_tensor_tensor(out=sc[:], in0=sc[:], scalar=0.2, in1=sc[:], op0=ALU.mult, op1=ALU.max))
            yield
            s.need(t)
            t = s.go(dve.tensor_tensor(sc[:], sc[:], pk[:].unsqueeze(1).to_broadcast([P, G2, HK]), ALU.mult))
            yield
            s.need(t)
            t = s.go(dve.tensor_reduce(al[:], sc[:].rearrange("p k (h c) -> p k h c", h=H), AX.X, ALU.add))
            yield
            s.need(t)

        def pair_memory(c, width):
            pairs, slot, slots_in, rows_in, rows_free, marker = pass_memory(c, width, pairs=True)
            return pairs, [pairs[q // 2][:, q % 2] for q in range(RB)], slot, slots_in, rows_in, rows_free, marker

        with ExitStack() as c1:
            pairs, rows, slot, slots_in, rows_in, rows_free, marker = pair_memory(c1, TW)
            keep = [sb(f"keep{p}", [P, G2, D], F32, c1) for p in range(NPAIR)]
            small = [sb(f"small{p}", [P, G2, SW], F32, c1) for p in range(NPAIR)]
            prod = sb("prod", [P, G2, T, HK], F32, c1)
            sc = sb("sc", [P, G2, HK], F32, c1)
            al = [sb(f"alpha{p}", [P, G2, H], F32, c1) for p in range(NPAIR)]
            pen = [sb(f"pen{p}", [P, G2, T], F32, c1) for p in range(NPAIR)]
            cand = sb("cand", [P, 2, G, T, H], F32, c1)
            top = sb("top", [P, G, T, H], F32, c1)
            mnew = sb("mnew", [P, G, T, H], F32, c1)
            ex = sb("ex", [P, 3, G, T, H], F32, c1)
            MAX = sb("MAX", [P, NTILE, T, H], F32, c1)
            DEN = sb("DEN", [P, NTILE, T, H], F32, c1)
            own, exp_in, exp_out, blank, copied = (
                sem(n, c1) for n in ("own", "exp_in", "exp_out", "blank", "copied"))
            kept_out = [sem(f"kept_out{p}", c1) for p in range(NPAIR)]
            with nc.Block() as block:
                @block.sync
                def _(sp):
                    load_slots(sp, slot_typed, slot, slots_in, rows_in)

                @block.gpsimd
                def _(pool):
                    ub = unit_bounds(pool)
                    for g in range(NGRP):
                        with pool.Fori(ub[g], ub[g + 1]) as u:
                            gather_unit(pool, u, t_rows, slot, rows, slots_in, rows_in, rows_free, marker)

                @block.scalar
                def _(act):
                    ub = unit_bounds(act)

                    def store(at, p):
                        for table, mine in ((kept_rows, keep), (kept_scores, small)):
                            act.dma_start(table[at, p].rearrange("o p n -> (o p) n"),
                                          mine[p][:].rearrange("p k w -> p (k w)")).then_inc(kept_out[p], 16)

                    act.wait_ge(blank, 2 * NPAIR)
                    for p in range(NPAIR):
                        store(slice(CAP, CAP + 1), p)
                    for g in range(NGRP):
                        with act.Fori(ub[g], ub[g + 1]) as u:
                            at = nc.s_assert_within((u - CAP) * (u < CAP) + CAP, 0, CAP)
                            for p in range(NPAIR):
                                for q in (2 * p, 2 * p + 1):
                                    act.wait_ge(rows_in[q], (16 * G) * u + 16 * G)
                                act.wait_ge(kept_out[p], 32 * u + 32)
                                act.activation(keep[p][:], pairs[p][:].rearrange("p j k w -> p (j k) w")[:, :, 0:D],
                                               ACT.Copy).then_inc(copied, 1)
                                act.wait_ge(exp_in, u * NPAIR + (p + 1))
                                act.activation(ex[:], ex[:], ACT.Exp).then_inc(exp_out, 1)
                                act.wait_ge(copied, u * NPAIR + (p + 1))
                                store(bass.ds(at, 1), p)
                    units = ub[NGRP]
                    for p in range(NPAIR):
                        act.wait_ge(kept_out[p], 32 * units + 32)
                        act.sem_inc(marker, 1)

                @block.vector
                def _(dve):
                    ub = unit_bounds(dve)
                    s = Steps(dve, own)
                    TT = dve.tensor_tensor
                    for p in range(NPAIR):
                        dve.memset(keep[p][:], 0.0).then_inc(blank, 1)
                        dve.memset(small[p][:], 0.0).then_inc(blank, 1)
                    s.go(dve.memset(MAX[:], NEG))
                    s.go(dve.memset(DEN[:], 0.0))
                    s.need(s.n)
                    dve.wait_ge(blank, 2 * NPAIR)
                    for q in range(RB):
                        dve.sem_inc(rows_free[q], 1)

                    def score(g, u, p):
                        R = pairs[p][:]
                        oh = R.rearrange("p j k w -> p (j k) w")[:, :, D + HK:TW]
                        for q in (2 * p, 2 * p + 1):
                            dve.wait_ge(rows_in[q], (16 * G) * u + 16 * G)
                        dve.wait_ge(kept_out[p], 32 * u + 32)
                        s.go(dve.tensor_copy(small[p][:, :, H:SW], oh))
                        s.go(dve.tensor_scalar(pen[p][:], oh, -1.0, -NEG, ALU.add, ALU.mult))
                        yield
                        yield from scores(s, dve, R, g, prod, sc, al[p])
                        s.go(dve.tensor_copy(small[p][:, :, 0:H], al[p][:]))
                        dve.wait_ge(copied, u * NPAIR + (p + 1))
                        dve.sem_inc(rows_free[2 * p], 1)
                        dve.sem_inc(rows_free[2 * p + 1], 1)

                    def add_up(g, u, p, side):
                        oh = small[p][:, :, H:SW]
                        cd = cand[:].rearrange("p j k t h -> p (j k) t h")

                        def link(ins):
                            t = s.go(ins)
                            next(side, None)
                            s.need(t)

                        link(TT(cd, al[p][:].unsqueeze(2).to_broadcast([P, G2, T, H]),
                                oh.unsqueeze(3).to_broadcast([P, G2, T, H]), ALU.mult))
                        link(TT(cd, cd, pen[p][:].unsqueeze(3).to_broadcast([P, G2, T, H]), ALU.add))
                        M, S = MAX[:, cols(g)], DEN[:, cols(g)]
                        link(TT(top[:], cand[:, 0], cand[:, 1], ALU.max))
                        link(TT(mnew[:], M, top[:], ALU.max))
                        s.go(TT(ex[:, 0], cand[:, 0], mnew[:], ALU.subtract))
                        s.go(TT(ex[:, 1], cand[:, 1], mnew[:], ALU.subtract))
                        s.link(TT(ex[:, 2], M, mnew[:], ALU.subtract))
                        dve.sem_inc(exp_in, 1)
                        link(dve.tensor_copy(M, mnew[:]))
                        next(side, None)
                        dve.wait_ge(exp_out, u * NPAIR + (p + 1))
                        e01 = ex[:, 0:2].rearrange("p j k t h -> p (j k) t h")
                        s.go(TT(S, S, ex[:, 2], ALU.mult))
                        link(TT(e01, e01, oh.unsqueeze(3).to_broadcast([P, G2, T, H]), ALU.mult))
                        link(TT(ex[:, 0], ex[:, 0], ex[:, 1], ALU.add))
                        link(TT(S, S, ex[:, 0], ALU.add))
                        for _ in side:
                            pass

                    for g in range(NGRP):
                        with dve.Fori(ub[g], ub[g + 1]) as u:
                            s.restart()
                            for _ in score(g, u, 0):
                                pass
                            for p in range(NPAIR):
                                add_up(g, u, p, score(g, u, p + 1) if p + 1 < NPAIR else iter(()))
                    s.restart()
                    s.link(dve.tensor_copy(MX[:, :, :, 0, :], MAX[:]))
                    s.link(dve.tensor_scalar(MAX[:], DEN[:], 0.0, None, ALU.is_equal))
                    s.link(TT(DEN[:], DEN[:], MAX[:], ALU.add))
                    s.link(dve.reciprocal(DEN[:], DEN[:]))
                    s.link(TT(MX[:, :, :, 1, :], DEN[:],
                              imp[:].unsqueeze(1).unsqueeze(3).to_broadcast([P, NTILE, T, H]), ALU.mult))

        def weights(s, dve, oh, al, g, prod, sel, wgt, exp_in, exp_out, turn):
            mx = MX[:, cols(g)].rearrange("p k t a h -> p k t (a h)")
            for j in range(2):
                t = s.go(dve.tensor_tensor(prod[:, j * G:(j + 1) * G, :, 0:2 * H], mx,
                                           oh[:, j * G:(j + 1) * G].unsqueeze(3).to_broadcast([P, G, T, 2 * H]), ALU.mult))
            yield
            s.need(t)
            t = s.go(dve.tensor_reduce(sel[:], prod[:, :, :, 0:2 * H].rearrange("p k t n -> p k n t"), AX.X, ALU.add))
            yield
            s.need(t)
            t = s.go(dve.tensor_tensor(wgt[:], al, sel[:, :, 0:H], ALU.subtract))
            yield
            s.need(t)
            dve.sem_inc(exp_in, 1)
            yield
            dve.wait_ge(exp_out, turn)
            t = s.go(dve.tensor_tensor(wgt[:], wgt[:], sel[:, :, H:2 * H], ALU.mult))
            yield
            s.need(t)

        for again in (False, True):
            with ExitStack() as c1:
                if again:
                    pairs, rows, slot, slots_in, rows_in, rows_free, marker = pair_memory(c1, TW)
                    sc = sb("sc", [P, G2, HK], F32, c1)
                    al = sb("al", [P, G2, H], F32, c1)
                else:
                    pairs = [sb(f"kept{p}", [P, G2, D], F32, c1) for p in range(NPAIR)]
                    small = [sb(f"kept_small{p}", [P, G2, SW], F32, c1) for p in range(NPAIR)]
                    kept_in, small_in, kept_free, small_free = (
                        [sem(f"{name}{p}", c1) for p in range(NPAIR)]
                        for name in ("kept_in", "small_in", "kept_free", "small_free"))
                prod = [sb(f"wprod{i}", [P, G2, T, HK], F32, c1) for i in range(2)]
                sel = [sb(f"sel{i}", [P, G2, 2 * H], F32, c1) for i in range(2)]
                wgt = [sb(f"wgt{i}", [P, G2, H], F32, c1) for i in range(2)]
                wrow = [sb(f"wrow{i}", [P, G2, D], F32, c1) for i in range(2)]
                acc = psum("acc", [P, 2, 1024], c1)
                own, exp_in, exp_out, weighted, added, closed, summed = (
                    sem(n, c1) for n in ("own", "exp_in", "exp_out", "weighted", "added", "closed", "summed"))
                at0 = CB if again else BB
                hi = [max(n - CAP, 0) for n in unit_hi] if again else [min(n, CAP) for n in unit_hi]

                def part_bounds(eng):
                    return bounds(eng, at0, NGRP + 1, [0] * (NGRP + 1), hi)

                def each_unit(eng, body, after=None, before=None):
                    pb = part_bounds(eng)
                    for g in range(NGRP):
                        if before:
                            before(g)
                        with eng.If(pb[g] < pb[g + 1]):
                            with eng.Fori(pb[g], pb[g + 1]) as u:
                                body(g, u)
                        if after:
                            after(g, pb[g + 1])

                with nc.Block() as block:
                    @block.sync
                    def _(sp):
                        if again:
                            last = part_bounds(sp)[NGRP]
                            with sp.If(0 < last):
                                load_slots(sp, slot_typed, slot, slots_in, rows_in, last, CAP)
                        else:
                            def body(g, u):
                                for free, mine, table, there in ((small_free, small, kept_scores, small_in),
                                                                 (kept_free, pairs, kept_rows, kept_in)):
                                    for p in range(NPAIR):
                                        sp.wait_ge(free[p], u + 1)
                                        sp.dma_start(mine[p][:].rearrange("p k w -> p (k w)"),
                                                     table[bass.ds(u, 1), p].rearrange("o p n -> (o p) n")
                                                     ).then_inc(there[p], 16)

                            each_unit(sp, body)

                    if again:
                        @block.gpsimd
                        def _(pool):
                            each_unit(pool, lambda g, u: gather_unit(pool, u, t_rows, slot, rows, slots_in, rows_in,
                                                                     rows_free, marker))

                    @block.scalar
                    def _(act):
                        def body(g, u):
                            for p in range(NPAIR):
                                act.wait_ge(exp_in, u * NPAIR + (p + 1))
                                act.activation(wgt[p][:], wgt[p][:], ACT.Exp).then_inc(exp_out, 1)

                        each_unit(act, body)

                    @block.tensor
                    def _(pe):
                        def clear(g):
                            if g >= 2:
                                pe.wait_ge(summed, g - 1)
                            clear_sums(pe, acc[:, g % 2, :])

                        def body(g, u):
                            for p in range(NPAIR):
                                pe.wait_ge(weighted, u * NPAIR + (p + 1))
                                add_rows(pe, acc[:, g % 2, :], wrow[p][:, 0:G])
                                add_rows(pe, acc[:, g % 2, :], wrow[p][:, G:G2]).then_inc(added, 1)

                        each_unit(pe, body, before=clear, after=lambda g, n: pe.matmul(
                            acc[:, g % 2, 5 * P:6 * P], ident[:], zeros[:, 0:P], start=True, stop=True,
                            skip_group_check=True).then_inc(closed, 1))

                    @block.vector
                    def _(dve):
                        s = Steps(dve, own)
                        TT = dve.tensor_tensor
                        if again:
                            for q in range(RB):
                                dve.sem_inc(rows_free[q], 1)
                        else:
                            for p in range(NPAIR):
                                dve.sem_inc(small_free[p], 1)
                                dve.sem_inc(kept_free[p], 1)
                        dve.sem_inc(added, NPAIR)

                        def pair(g, u, p):
                            if again:
                                for q in (2 * p, 2 * p + 1):
                                    dve.wait_ge(rows_in[q], (16 * G) * u + 16 * G)
                                for _ in scores(s, dve, pairs[p][:], g, prod[p], sc, al):
                                    pass
                                R = pairs[p][:].rearrange("p j k w -> p (j k) w")
                                oh, score = R[:, :, D + HK:TW], al[:]
                            else:
                                dve.wait_ge(small_in[p], 16 * u + 16)
                                R = pairs[p][:]
                                oh, score = small[p][:, :, H:SW], small[p][:, :, 0:H]
                            yield from weights(s, dve, oh, score, g, prod[p], sel[p], wgt[p], exp_in, exp_out,
                                               u * NPAIR + (p + 1))
                            if not again:
                                dve.sem_inc(small_free[p], 1)
                                dve.wait_ge(kept_in[p], 16 * u + 16)
                            dve.wait_ge(added, u * NPAIR + (p + 1))
                            s.link(TT(wrow[p][:].rearrange("p k (h c) -> p k h c", h=H),
                                      R[:, :, 0:D].rearrange("p k (h c) -> p k h c", h=H),
                                      wgt[p][:].unsqueeze(3).to_broadcast([P, G2, H, C]), ALU.mult))
                            dve.sem_inc(weighted, 1)
                            if again:
                                dve.sem_inc(rows_free[2 * p], 1)
                                dve.sem_inc(rows_free[2 * p + 1], 1)
                            else:
                                dve.sem_inc(kept_free[p], 1)

                        def body(g, u):
                            s.restart()
                            chains = [pair(g, u, p) for p in range(NPAIR)]
                            if again:
                                for chain in chains:
                                    for _ in chain:
                                        pass
                            else:
                                for _ in zip_longest(*chains):
                                    pass

                        def take(g, n):
                            s.restart()
                            dve.wait_ge(closed, g + 1)
                            dve.wait_ge(added, n * NPAIR + NPAIR)
                            s.link(TT(RES[:, cols(g), :], RES[:, cols(g), :],
                                      acc[:, g % 2, 0:5 * P].rearrange("p (k d) -> p k d", k=G), ALU.add))
                            dve.sem_inc(summed, 1)

                        each_unit(dve, body, after=take)

        with ExitStack() as c1:
            sq = sb("sq", [P, G, D], F32, c1)
            st = sb("st", [P, 4, G], F32, c1)
            own, std_in, std_out = (sem(n, c1) for n in ("own", "std_in", "std_out"))
            with nc.Block() as block:
                @block.scalar
                def _(act):
                    for g in range(NGRP):
                        roots(act, st, std_in, std_out, g)

                @block.vector
                def _(dve):
                    s = Steps(dve, own)
                    for g in range(NGRP):
                        normalise(s, dve, None, g, RES, sq, st, std_in, std_out, g)
                        s.link(dve.tensor_copy(X[:, cols(g), :], RES[:, cols(g), :]))

        with ExitStack() as c1:
            Wa = sb("Wa", [P, 2, D], F32, c1)
            Wb = sb("Wb", [P, D], F32, c1)
            b1 = sb("b1", [P, 1], F32, c1)
            b2 = sb("b2", [P, D], F32, c1)
            inT = [sb(f"inT{i}", [P, 2 * D], F32, c1) for i in range(2)]
            hT = [sb(f"hT{i}", [P, D], F32, c1) for i in range(2)]
            sq = sb("sq", [P, G, D], F32, c1)
            st = sb("st", [P, 4, G], F32, c1)
            in_ps = psum("in_ps", [P, 2, 512], c1)
            h_ps = psum("h_ps", [P, 2, 512], c1)
            y_ps = psum("y_ps", [P, 2, 512], c1)
            signals = [sem(n, c1) for n in ("loaded", "own", "turned", "kept", "hidden", "active", "outed", "taken",
                                            "std_in", "std_out", "normed")]
            loaded, own, turned, kept, hidden, active, outed, taken, std_in, std_out, normed = signals
            with nc.Block() as block:
                @block.sync
                def _(sp):
                    for one in signals:
                        sp.sem_clear(one)
            with nc.Block() as block:
                @block.sync
                def _(sp):
                    sp.dma_start(Wa[:], W1m.rearrange("(a i) o -> i a o", a=2)).then_inc(loaded, 16)
                    sp.dma_start(Wb[:], W2m).then_inc(loaded, 16)
                    sp.dma_start(b1[:], b1m.rearrange("(d o) -> d o", o=1)).then_inc(loaded, 16)
                    sp.dma_start(b2[:], b2m.rearrange("(o d) -> o d", o=1).to_broadcast([P, D])).then_inc(loaded, 16)

                @block.tensor
                def _(pe):
                    def turn(t):
                        pe.transpose(in_ps[:, t % 2, 0:D], X[:, t, :], ident[:])
                        pe.transpose(in_ps[:, t % 2, D:2 * D], ATT[:, t, :], ident[:]).then_inc(turned, 1)

                    def first(t):
                        pe.wait_ge(kept, t + 1)
                        pe.matmul(h_ps[:, t % 2, 0:D], Wa[:, 0, :], inT[t % 2][:, 0:D], start=True, stop=False)
                        pe.matmul(h_ps[:, t % 2, 0:D], Wa[:, 1, :], inT[t % 2][:, D:2 * D], start=False,
                                  stop=True).then_inc(hidden, 1)

                    def second(t):
                        pe.wait_ge(active, t + 1)
                        if t >= 2:
                            pe.wait_ge(taken, t - 1)
                        pe.matmul(y_ps[:, t % 2, 0:D], hT[t % 2][:], Wb[:], start=True, stop=True).then_inc(outed, 1)

                    pe.wait_ge(loaded, 64)
                    turn(0)
                    for t in range(NTILE):
                        if t + 1 < NTILE:
                            turn(t + 1)
                        first(t)
                        if t:
                            second(t - 1)
                    second(NTILE - 1)

                @block.scalar
                def _(act):
                    def keep_turned(t):
                        act.wait_ge(turned, t + 1)
                        act.activation(inT[t % 2][:], in_ps[:, t % 2, 0:2 * D], ACT.Copy).then_inc(kept, 1)

                    act.wait_ge(loaded, 64)
                    keep_turned(0)
                    for t in range(NTILE):
                        if t + 1 < NTILE:
                            keep_turned(t + 1)
                        act.wait_ge(hidden, t + 1)
                        act.activation(hT[t % 2][:], h_ps[:, t % 2, 0:D], ACT.Relu, bias=b1[:, 0:1]).then_inc(active, 1)
                        if t >= G and t % G == 0:
                            roots(act, st, std_in, std_out, t // G - 1)
                    roots(act, st, std_in, std_out, NGRP - 1)

                @block.vector
                def _(dve):
                    s = Steps(dve, own)
                    dve.wait_ge(loaded, 64)
                    for g in range(NGRP):
                        for t in range(g * G, g * G + G):
                            s.link(dve.tensor_tensor(RES[:, t, :], X[:, t, :], b2[:], ALU.add))
                            dve.wait_ge(outed, t + 1)
                            s.link(dve.tensor_tensor(RES[:, t, :], RES[:, t, :], y_ps[:, t % 2, 0:D], ALU.add))
                            dve.sem_inc(taken, 1)
                        normalise(s, dve, None, g, RES, sq, st, std_in, std_out, g)
                        dve.sem_inc(normed, 1)

                @block.gpsimd
                def _(pool):
                    for g in range(NGRP):
                        pool.wait_ge(normed, g + 1)
                        for k in range(G):
                            t = g * G + k
                            pool.indirect_dma_start(out, bass.IndirectOffsetOnAxis(ap=node[:, t, 2:3], axis=0),
                                                    RES[:, t, :], None, bounds_check=N - 1, oob_is_err=False
                                                    ).then_inc(out_stored, 16)
                    pool.wait_ge(out_stored, 16 * NTILE)


_INS = ['x', 'src', 'dst', 'edge_attr_128', 'edge_type_4', 'L2_gnn_W', 'L2_gnn_att_vectors',
        'L2_gnn_confounder_probs', 'L2_gnn_edge_importance', 'L2_gnn_bias', 'L3_gnn_W1', 'L3_gnn_b1',
        'L3_gnn_W2', 'L3_gnn_b2']
_OUTS = [((3125, 128), 'float32')]


def kernel(**inputs):
    import numpy as _np
    import concourse.bacc as _bacc
    from concourse import mybir as _mybir
    from concourse.bass_utils import run_bass_kernel_spmd as _run

    nc = _bacc.Bacc("TRN2", target_bir_lowering=False, num_devices=1)
    arrays, args = {}, []
    for name in _INS:
        a = _np.ascontiguousarray(inputs[name])
        arrays[f"in_{name}_dram"] = a
        args.append(nc.dram_tensor(f"in_{name}_dram", a.shape, _mybir.dt.from_np(a.dtype), kind="ExternalInput").ap())
    for i, (shape, dtype) in enumerate(_OUTS):
        dt = _mybir.dt.from_np(_np.dtype(dtype))
        args.append(nc.dram_tensor(f"out_{i}_dram", shape, dt, kind="ExternalOutput").ap())
    build_program(nc, *args)
    r = _run(nc, [arrays], core_ids=[0])
    got = tuple(r.results[0][f"out_{i}_dram"] for i in range(len(_OUTS)))
    return got[0]
```

```python
from contextlib import ExitStack
from itertools import zip_longest

import concourse.bass as bass
from concourse import mybir

F32 = mybir.dt.float32
BF16 = mybir.dt.bfloat16
I32 = mybir.dt.int32
ALU = mybir.AluOpType
ACT = mybir.ActivationFunctionType
AX = mybir.AxisListType

P = 128
LN_EPS = 1e-5
MOB_EPS = 1e-7
NEG = -1e30

G = 5
RB = 4
SLOTS = RB * G
W = 32
UPW = W // RB
CAP = 64
HIST_COLS = 25


class Steps:

    def __init__(self, eng, sem):
        self.eng, self.sem, self.n, self.seen = eng, sem, 0, 0

    def restart(self):
        self.eng.sem_clear(self.sem)
        self.n = self.seen = 0

    def go(self, ins):
        self.n += 1
        ins.then_inc(self.sem, 1)
        return self.n

    def link(self, ins):
        self.need(self.go(ins))

    def need(self, n):
        if n > self.seen:
            self.eng.wait_ge(self.sem, n)
            self.seen = n


def build_program(nc, x, src, dst, edge_attr, edge_type, W2n, att, conf, importance, bias2,
                  W1m, b1m, W2m, b2m, out):
    N, D = x.shape
    E = src.shape[0]
    NTILE = -(-N // P)
    NP = NTILE * P
    NGRP = NTILE // G
    T, H, K = W2n.shape[0], att.shape[1], att.shape[0]
    C = D // H
    HK = H * K
    LD = E // 125
    assert T & (T - 1) == 0 and NTILE % G == 0 and E % 125 == 0 and D == P and NP > N and LD % HIST_COLS == 0
    NCHUNK = LD // HIST_COLS
    deg_max = [E] + [E // (g * G * P) for g in range(1, NGRP)]
    NU = sum(-(-d // RB) + 1 for d in deg_max)
    NWIN = [-(-d // W) + 1 for d in deg_max]
    MW = D + 4
    TW = D + HK + T

    def dram(name, shape, dt=F32):
        return nc.dram_tensor(name, shape, dt, kind="Internal").ap()

    node_tab = dram("node_tab", [NP, 4], I32)
    h_tab = [dram(f"h_tab{i}", [NP, D]) for i in range(3)]
    m_tab = dram("m_tab", [NP, MW])
    t_tab = dram("t_tab", [NP, T * TW])
    edge_pad = dram("edge_pad", [E + W], I32)
    unit_hi = [sum(-(-d // RB) + 1 for d in deg_max[:g]) for g in range(NGRP + 1)]
    NLIST = max(unit_hi[g] + NWIN[g] * UPW for g in range(NGRP)) + 1
    slot_node = dram("slot_node", [NLIST, P, SLOTS], I32)
    slot_typed = dram("slot_typed", [NLIST, P, SLOTS], I32)

    def flat(ap):
        names = "abcd"[:len(ap.shape)]
        ap = ap.rearrange(" ".join(names) + " -> (" + " ".join(names) + ")") if len(ap.shape) > 1 else ap
        return ap.rearrange("(n o) -> n o", o=1)

    ctx = ExitStack()
    with ctx:
        made = {}

        def unique(name):
            made[name] = made.get(name, 0) + 1
            return name if made[name] == 1 else f"{name}_{made[name]}"

        def sb(name, shape, dt=F32, c=ctx):
            return c.enter_context(nc.sbuf_tensor(unique(name), shape, dt))

        def psum(name, shape, c):
            return c.enter_context(nc.psum_tensor(unique(name), shape, F32))

        def sem(name, c):
            return c.enter_context(nc.semaphore(unique(name)))

        X = sb("X", [P, NTILE, D])
        RES = sb("RES", [P, NTILE, D])
        O = sb("O", [P, NTILE, D])
        ATT = sb("ATT", [P, NTILE, D])
        node = sb("node", [P, NTILE, 4], I32)
        nodef = sb("nodef", [P, NTILE, 4])
        rdeg = sb("rdeg", [P, NTILE])
        real = sb("real", [P, NTILE])
        ctl = sb("ctl", [1, 64], I32)
        ident = sb("ident", [P, P])
        zeros = sb("zeros", [P, 4 * P])
        iota_w = sb("iota_w", [P, W])
        d2 = sb("d2", [P, NTILE])
        UB, WB, FB, LONE, BB, CB = 0, 8, 16, 22, 24, 32

        def bounds(eng, at, n, lo, hi):
            return [eng.value_load(ctl[0:1, at + i:at + i + 1], min_val=lo[i], max_val=hi[i]) for i in range(n)]

        def unit_bounds(eng):
            return bounds(eng, UB, NGRP + 1, list(range(NGRP + 1)), unit_hi)

        with ExitStack() as c0:
            cnt = sb("cnt", [P, NTILE], F32, c0)
            low = sb("low", [P, P], F32, c0)
            high = sb("high", [P, P], F32, c0)
            ones = sb("ones", [P, P], F32, c0)
            nodeid = sb("nodeid", [P, NTILE], I32, c0)
            dsts = sb("dsts", [125, LD], I32, c0)
            dlo = sb("dlo", [125, LD], I32, c0)
            dhi = sb("dhi", [125, LD], I32, c0)
            dlof = sb("dlof", [125, LD], BF16, c0)
            dhif = sb("dhif", [125, LD], BF16, c0)
            iol = sb("iol", [P, P], BF16, c0)
            zi = sb("zi", [1, W], I32, c0)
            with ExitStack() as c1, nc.Block() as block:
                srcs = sb("srcs", [125, LD], I32, c1)
                types = sb("types", [125, LD], I32, c1)
                masked, filled, loaded, ends_in, joined, copied, split, cleared = (
                    sem(n, c1) for n in ("masked", "filled", "loaded", "ends_in", "joined", "copied", "split", "cleared"))

                @block.gpsimd
                def _(pool):
                    pool.memset(ident[:], 0.0).then_inc(filled, 1)
                    pool.memset(low[:], 1.0).then_inc(filled, 1)
                    pool.memset(high[:], 1.0).then_inc(filled, 1)
                    pool.wait_ge(filled, 3)
                    pool.affine_select(out=ident[:], in_=ident[:], compare_op=ALU.not_equal, fill=1.0, base=0,
                                       pattern=[[-1, P]], channel_multiplier=1).then_inc(masked, 1)
                    pool.affine_select(out=low[:], in_=low[:], compare_op=ALU.is_gt, fill=0.0, base=0,
                                       pattern=[[-1, P]], channel_multiplier=1).then_inc(masked, 1)
                    pool.affine_select(out=high[:], in_=high[:], compare_op=ALU.is_gt, fill=0.0, base=0,
                                       pattern=[[1, P]], channel_multiplier=-1).then_inc(masked, 1)
                    pool.iota(nodeid[:], pattern=[[P, NTILE]], base=0, channel_multiplier=1).then_inc(masked, 1)
                    pool.iota(iota_w[:], pattern=[[1, W]], base=0, channel_multiplier=0,
                              allow_small_or_imprecise_dtypes=True).then_inc(masked, 1)
                    pool.iota(iol[:], pattern=[[1, P]], base=0, channel_multiplier=0,
                              allow_small_or_imprecise_dtypes=True).then_inc(masked, 1)

                @block.sync
                def _(sp):
                    sp.dma_start(dsts[:], dst.rearrange("(p n) -> p n", p=125)).then_inc(loaded, 16)
                    sp.dma_start(srcs[:], src.rearrange("(p n) -> p n", p=125)).then_inc(ends_in, 16)
                    sp.dma_start(types[:], edge_type.rearrange("(p n) -> p n", p=125)).then_inc(ends_in, 16)
                    sp.dma_start(h_tab[0][0:N, :], x).then_inc(copied, 16)
                    sp.wait_ge(cleared, 2)
                    sp.dma_start(edge_pad[E:E + W].rearrange("(o n) -> o n", o=1), zi[:]).then_inc(copied, 16)
                    sp.dma_start(h_tab[0][N:NP, :], zeros[0:NP - N, 0:D]).then_inc(copied, 16)
                    sp.wait_ge(joined, 1)
                    sp.dma_start(edge_pad[0:E].rearrange("(p n) -> p n", p=125), types[:]).then_inc(copied, 16)
                    sp.wait_ge(copied, 64)

                @block.vector
                def _(dve):
                    dve.memset(zeros[:], 0.0).then_inc(cleared, 1)
                    dve.memset(zi[:], 0).then_inc(cleared, 1)
                    dve.memset(ones[:], 1.0).then_inc(split, 1)
                    dve.wait_ge(loaded, 16)
                    dve.tensor_scalar(dlo[:], dsts[:], P - 1, None, ALU.bitwise_and).then_inc(split, 1)
                    dve.tensor_scalar(dhi[:], dsts[:], 7, None, ALU.arith_shift_right).then_inc(split, 1)
                    dve.wait_ge(split, 3)
                    dve.tensor_copy(dlof[:], dlo[:]).then_inc(split, 1)
                    dve.tensor_copy(dhif[:], dhi[:]).then_inc(split, 1)
                    dve.wait_ge(ends_in, 32)
                    dve.scalar_tensor_tensor(out=types[:], in0=srcs[:], scalar=float(T), in1=types[:],
                                             op0=ALU.mult, op1=ALU.add).then_inc(joined, 1)

            with ExitStack() as c1:
                hlo = [sb(f"hlo{i}", [125, HIST_COLS, P], BF16, c1) for i in range(2)]
                hhi = [sb(f"hhi{i}", [125, HIST_COLS, NTILE], BF16, c1) for i in range(2)]
                zb = sb("zb", [P, P], BF16, c1)
                count_ps = psum("count_ps", [P, 512], c1)
                zeroed = sem("zeroed", c1)
                hot = [sem(f"hot{i}", c1) for i in range(2)]
                hot_used = [sem(f"hot_used{i}", c1) for i in range(2)]
                counted, degrees = sem("counted", c1), sem("degrees", c1)
                PAIRS = NCHUNK // 2

                def at(i, b):
                    return bass.ds(i * (2 * HIST_COLS) + b * HIST_COLS, HIST_COLS)

                def last_chunk():
                    return bass.ds(2 * PAIRS * HIST_COLS, HIST_COLS)

                with nc.Block() as block:
                    @block.vector
                    def _(dve):
                        def one_hots(b, cols):
                            dve.tensor_tensor(
                                hlo[b][:], iol[0:125, :].unsqueeze(1).to_broadcast([125, HIST_COLS, P]),
                                dlof[:, cols].unsqueeze(2).to_broadcast([125, HIST_COLS, P]), ALU.is_equal,
                            ).then_inc(hot[b], 1)
                            dve.tensor_tensor(
                                hhi[b][:], iol[0:125, 0:NTILE].unsqueeze(1).to_broadcast([125, HIST_COLS, NTILE]),
                                dhif[:, cols].unsqueeze(2).to_broadcast([125, HIST_COLS, NTILE]), ALU.is_equal,
                            ).then_inc(hot[b], 1)

                        dve.memset(zb[:], 0.0).then_inc(zeroed, 1)
                        with dve.Fori(0, PAIRS) as i:
                            for b in range(2):
                                dve.wait_ge(hot_used[b], i + 1)
                                one_hots(b, at(i, b))
                        dve.wait_ge(hot_used[0], PAIRS + 1)
                        one_hots(0, last_chunk())
                        dve.wait_ge(counted, 1)
                        dve.tensor_copy(cnt[:], count_ps[:, 0:NTILE]).then_inc(degrees, 1)

                    @block.tensor
                    def _(pe):
                        def products(b):
                            for j in range(HIST_COLS):
                                mm = pe.matmul(count_ps[:, 0:NTILE], hlo[b][:, j, :], hhi[b][:, j, :],
                                               start=False, stop=False, skip_group_check=True)
                            return mm

                        for b in range(2):
                            pe.sem_inc(hot_used[b], 1)
                        pe.wait_ge(zeroed, 1)
                        pe.matmul(count_ps[:, :], zb[:], zeros[:].bitcast(BF16)[:, 0:512], start=True, stop=False,
                                  skip_group_check=True)
                        with pe.Fori(0, PAIRS) as i:
                            for b in range(2):
                                pe.wait_ge(hot[b], 2 * i + 2)
                                products(b).then_inc(hot_used[b], 1)
                        pe.wait_ge(hot[0], 2 * PAIRS + 2)
                        products(0).then_inc(counted, 1)

            with ExitStack() as c1:
                diag = sb("diag", [P, NTILE, P], F32, c1)
                drow = sb("drow", [P, NP], F32, c1)
                junk = sb("junk", [P, NP], F32, c1)
                signs = sb("signs", [P, 2, NP], BF16, c1)
                below = sb("below", [P, NTILE], F32, c1)
                later = sb("later", [P, NTILE], F32, c1)
                tots = sb("tots", [P, NTILE], F32, c1)
                incl = sb("incl", [P, NTILE], F32, c1)
                onesc = sb("onesc", [P, NTILE], F32, c1)
                firstf = sb("firstf", [P, NTILE], F32, c1)
                part = sb("part", [P, 4, NTILE], F32, c1)
                posf = sb("posf", [P, NTILE], F32, c1)
                pos = sb("pos", [P, NTILE], I32, c1)
                rec = sb("rec", [P, NTILE, 4], I32, c1)
                cf = sb("cf", [1, 64], F32, c1)
                ci = sb("ci", [1, 64], I32, c1)
                row_ps = psum("row_ps", [P, 7 * 512], c1)
                pre_ps = psum("pre_ps", [P, 512], c1)
                diag_made, row_made, row_kept, prefixed, below_made, compared, ordered, placed, read_back, own = (
                    sem(n, c1) for n in ("diag_made", "row_made", "row_kept", "prefixed", "below_made", "compared",
                                         "ordered", "placed", "read_back", "own"))
                with nc.Block() as block:
                    @block.tensor
                    def _(pe):
                        pe.matmul(pre_ps[:, 0:NTILE], high[:], cnt[:], start=True, stop=True)
                        pe.matmul(pre_ps[:, 32:32 + NTILE], ones[:], cnt[:], start=True, stop=True).then_inc(prefixed, 1)
                        pe.wait_ge(diag_made, 1)
                        df = diag[:].rearrange("p t j -> p (t j)")
                        for b in range(-(-NP // 512)):
                            e = min(NP, 512 * b + 512)
                            mm = pe.matmul(row_ps[:, 512 * b:e], ones[:], df[:, 512 * b:e], start=True, stop=True)
                            mm.then_inc(row_made, 1)

                    @block.scalar
                    def _(act):
                        for b in range(-(-NP // 512)):
                            e = min(NP, 512 * b + 512)
                            act.wait_ge(row_made, b + 1)
                            act.activation(drow[:, 512 * b:e], row_ps[:, 512 * b:e], ACT.Copy).then_inc(row_kept, 1)
                        act.wait_ge(row_kept, -(-NP // 512))
                        act.wait_ge(below_made, 1)
                        for t in range(NTILE - 1):
                            if t >= 2:
                                act.wait_ge(compared, t - 1)
                            act.activation(signs[:, t % 2, (t + 1) * P:], drow[:, (t + 1) * P:], ACT.Sign, bias=below[:, t:t + 1],
                                           accum_out=part[:, 1, t:t + 1]).then_inc(compared, 1)

                    @block.vector
                    def _(dve):
                        s = Steps(dve, own)
                        dve.tensor_tensor(diag[:], ident[:].unsqueeze(1).to_broadcast([P, NTILE, P]),
                                          cnt[:].unsqueeze(2).to_broadcast([P, NTILE, P]), ALU.mult).then_inc(diag_made, 1)
                        s.link(dve.memset(onesc[:], 1.0))
                        s.link(dve.memset(part[:], 0.0))
                        s.link(dve.tensor_scalar(below[:], cnt[:], -1.0, -0.5, ALU.mult, ALU.add))
                        dve.sem_inc(below_made, 1)
                        for t in range(NTILE):
                            s.go(dve.memset(later[:, t:t + 1], float((NTILE - 1 - t) * P)))
                        s.need(s.n)
                        dve.wait_ge(prefixed, 1)
                        s.link(dve.tensor_copy(tots[:], pre_ps[:, 32:32 + NTILE]))
                        s.link(dve.tensor_tensor_scan(incl[:], onesc[:], tots[:], 0.0, ALU.mult, ALU.add))
                        s.link(dve.tensor_tensor(incl[:], incl[:], tots[:], ALU.subtract))
                        s.link(dve.tensor_tensor(firstf[:], incl[:], pre_ps[:, 0:NTILE], ALU.add))
                        dve.wait_ge(row_kept, -(-NP // 512))
                        for t in range(NTILE):
                            mine = drow[:, t * P:(t + 1) * P]
                            deg = cnt[:, t:t + 1]
                            if t:
                                s.go(dve.tensor_scalar(junk[:, 0:t * P], drow[:, 0:t * P], deg, 0.0, ALU.is_ge, ALU.add,
                                                       accum_out=part[:, 0, t:t + 1]))
                            s.go(dve.scalar_tensor_tensor(out=diag[:, 0, :], in0=mine, scalar=deg, in1=low[:],
                                                          op0=ALU.is_ge, op1=ALU.mult, accum_out=part[:, 2, t:t + 1]))
                            s.link(dve.scalar_tensor_tensor(out=diag[:, 1, :], in0=mine, scalar=deg, in1=high[:],
                                                            op0=ALU.is_gt, op1=ALU.mult, accum_out=part[:, 3, t:t + 1]))
                        dve.wait_ge(compared, NTILE - 1)
                        s.link(dve.tensor_tensor(part[:, 1, :], part[:, 1, :], later[:], ALU.add))
                        s.link(dve.tensor_scalar(part[:, 1, :], part[:, 1, :], 0.5, None, ALU.mult))
                        s.link(dve.tensor_reduce(posf[:], part[:].rearrange("p a t -> p t a"), AX.X, ALU.add))
                        s.go(dve.tensor_copy(pos[:], posf[:]))
                        s.go(dve.memset(rec[:], 0))
                        s.need(s.n)
                        s.go(dve.tensor_copy(rec[:, :, 0], firstf[:]))
                        s.go(dve.tensor_copy(rec[:, :, 1], cnt[:]))
                        s.go(dve.tensor_copy(rec[:, :, 2], nodeid[:]))
                        s.need(s.n)
                        dve.sem_inc(ordered, 1)
                        dve.wait_ge(read_back, 16)
                        s.link(dve.tensor_copy(nodef[:], node[:]))
                        s.link(dve.tensor_scalar(rdeg[:], nodef[:, :, 1], 1.0, None, ALU.max))
                        s.link(dve.reciprocal(rdeg[:], rdeg[:]))
                        s.link(dve.tensor_scalar(real[:], nodef[:, :, 2], float(N), None, ALU.is_lt))
                        high_of = node[0:1, 0:NTILE:G, 1]
                        highest = ci[:, 8:8 + NGRP]
                        s.link(dve.tensor_scalar(highest, high_of, RB - 1, None, ALU.add))
                        s.link(dve.tensor_scalar(highest, highest, RB.bit_length() - 1, None, ALU.arith_shift_right))
                        s.link(dve.tensor_scalar(highest, highest, 1, None, ALU.max))
                        whole, lone = ci[:, 16:17], ci[:, 17:18]
                        s.link(dve.tensor_scalar(whole, node[0:1, 1:2, 1], RB - 1, None, ALU.add))
                        s.link(dve.tensor_scalar(whole, whole, RB.bit_length() - 1, None, ALU.arith_shift_right))
                        s.link(dve.tensor_scalar(whole, whole, 1, None, ALU.max))
                        s.link(dve.tensor_tensor(lone, ci[:, 8:9], whole, ALU.subtract))
                        s.link(dve.tensor_scalar(lone, lone, 1, None, ALU.max))
                        s.link(dve.tensor_tensor(ci[:, 8:9], whole, lone, ALU.add))
                        s.link(dve.memset(ctl[:], 0))
                        s.link(dve.tensor_copy(ctl[:, LONE:LONE + 1], lone))
                        s.link(dve.tensor_scalar(ctl[:, WB:WB + NGRP], highest, UPW - 1, None, ALU.add))
                        s.link(dve.tensor_scalar(ctl[:, WB:WB + NGRP], ctl[:, WB:WB + NGRP], UPW.bit_length() - 1, None,
                                                 ALU.arith_shift_right))
                        s.link(dve.tensor_copy(cf[:, 0:NGRP], highest))
                        s.link(dve.tensor_tensor_scan(cf[:, 32:32 + NGRP], onesc[0:1, 0:NGRP], cf[:, 0:NGRP], 0.0,
                                                      ALU.mult, ALU.add))
                        s.link(dve.tensor_copy(ctl[:, UB + 1:UB + 1 + NGRP], cf[:, 32:32 + NGRP]))
                        s.link(dve.tensor_tensor(ctl[:, FB + 1:FB + 1 + NGRP], ctl[:, UB + 1:UB + 1 + NGRP],
                                                 lone.to_broadcast([1, NGRP]), ALU.subtract))
                        s.link(dve.tensor_scalar(ctl[:, BB + 1:BB + 2], whole, CAP, None, ALU.min))
                        s.link(dve.tensor_scalar(ctl[:, BB + 2:BB + 2 + NGRP], ctl[:, UB + 1:UB + 1 + NGRP], CAP, None, ALU.min))
                        s.link(dve.tensor_scalar(ctl[:, CB:CB + NGRP + 1], ctl[:, UB:UB + NGRP + 1], CAP, None, ALU.max))
                        s.link(dve.tensor_scalar(ctl[:, CB:CB + NGRP + 1], ctl[:, CB:CB + NGRP + 1], -CAP, None, ALU.add))

                    @block.gpsimd
                    def _(pool):
                        pool.wait_ge(ordered, 1)
                        for t in range(NTILE):
                            pool.indirect_dma_start(node_tab, bass.IndirectOffsetOnAxis(ap=pos[:, t:t + 1], axis=0),
                                                    rec[:, t, :], None).then_inc(placed, 16)

                    @block.sync
                    def _(sp):
                        sp.wait_ge(placed, 16 * NTILE)
                        sp.dma_start(node[:], node_tab.rearrange("(t p) c -> p t c", p=P)).then_inc(read_back, 16)
                        sp.wait_ge(read_back, 16)

        pk = sb("pk", [P, HK])
        imp = sb("imp", [P, T])
        Wj = sb("Wj", [P, T, D + HK])
        Wi = sb("Wi", [P, T * HK])
        bias = sb("bias", [P, D])
        hot = sb("hot", [P, T, T])
        with ExitStack() as c1:
            offi = sb("offi", [P, G], I32, c1)
            off = sb("off", [P, G], F32, c1)
            window = sb("window", [P, G, W], I32, c1)
            end = sb("end", [P, NTILE], F32, c1)
            start_of = sb("start_of", [P, NTILE], F32, c1)
            val = sb("val", [P, G, W], F32, c1)
            tf = sb("tf", [P, G, W], F32, c1)
            pn = sb("pn", [P, UPW, RB, G], I32, c1)
            pt = sb("pt", [P, UPW, RB, G], I32, c1)
            Wt = sb("Wt", [P, T, D], F32, c1)
            WT = sb("WT", [P, T, D], F32, c1)
            A2 = sb("A2", [P, 2, H, K], F32, c1)
            cf = sb("cf", [P, K], F32, c1)
            cs = sb("cs", [P, 4], F32, c1)
            turn_ps = psum("wturn_ps", [P, 2, 512], c1)
            loaded, zeroed, turned, kept, vecs, vkept, exp_in, exp_out = (
                sem(n, c1) for n in ("loaded", "zeroed", "turned", "kept", "vecs", "vkept", "exp_in", "exp_out"))
            LOADS = 16 * (4 + 2 * H * K)
            offsets, windows, listed, written, list_free, own, gone, features, marker = (
                sem(n, c1) for n in ("offsets", "windows", "listed", "written", "list_free", "own", "gone",
                                     "features", "marker"))
            with nc.Block() as block:
                def each_turn(eng, body, after=None):
                    wn = bounds(eng, WB, NGRP, [1] * NGRP, NWIN)
                    ub = unit_bounds(eng)
                    first = 0
                    for g in range(NGRP):
                        with eng.Fori(0, wn[g]) as w:
                            body(g, w, first + w, ub[g])
                        if after:
                            after(g)
                        first = first + wn[g]
                    return first

                @block.tensor
                def _(pe):
                    pe.wait_ge(loaded, LOADS)
                    for t in range(T):
                        pe.transpose(turn_ps[:, 0, t * D:(t + 1) * D], Wt[:, t, :], ident[:]).then_inc(turned, 1)
                    pe.wait_ge(kept, 1)
                    for t in range(T):
                        pe.matmul(turn_ps[:, 1, t * 64:t * 64 + 2 * HK], WT[:, t, :],
                                  A2[:].rearrange("p s h k -> p (s h k)"), start=True, stop=True).then_inc(vecs, 1)
                    pe.wait_ge(vkept, 1)

                @block.scalar
                def _(act):
                    act.dma_start(Wt[:], W2n.rearrange("t i o -> i t o")).then_inc(loaded, 16)
                    act.dma_start(cf[:], conf.rearrange("(o k) -> o k", o=1).to_broadcast([P, K])).then_inc(loaded, 16)
                    act.dma_start(imp[:], importance.rearrange("(o k) -> o k", o=1).to_broadcast([P, T])).then_inc(loaded, 16)
                    act.dma_start(bias[:], bias2.rearrange("(o k) -> o k", o=1).to_broadcast([P, D])).then_inc(loaded, 16)
                    act.wait_ge(zeroed, 1)
                    with nc.allow_non_contiguous_dma("1280 values, once"):
                        for h in range(H):
                            for side, at in ((0, C), (1, 0)):
                                for k in range(K):
                                    act.dma_start(A2[h * C:(h + 1) * C, side, h, k:k + 1],
                                                 att[k, h, at:at + C].rearrange("(c o) -> c o", o=1)).then_inc(loaded, 16)
                    act.wait_ge(exp_in, 1)
                    act.activation(cf[:], cf[:], ACT.Exp, accum_out=cs[:, 1:2]).then_inc(exp_out, 1)

                @block.gpsimd
                def _(pool):
                    def own_features(g):
                        for t in range(g * G, g * G + G):
                            pool.indirect_dma_start(X[:, t, :], None, h_tab[0],
                                                    bass.IndirectOffsetOnAxis(ap=node[:, t, 2:3], axis=0)
                                                    ).then_inc(features, 16)

                    def body(g, w, turn, u0):
                        pool.wait_ge(offsets, turn + 1)
                        pool.sem_inc(marker, 1)
                        for k in range(G):
                            pool.indirect_dma_start(window[:, k, :], None, flat(edge_pad),
                                                    bass.IndirectOffsetOnAxis(ap=offi[:, k:k + 1], axis=0)).then_inc(windows, 16)

                    each_turn(pool, body, after=own_features)
                    pool.wait_ge(features, 16 * NTILE)

                @block.vector
                def _(dve):
                    s = Steps(dve, own)
                    dve.tensor_tensor(end[:], nodef[:, :, 0], nodef[:, :, 1], ALU.add).then_inc(gone, 1)
                    dve.wait_ge(gone, 1)

                    def body(g, w, turn, u0):
                        s.restart()
                        cols = slice(g * G, (g + 1) * G)
                        s.link(dve.tensor_scalar(off[:], start_of[:, cols], float(E), None, ALU.min))
                        dve.tensor_copy(offi[:], off[:]).then_inc(offsets, 1)
                        s.link(dve.tensor_tensor(val[:], iota_w[:].unsqueeze(1).to_broadcast([P, G, W]),
                                                 off[:].unsqueeze(2).to_broadcast([P, G, W]), ALU.add))
                        s.link(dve.tensor_tensor(val[:], val[:], end[:, cols].unsqueeze(2).to_broadcast([P, G, W]), ALU.is_lt))
                        s.link(dve.tensor_scalar(start_of[:, cols], start_of[:, cols], float(W), None, ALU.add))
                        dve.wait_ge(windows, (turn + 1) * (G * 16))
                        dve.wait_ge(list_free, turn + 1)
                        s.link(dve.scalar_tensor_tensor(out=tf[:], in0=window[:], scalar=float(-N * T), in1=val[:],
                                                        op0=ALU.add, op1=ALU.mult))
                        s.link(dve.tensor_scalar(pt[:].rearrange("p u r k -> p (u r) k"), tf[:].rearrange("p k w -> p w k"),
                                                 float(N * T), None, ALU.add))
                        s.link(dve.tensor_scalar(pn[:], pt[:], T.bit_length() - 1, None, ALU.arith_shift_right))
                        dve.sem_inc(listed, 1)

                    dve.tensor_copy(start_of[:], nodef[:, :, 0]).then_inc(gone, 1)
                    dve.wait_ge(gone, 2)
                    dve.memset(A2[:], 0.0).then_inc(zeroed, 1)
                    each_turn(dve, body)
                    s.restart()
                    s.link(dve.memset(hot[:], 0.0))
                    for t in range(T):
                        s.go(dve.memset(hot[:, t, t:t + 1], 1.0))
                    dve.wait_ge(loaded, LOADS)
                    s.link(dve.tensor_reduce(cs[:, 0:1], cf[:], AX.X, ALU.max))
                    s.link(dve.tensor_scalar(cf[:], cf[:], cs[:, 0:1], None, ALU.subtract))
                    dve.sem_inc(exp_in, 1)
                    dve.wait_ge(exp_out, 1)
                    s.link(dve.reciprocal(cs[:, 2:3], cs[:, 1:2]))
                    s.link(dve.tensor_scalar(cf[:], cf[:], cs[:, 2:3], None, ALU.mult))
                    s.link(dve.tensor_copy(pk[:].rearrange("p (h k) -> p h k", h=H),
                                           cf[:].unsqueeze(1).to_broadcast([P, H, K])))
                    dve.wait_ge(turned, T)
                    s.go(dve.tensor_copy(Wj[:, :, 0:D], Wt[:]))
                    s.link(dve.tensor_copy(WT[:].rearrange("p t d -> p (t d)"), turn_ps[:, 0, :]))
                    dve.sem_inc(kept, 1)
                    dve.wait_ge(vecs, T)
                    vps = turn_ps[:, 1, 0:T * 64].rearrange("p (t n) -> p t n", n=64)
                    s.link(dve.tensor_copy(Wj[:, :, D:D + HK], vps[:, :, 0:HK]))
                    s.link(dve.tensor_copy(Wi[:].rearrange("p (t n) -> p t n", t=T), vps[:, :, HK:2 * HK]))
                    dve.sem_inc(vkept, 1)

                @block.sync
                def _(sp):
                    def body(g, w, turn, u0):
                        sp.wait_ge(listed, turn + 1)
                        at = bass.ds(u0 + w * UPW, UPW)
                        sp.dma_start(slot_node[at].rearrange("u p s -> p u s"),
                                     pn[:].rearrange("p u r k -> p u (r k)")).then_inc(written, 16)
                        sp.dma_start(slot_typed[at].rearrange("u p s -> p u s"),
                                     pt[:].rearrange("p u r k -> p u (r k)")).then_inc(written, 16)
                        sp.wait_ge(written, (turn + 1) * 32)
                        sp.sem_inc(list_free, 1)

                    sp.sem_inc(list_free, 1)
                    turns = each_turn(sp, body)
                    past = bass.ds(bounds(sp, UB + NGRP, 1, [NGRP], [unit_hi[NGRP]])[0], 1)
                    for lists, mine in ((slot_node, pn), (slot_typed, pt)):
                        sp.dma_start(lists[past].rearrange("u p s -> p (u s)"),
                                     mine[:, 0].rearrange("p r k -> p (r k)")).then_inc(written, 16)
                    sp.wait_ge(written, turns * 32 + 32)
                    sp.sem_inc(marker, 1)

        def sweep(eng, body, before=None, after=None):
            fb = bounds(eng, FB, NGRP + 1, [0, *range(1, NGRP + 1)], unit_hi)
            lone = bounds(eng, LONE, 1, [1], [unit_hi[1]])[0]
            for g in range(NGRP):
                if before:
                    before(g, (16 * G) * fb[g] + 16 * lone + 16 * G if g else 16 * G)
                with eng.Fori(fb[g], fb[g + 1]) as w:
                    if g == 0:
                        body(g, w, G, w, (16 * G) * w + 16 * G)
                    else:
                        body(g, nc.s_assert_within(w + lone, 0, unit_hi[NGRP] - 1), G, w,
                             (16 * G) * w + 16 * lone + 16 * G)
                if g == 0:
                    with eng.Fori(0, lone) as v:
                        body(g, nc.s_assert_within(v + fb[1], 0, unit_hi[1] - 1), 1, None,
                             16 * v + (16 * G) * fb[1] + 16)
                if after:
                    after(g, fb[g + 1] + lone)

        def load_slots(sp, lists, slot, slots_in, rows_in, units=None, first=0):
            def load(u, q):
                sp.dma_start(slot[q][:], lists[bass.ds(u + first, 1), :, q * G:(q + 1) * G]
                             .rearrange("o p k -> (o p) k")).then_inc(slots_in[q], 16)

            def body(g, u, n, w, rows):
                for q in range(RB):
                    sp.wait_ge(rows_in[q], rows)
                    load(u + 1, q)

            for q in range(RB):
                load(0, q)
            if units is None:
                sweep(sp, body)
                units = bounds(sp, UB + NGRP, 1, [NGRP], [unit_hi[NGRP]])[0]
            else:
                with sp.Fori(0, units) as u:
                    body(None, u, G, u, (16 * G) * u + 16 * G)
            for q in range(RB):
                sp.wait_ge(slots_in[q], 16 * units + 16)
                sp.sem_inc(pass_marker, 1)

        def gather_rank(pool, u, n, q, table, slot, rows, slots_in, rows_in, rows_free, marker):
            pool.wait_ge(slots_in[q], 16 * u + 16)
            pool.wait_ge(rows_free[q], u + 1)
            pool.sem_inc(marker, 1)
            for k in range(n):
                pool.indirect_dma_start(rows[q][:, k, :], None, table,
                                        bass.IndirectOffsetOnAxis(ap=slot[q][:, k:k + 1], axis=0)
                                        ).then_inc(rows_in[q], 16)

        def gather_unit(pool, u, n, table, slot, rows, slots_in, rows_in, rows_free, marker):
            for q in range(RB):
                gather_rank(pool, u, n, q, table, slot, rows, slots_in, rows_in, rows_free, marker)

        def scatter_group(pool, g, table, rows_of, stored):
            for k in range(G):
                t = g * G + k
                pool.indirect_dma_start(table, bass.IndirectOffsetOnAxis(ap=node[:, t, 2:3], axis=0),
                                        rows_of(t), None).then_inc(stored, 16)

        pass_sems = [[sem(f"{name}{q}", ctx) for q in range(RB)] for name in ("slots_in", "rows_free")]
        pass_marker = sem("pass_marker", ctx)
        out_stored = sem("out_stored", ctx)
        passes = [0]

        def pass_memory(c, width, pairs=False):
            if passes[0]:
                with nc.Block() as block:
                    @block.sync
                    def _(sp):
                        for one in (*pass_sems[0], *pass_sems[1], pass_marker):
                            sp.sem_clear(one)
            passes[0] += 1
            if pairs:
                rows = [sb(f"pair{p}", [P, 2, G, width], F32, c) for p in range(RB // 2)]
            else:
                rows = [sb(f"rows{q}", [P, G, width], F32, c) for q in range(RB)]
            slot = [sb(f"slot{q}", [P, G], I32, c) for q in range(RB)]
            rows_in = [sem(f"rows_in{q}", ctx) for q in range(RB)]
            return rows, slot, pass_sems[0], rows_in, pass_sems[1], pass_marker

        def add_rows(pe, acc, rows, n=G, start=False):
            if n == 1:
                return pe.matmul(acc[:, 0:P], ident[:], rows[:, 0, 0:D], start=start, stop=False, skip_group_check=True)
            pe.matmul(acc[:, 0:4 * P].rearrange("p (k d) -> p k d", k=4), ident[:], rows[:, 0:4, 0:D],
                      start=start, stop=False, skip_group_check=True)
            return pe.matmul(acc[:, 4 * P:5 * P], ident[:], rows[:, 4, 0:D], start=start, stop=False,
                             skip_group_check=True)

        def clear_sums(pe, acc):
            pe.matmul(acc[:, 0:4 * P], ident[:], zeros[:], start=True, stop=False, skip_group_check=True)
            pe.matmul(acc[:, 4 * P:5 * P], ident[:], zeros[:, 0:P], start=True, stop=False, skip_group_check=True)

        def cols(g):
            return slice(g * G, (g + 1) * G)

        def wide(ap, n=D):
            return ap.unsqueeze(2).to_broadcast([P, G, n])

        def normalise(s, dve, g, A, B, st, std_in, std_out, turn):
            a, b = A[:, cols(g), :], B[:]
            s.link(dve.tensor_reduce(st[:, 0, :], a, AX.X, ALU.add))
            s.link(dve.tensor_scalar(st[:, 0, :], st[:, 0, :], 1.0 / D, None, ALU.mult))
            s.link(dve.tensor_tensor(a, a, wide(st[:, 0, :]), ALU.subtract))
            s.link(dve.tensor_tensor(b, a, a, ALU.mult))
            s.link(dve.tensor_reduce(st[:, 1, :], b, AX.X, ALU.add))
            dve.tensor_scalar(st[:, 1, :], st[:, 1, :], 1.0 / D, LN_EPS, ALU.mult, ALU.add).then_inc(std_in, 1)
            dve.wait_ge(std_out, turn + 1)
            s.link(dve.reciprocal(st[:, 3, :], st[:, 2, :]))
            s.link(dve.tensor_tensor(a, a, wide(st[:, 3, :]), ALU.mult))

        def roots(act, st, std_in, std_out, turn):
            act.wait_ge(std_in, turn + 1)
            act.activation(st[:, 2, :], st[:, 1, :], ACT.Sqrt).then_inc(std_out, 1)

        for layer in range(3):
            with ExitStack() as c1:
                rows, slot, slots_in, rows_in, rows_free, marker = pass_memory(c1, D)
                acc = psum("acc", [P, 2, 1024], c1)
                own, summed, stored = sem("own", c1), sem("summed", c1), sem("stored", c1)
                with nc.Block() as block:
                    @block.sync
                    def _(sp):
                        load_slots(sp, slot_node, slot, slots_in, rows_in)

                    @block.gpsimd
                    def _(pool):
                        def store(g):
                            pool.wait_ge(summed, g + 1)
                            scatter_group(pool, g, h_tab[layer + 1], lambda t: X[:, t, :], stored)

                        def stores(g, units):
                            if g and layer < 2:
                                store(g - 1)

                        sweep(pool, lambda g, u, n, w, in_: gather_unit(
                            pool, u, n, h_tab[layer], slot, rows, slots_in, rows_in, rows_free, marker), after=stores)
                        if layer < 2:
                            store(NGRP - 1)
                            pool.wait_ge(stored, 16 * NTILE)

                    @block.tensor
                    def _(pe):
                        def clear(g, first):
                            if g >= 2:
                                pe.wait_ge(summed, g - 1)
                            clear_sums(pe, acc[:, g % 2, :])

                        def body(g, u, n, w, in_):
                            for q in range(RB):
                                pe.wait_ge(rows_in[q], in_)
                                add_rows(pe, acc[:, g % 2, :], rows[q], n).then_inc(rows_free[q], 1)

                        for q in range(RB):
                            pe.sem_inc(rows_free[q], 1)
                        sweep(pe, body, before=clear)

                    @block.vector
                    def _(dve):
                        ub = unit_bounds(dve)
                        s = Steps(dve, own)
                        for g in range(NGRP):
                            if layer == 0:
                                s.link(dve.tensor_scalar(RES[:, cols(g), :], X[:, cols(g), :], 2.0, None, ALU.mult))
                            dve.wait_ge(rows_free[RB - 1], ub[g + 1] + 1)
                            for k in range(G):
                                t = g * G + k
                                s.go(dve.scalar_tensor_tensor(
                                    out=X[:, t, :], in0=acc[:, g % 2, k * P:(k + 1) * P], scalar=rdeg[:, t:t + 1],
                                    in1=X[:, t, :], op0=ALU.mult, op1=ALU.add))
                            s.need(s.n)
                            dve.sem_inc(summed, 1)
                            for k in range(G):
                                t = g * G + k
                                s.go(dve.scalar_tensor_tensor(
                                    out=RES[:, t, :], in0=X[:, t, :], scalar=1.0 / (1.0 + layer),
                                    in1=RES[:, t, :], op0=ALU.mult, op1=ALU.add))
                        s.need(s.n)

        with ExitStack() as c1:
            stage = [sb(f"stage{i}", [P, G, MW], F32, c1) for i in range(2)]
            sq = sb("sq", [P, G, D], F32, c1)
            st = sb("st", [P, 4, G], F32, c1)
            own, std_in, std_out, staged = (sem(n, c1) for n in ("own", "std_in", "std_out", "staged"))
            stored = [sem(f"stored{i}", c1) for i in range(2)]
            with nc.Block() as block:
                @block.vector
                def _(dve):
                    s = Steps(dve, own)
                    for i in range(2):
                        s.go(dve.memset(stage[i][:], 0.0))
                    for g in range(NGRP):
                        normalise(s, dve, g, RES, sq, st, std_in, std_out, g)
                        x1 = RES[:, cols(g), :]
                        s.link(dve.tensor_copy(X[:, cols(g), :], x1))
                        s.link(dve.tensor_tensor(sq[:], x1, x1, ALU.mult))
                        s.link(dve.tensor_reduce(d2[:, cols(g)], sq[:], AX.X, ALU.add))
                        if g >= 2:
                            dve.wait_ge(stored[g % 2], 16 * G * (g // 2))
                        b = stage[g % 2]
                        s.go(dve.tensor_copy(b[:, :, 0:D], x1))
                        s.go(dve.tensor_copy(b[:, :, D], d2[:, cols(g)]))
                        s.go(dve.tensor_copy(b[:, :, D + 1], real[:, cols(g)]))
                        s.need(s.n)
                        dve.sem_inc(staged, 1)

                @block.scalar
                def _(act):
                    for g in range(NGRP):
                        roots(act, st, std_in, std_out, g)

                @block.gpsimd
                def _(pool):
                    for g in range(NGRP):
                        pool.wait_ge(staged, g + 1)
                        scatter_group(pool, g, m_tab, lambda t: stage[g % 2][:, t - g * G, :], stored[g % 2])
                    pool.wait_ge(stored[0], 16 * G * ((NGRP + 1) // 2))
                    pool.wait_ge(stored[1], 16 * G * (NGRP // 2))

        with ExitStack() as c1:
            gam = sb("gam", [P, NTILE], F32, c1)
            with ExitStack() as c2:
                rows, slot, slots_in, rows_in, rows_free, marker = pass_memory(c2, MW)
                junk = sb("junk", [P, 2 * G, D], F32, c2)
                us = sb("us", [P, G, D], F32, c2)
                sums = sb("sums", [P, NGRP, 3, G], F32, c2)
                squares = sb("squares", [P, NGRP, 4, G], F32, c2)
                two = lambda name, n: [sb(f"{name}{i}", [P, n, G], F32, c2) for i in range(2)]
                sdd, den, nn, mm, tmp = two("sdd", 3), two("den", 2), two("nn", 2), two("mm", 4), two("tmp", 2)
                mix = two("mix", 4)
                p3 = sb("p3", [P, 3, G], F32, c2)
                ab = sb("ab", [P, 2, G], F32, c2)
                nb = sb("nb", [P, 2, G], F32, c2)
                bab = sb("bab", [P, 3, G], F32, c2)
                dn = sb("dn", [P, G], F32, c2)
                z4 = sb("z4", [P, 4, G], F32, c2)
                z2 = sb("z2", [P, 2, G], F32, c2)
                w2 = sb("w2", [P, 2, G], F32, c2)
                own, scaled, scale_in = sem("own", c2), sem("scaled", c2), sem("scale_in", c2)
                attr = [sb(f"attr{k}", [P, RB, D], F32, c2) for k in range(G)]
                offs = sb("offs", [P, G], I32, c2)
                off = sb("off", [P, G], F32, c2)
                at0 = sb("at0", [P, NTILE], F32, c2)
                end = sb("end", [P, NTILE], F32, c2)
                eid = sb("eid", [P, G, RB], F32, c2)
                val = sb("val", [P, G, RB], F32, c2)
                val2 = sb("val2", [P, G, RB], F32, c2)
                acc = psum("acc", [P, 2, 1024], c2)
                offsets, masked, added, summed = (sem(n, c2) for n in ("offsets", "masked", "added", "summed"))
                attr_in = [sem(f"attr_in{k}", c2) for k in range(G)]
                mask_after = {1: (0, 1), 2: (2, 3), 3: (4,)}
                with nc.Block() as block:
                    @block.sync
                    def _(sp):
                        load_slots(sp, slot_node, slot, slots_in, rows_in)

                    @block.gpsimd
                    def _(pool):
                        def body(g, u, n, w, in_):
                            gather_unit(pool, u, n, m_tab, slot, rows, slots_in, rows_in, rows_free, marker)
                            pool.wait_ge(offsets, u + 1)
                            pool.wait_ge(added, u + 1)
                            pool.sem_inc(marker, 1)
                            for k in range(n):
                                pool.indirect_dma_start(attr[k][:].rearrange("p r d -> p (r d)"), None, flat(edge_attr),
                                                        bass.IndirectOffsetOnAxis(ap=offs[:, k:k + 1], axis=0)
                                                        ).then_inc(attr_in[k], 16)

                        ub = unit_bounds(pool)
                        sweep(pool, body)
                        for q in range(2):
                            gather_rank(pool, ub[NGRP], G, q, m_tab, slot, rows, slots_in, rows_in, rows_free, marker)

                    @block.tensor
                    def _(pe):
                        def clear(g, first):
                            if g >= 2:
                                pe.wait_ge(summed, g - 1)
                            clear_sums(pe, acc[:, g % 2, :])

                        def body(g, u, n, w, in_):
                            for k in range(n):
                                pe.wait_ge(masked, u * G + (G + (k + 1 if n == G else G)))
                                for r in range(RB):
                                    mm = pe.matmul(acc[:, g % 2, k * P:(k + 1) * P], ident[:], attr[k][:, r, :],
                                                   start=False, stop=False, skip_group_check=True)
                            mm.then_inc(added, 1)

                        pe.sem_inc(added, 1)
                        sweep(pe, body, before=clear)

                    @block.scalar
                    def _(act):
                        def body(g, u, n, w, in_):
                            for q in range(RB):
                                act.wait_ge(scale_in, u * RB + (q + 1))
                                for k in range(n):
                                    a = act.activation(us[:, k, :], O[:, g * G + k, :], ACT.Copy,
                                                       scale=ab[:, 0, k:k + 1])
                                a.then_inc(scaled, 1)
                                for k in mask_after.get(q, ()):
                                    if k < n:
                                        act.wait_ge(attr_in[k], 16 * (w if k else u) + 16)
                                        for r in range(RB):
                                            a = act.activation(attr[k][:, r, :], attr[k][:, r, :], ACT.Copy,
                                                               scale=val[:, k, r:r + 1])
                                        a.then_inc(masked, 1 if n == G else G)

                        def take(g, units):
                            act.wait_ge(added, units + 1)
                            act.activation(ATT[:, cols(g), :], acc[:, g % 2, 0:5 * P].rearrange("p (k d) -> p k d", k=G),
                                           ACT.Copy).then_inc(summed, 1)

                        sweep(act, body, after=take)
                        act.wait_ge(summed, NGRP)

                    @block.vector
                    def _(dve):
                        s = Steps(dve, own)
                        TT, TS, STT = dve.tensor_tensor, dve.tensor_scalar, dve.scalar_tensor_tensor

                        for a in (O, sums, squares):
                            s.go(dve.memset(a[:], 0.0))
                        s.go(TT(end[:], nodef[:, :, 0], nodef[:, :, 1], ALU.add))
                        s.go(dve.tensor_copy(at0[:], nodef[:, :, 0]))
                        dve.sem_inc(masked, G)
                        s.need(s.n)
                        for q in range(RB):
                            dve.sem_inc(rows_free[q], 1)

                        def each(ap, n):
                            return ap.unsqueeze(1).to_broadcast([P, n, G])

                        def dots(g, n, in_, q):
                            dve.wait_ge(rows_in[q], in_)
                            for k in range(n):
                                dotted[q % 2] = s.go(dve.tensor_tensor_reduce(
                                    junk[:, k, :], rows[q][:, k, 0:D], X[:, g * G + k, :], 1.0, 0.0,
                                    ALU.mult, ALU.add, sdd[q % 2][:, 1, k:k + 1]))

                        def message(g, q):
                            R, c, i = rows[q], cols(g), q % 2
                            s2, valid = R[:, :, D], R[:, :, D + 1]
                            sd, dot, dd = sdd[i], sdd[i][:, 1, :], d2[:, c]
                            s.go(dve.tensor_copy(sd[:, 0, :], s2))
                            s.go(TT(den[i][:, 0, :], s2, dd, ALU.mult))
                            s.go(TS(nn[i][:, 1, :], s2, -1.0, None, ALU.add))
                            yield
                            s.need(dotted[i])
                            t = s.go(TS(tmp[i][:, 0, :], dot, -2.0, 1.0, ALU.mult, ALU.add))
                            yield
                            s.need(t)
                            t1 = s.go(TT(den[i][:, 0, :], den[i][:, 0, :], tmp[i][:, 0, :], ALU.add))
                            s.go(TT(nn[i][:, 0, :], tmp[i][:, 0, :], dd, ALU.add))
                            yield
                            s.need(t1)
                            t = s.go(TS(den[i][:, 0, :], den[i][:, 0, :], MOB_EPS, None, ALU.max))
                            yield
                            s.need(t)
                            t = s.go(dve.reciprocal(den[i][:, 0, :], den[i][:, 0, :]))
                            yield
                            s.need(t)
                            t = s.go(TT(den[i][:, 0, :], den[i][:, 0, :], valid, ALU.mult))
                            yield
                            s.need(t)
                            t = s.go(TT(mix[i][:, 2:4, :], nn[i][:], each(den[i][:, 0, :], 2), ALU.mult))
                            yield
                            s.need(t)
                            al, be = mix[i][:, 2, :], mix[i][:, 3, :]
                            s.go(TT(mix[i][:, 0:2, :], sd[:, 0:2, :], each(al, 2), ALU.mult))
                            t = s.go(TT(tmp[i][:], sd[:, 1:3, :], each(be, 2), ALU.mult))
                            yield
                            s.need(t)
                            t = s.go(TT(mm[i][:, 0:2, :], mix[i][:, 0:2, :], tmp[i][:], ALU.add))
                            yield
                            s.need(t)
                            t = s.go(TT(tmp[i][:], mm[i][:, 0:2, :], mix[i][:, 2:4, :], ALU.mult))
                            yield
                            s.need(t)
                            t = s.go(TT(mm[i][:, 2, :], tmp[i][:, 0, :], tmp[i][:, 1, :], ALU.add))
                            yield
                            s.need(t)
                            t = s.go(TS(mm[i][:, 3, :], mm[i][:, 2, :], 1.0, None, ALU.add))
                            ready[i] = t
                            yield

                        def add_message(g, u, n, q, side, after_next=None):
                            R, i = rows[q], q % 2
                            G2, quad = sums[:, g, 0:3:2, :], squares[:, g]
                            S2 = quad[:, 0, :]
                            y2, mp = mm[i][:, 2, :], mm[i][:, 1, :]
                            for k in range(n):
                                s.go(dve.tensor_tensor_reduce(junk[:, G + k, :], R[:, k, 0:D], O[:, g * G + k, :], 1.0, 0.0,
                                                              ALU.mult, ALU.add, sums[:, g, 1, k:k + 1]))
                            s.need(ready[i])
                            s.go(dve.tensor_copy(quad[:, 3, :], y2))
                            s.go(TS(nb[:, 1, :], S2, -1.0, 1.0, ALU.mult, ALU.add))
                            xx = s.go(TT(tmp[i][:, 0, :], S2, y2, ALU.mult))
                            s.need(xx)
                            t = s.go(TT(p3[:], sums[:, g], mix[i][:, 1:4, :], ALU.mult))
                            next(side, None)
                            s.need(t)
                            t = s.go(TT(dn[:], p3[:, 0, :], p3[:, 1, :], ALU.add))
                            next(side, None)
                            s.need(t)
                            xy = quad[:, 1, :]
                            t = s.go(TT(xy, dn[:], p3[:, 2, :], ALU.add))
                            next(side, None)
                            s.need(t)
                            t = s.go(STT(out=dn[:], in0=xy, scalar=2.0, in1=tmp[i][:, 0, :], op0=ALU.mult, op1=ALU.add))
                            s.go(STT(out=nb[:, 0, :], in0=xy, scalar=2.0, in1=mm[i][:, 3, :], op0=ALU.mult, op1=ALU.add))
                            s.go(dve.tensor_copy(quad[:, 2, :], xy))
                            next(side, None)
                            s.need(t)
                            t = s.go(TS(dn[:], dn[:], 1.0, MOB_EPS, ALU.add, ALU.max))
                            next(side, None)
                            s.need(t)
                            t = s.go(dve.reciprocal(dn[:], dn[:]))
                            next(side, None)
                            s.need(t)
                            s.link(TT(ab[:], nb[:], each(dn[:], 2), ALU.mult))
                            dve.sem_inc(scale_in, 1)
                            A, B = each(ab[:, 0, :], 2), each(ab[:, 1, :], 2)
                            s.go(TT(bab[:, 0:2, :], mix[i][:, 2:4, :], B, ALU.mult))
                            s.go(TT(w2[:], G2, A, ALU.mult))
                            t1 = s.go(TT(z4[:].rearrange("p (a b) k -> p a b k", a=2), quad.rearrange("p (a b) k -> p a b k", a=2),
                                         ab[:].unsqueeze(1).to_broadcast([P, 2, 2, G]), ALU.mult))
                            t2 = s.go(TT(bab[:, 2, :], mp, ab[:, 1, :], ALU.mult))
                            next(side, None)
                            s.need(t2)
                            t = s.go(TT(z2[:], z4[:, 0:4:2, :], z4[:, 1:4:2, :], ALU.add))
                            next(side, None)
                            s.need(t)
                            s.go(TT(G2[:, :, 0:n], w2[:, :, 0:n], bab[:, 1:3, 0:n], ALU.add))
                            t = s.go(TT(z2[:], z2[:], ab[:], ALU.mult))
                            next(side, None)
                            s.need(t)
                            t = s.go(TT(S2[:, 0:n], z2[:, 0, 0:n], z2[:, 1, 0:n], ALU.add))
                            next(side, None)
                            if after_next:
                                dots(g, n, *after_next)
                            dve.wait_ge(scaled, u * RB + (q + 1))
                            for k in range(n):
                                t = s.go(STT(out=O[:, g * G + k, :], in0=R[:, k, 0:D], scalar=bab[:, 0, k:k + 1],
                                             in1=us[:, k, :], op0=ALU.mult, op1=ALU.add))
                                next(side, None)
                            s.need(t)
                            dve.sem_inc(rows_free[q], 1)
                            for _ in side:
                                pass

                        def reads(g, u):
                            c = cols(g)
                            dve.wait_ge(masked, u * G + G)
                            t = s.go(TS(off[:], at0[:, c], float(E - RB), None, ALU.min))
                            yield
                            s.need(t)
                            s.go(TS(offs[:], off[:], float(D), None, ALU.mult))
                            t = s.go(TT(eid[:], iota_w[:, 0:RB].unsqueeze(1).to_broadcast([P, G, RB]), wide(off[:], RB),
                                        ALU.add))
                            yield
                            s.need(t)
                            s.go(TT(val[:], eid[:], wide(at0[:, c], RB), ALU.is_ge))
                            t = s.go(TT(val2[:], eid[:], wide(end[:, c], RB), ALU.is_lt))
                            yield
                            s.need(t)
                            s.go(TS(at0[:, c], at0[:, c], float(RB), None, ALU.add))
                            t = s.go(TT(val[:], val[:], val2[:], ALU.mult))
                            yield
                            s.need(t)
                            dve.sem_inc(offsets, 1)

                        def both(a, b):
                            for _ in a:
                                next(b, None)
                                yield
                            for _ in b:
                                yield

                        ready, dotted = [0, 0], [0, 0]

                        def ahead(g, first):
                            s.restart()
                            for i in range(2):
                                s.go(dve.tensor_copy(sdd[i][:, 2, :], d2[:, cols(g)]))
                            s.need(s.n)
                            if g:
                                dots(g, G, first, 0)
                                for _ in message(g, 0):
                                    pass
                                dots(g, G, first, 1)
                                s.need(s.n)

                        def body(g, u, n, w, in_):
                            s.restart()
                            ready[0] = dotted[1] = 0
                            if g == 0:
                                dots(g, n, in_, 0)
                                for _ in message(g, 0):
                                    pass
                                dots(g, n, in_, 1)
                            for q in range(RB - 1):
                                side = message(g, q + 1)
                                add_message(g, u, n, q, side if q else both(side, reads(g, u)),
                                            (in_, q + 2) if q + 2 < RB else (in_ + 16 * G, 0) if g else None)
                            if g == 0:
                                add_message(g, u, n, RB - 1, iter(()))
                            else:
                                add_message(g, u, n, RB - 1, message(g, 0), (in_ + 16 * G, 1))
                                s.need(s.n)

                        sweep(dve, body, before=ahead)
                        s.restart()
                        s.link(dve.tensor_copy(gam[:].rearrange("p (g k) -> p g k", g=NGRP), sums[:, :, 0, :]))

            with ExitStack() as c2:
                junk = sb("junk", [P, NTILE, D], F32, c2)
                st = sb("st", [P, 4, G], F32, c2)
                sq = sb("sq", [P, G, D], F32, c2)
                names = "n2 xo nrm nc lp lm z th f ok y2 xy den c1 c2 t".split()
                v = {n: sb("w_" + n, [P, NTILE], F32, c2) for n in names}
                V = {n: v[n][:] for n in names}
                own, roots_in, roots_out, std_in, std_out = (
                    sem(n, c2) for n in ("own", "roots_in", "roots_out", "std_in", "std_out"))
                with nc.Block() as block:
                    @block.scalar
                    def _(act):
                        act.wait_ge(roots_in, 1)
                        act.activation(V["nrm"], V["n2"], ACT.Sqrt).then_inc(roots_out, 1)
                        act.wait_ge(roots_in, 2)
                        act.activation(V["lp"], V["lp"], ACT.Ln).then_inc(roots_out, 1)
                        act.activation(V["lm"], V["lm"], ACT.Ln).then_inc(roots_out, 1)
                        act.wait_ge(roots_in, 3)
                        act.activation(V["th"], V["z"], ACT.Tanh).then_inc(roots_out, 1)
                        for g in range(NGRP):
                            roots(act, st, std_in, std_out, g)

                    @block.vector
                    def _(dve):
                        s = Steps(dve, own)
                        TT, TS, STT = dve.tensor_tensor, dve.tensor_scalar, dve.scalar_tensor_tensor

                        def tt(o, a, b, op=ALU.mult):
                            s.link(TT(V[o], a, b, op))

                        for t in range(NTILE):
                            s.go(STT(out=O[:, t, :], in0=X[:, t, :], scalar=gam[:, t:t + 1], in1=O[:, t, :],
                                     op0=ALU.mult, op1=ALU.add))
                        s.need(s.n)
                        for t in range(NTILE):
                            s.go(dve.tensor_tensor_reduce(junk[:, t, :], O[:, t, :], O[:, t, :], 1.0, 0.0,
                                                          ALU.mult, ALU.add, v["n2"][:, t:t + 1]))
                        s.need(s.n)
                        dve.sem_inc(roots_in, 1)
                        for t in range(NTILE):
                            s.go(dve.tensor_tensor_reduce(junk[:, t, :], O[:, t, :], X[:, t, :], 1.0, 0.0,
                                                          ALU.mult, ALU.add, v["xo"][:, t:t + 1]))
                        s.need(s.n)
                        dve.wait_ge(roots_out, 1)
                        s.link(TS(V["nc"], V["nrm"], MOB_EPS, 1.0 - MOB_EPS, ALU.max, ALU.min))
                        s.link(TS(V["lp"], V["nc"], 1.0, 1.0, ALU.mult, ALU.add))
                        s.link(TS(V["lm"], V["nc"], -1.0, 1.0, ALU.mult, ALU.add))
                        dve.sem_inc(roots_in, 1)
                        dve.wait_ge(roots_out, 3)
                        tt("z", V["lp"], V["lm"], ALU.subtract)
                        tt("z", V["z"], rdeg[:])
                        s.link(TS(V["z"], V["z"], 0.5, None, ALU.mult))
                        dve.sem_inc(roots_in, 1)
                        s.link(dve.reciprocal(V["f"], V["nc"]))
                        s.link(TS(V["ok"], V["nrm"], MOB_EPS, None, ALU.is_gt))
                        dve.wait_ge(roots_out, 4)
                        tt("f", V["f"], V["th"])
                        tt("f", V["f"], V["ok"])
                        tt("xy", V["f"], V["xo"])
                        tt("t", V["f"], V["f"])
                        tt("y2", V["t"], V["n2"])
                        tt("t", d2[:], V["y2"])
                        s.link(TS(V["xy"], V["xy"], 2.0, 1.0, ALU.mult, ALU.add))
                        tt("den", V["xy"], V["t"], ALU.add)
                        s.link(TS(V["den"], V["den"], MOB_EPS, None, ALU.max))
                        s.link(dve.reciprocal(V["den"], V["den"]))
                        tt("c1", V["xy"], V["y2"], ALU.add)
                        tt("c1", V["c1"], V["den"])
                        s.link(TS(V["c1"], V["c1"], 1.0, None, ALU.add))
                        s.link(TS(V["c2"], d2[:], -1.0, 1.0, ALU.mult, ALU.add))
                        tt("c2", V["c2"], V["f"])
                        tt("c2", V["c2"], V["den"])
                        for t in range(NTILE):
                            s.go(TS(O[:, t, :], O[:, t, :], v["c2"][:, t:t + 1], None, ALU.mult))
                        s.need(s.n)
                        for t in range(NTILE):
                            s.go(STT(out=X[:, t, :], in0=X[:, t, :], scalar=v["c1"][:, t:t + 1], in1=O[:, t, :],
                                     op0=ALU.mult, op1=ALU.add))
                        s.need(s.n)
                        for g in range(NGRP):
                            normalise(s, dve, g, X, sq, st, std_in, std_out, g)

        l2 = ctx.enter_context(ExitStack())
        XA = l2.enter_context(nc.sbuf_tensor("XA", [P, NTILE, T * HK], F32))
        with ExitStack() as c1:
            xT = [sb(f"xT{i}", [P, D], F32, c1) for i in range(2)]
            stage = [sb(f"tstage{i}", [P, T, TW], F32, c1) for i in range(2)]
            turn_ps = psum("turn_ps", [P, 2, 512], c1)
            prod_ps = psum("prod_ps", [P, 2, 1024], c1)
            own, staged = sem("own", c1), sem("staged", c1)
            x_turned, x_kept, multiplied = (sem(n, c1) for n in ("x_turned", "x_kept", "multiplied"))
            stored = [sem(f"stored{i}", c1) for i in range(2)]
            with nc.Block() as block:
                @block.tensor
                def _(pe):
                    wj = Wj[:].rearrange("p t n -> p (t n)")
                    CUT = 3 * (D + HK)
                    for t in range(NTILE):
                        b = t % 2
                        if t == 0:
                            pe.transpose(turn_ps[:, 0, 0:D], X[:, 0, :], ident[:]).then_inc(x_turned, 1)
                        if t + 1 < NTILE:
                            pe.transpose(turn_ps[:, 1 - b, 0:D], X[:, t + 1, :], ident[:]).then_inc(x_turned, 1)
                        pe.wait_ge(x_kept, t + 1)
                        if t >= 2:
                            pe.wait_ge(staged, t - 1)
                        pe.matmul(prod_ps[:, b, 0:CUT], xT[b][:], wj[:, 0:CUT], start=True, stop=True)
                        pe.matmul(prod_ps[:, b, 512:512 + D + HK], xT[b][:], wj[:, CUT:], start=True, stop=True)
                        pe.matmul(prod_ps[:, b, 512 + D + HK:512 + D + HK + T * HK], xT[b][:], Wi[:],
                                  start=True, stop=True).then_inc(multiplied, 1)

                @block.scalar
                def _(act):
                    for t in range(NTILE):
                        act.wait_ge(x_turned, t + 1)
                        if t >= 2:
                            act.wait_ge(multiplied, t - 1)
                        act.activation(xT[t % 2][:], turn_ps[:, t % 2, 0:D], ACT.Copy).then_inc(x_kept, 1)

                @block.vector
                def _(dve):
                    s = Steps(dve, own)
                    for i in range(2):
                        s.go(dve.memset(stage[i][:], 0.0))
                    s.need(s.n)
                    for t in range(NTILE):
                        b = stage[t % 2]
                        dve.wait_ge(multiplied, t + 1)
                        if t >= 2:
                            dve.wait_ge(stored[t % 2], 16 * (t // 2))
                        s.go(dve.tensor_copy(b[:, 0:3, 0:D + HK],
                                             prod_ps[:, t % 2, 0:3 * (D + HK)].rearrange("p (t n) -> p t n", t=3)))
                        s.go(dve.tensor_copy(b[:, 3, 0:D + HK], prod_ps[:, t % 2, 512:512 + D + HK]))
                        s.go(dve.tensor_scalar(b[:, :, D + HK:TW], hot[:], real[:, t:t + 1], None, ALU.mult))
                        s.go(dve.tensor_copy(XA[:, t, :], prod_ps[:, t % 2, 512 + D + HK:512 + D + HK + T * HK]))
                        s.link(dve.tensor_tensor(RES[:, t, :], X[:, t, :], prod_ps[:, t % 2, 0:D], ALU.add))
                        dve.sem_inc(staged, 1)
                        s.link(dve.tensor_tensor(RES[:, t, :], RES[:, t, :], bias[:], ALU.add))

                @block.gpsimd
                def _(pool):
                    for t in range(NTILE):
                        pool.wait_ge(staged, t + 1)
                        pool.indirect_dma_start(t_tab, bass.IndirectOffsetOnAxis(ap=node[:, t, 2:3], axis=0),
                                                stage[t % 2][:].rearrange("p t n -> p (t n)"), None
                                                ).then_inc(stored[t % 2], 16)
                    pool.wait_ge(stored[0], 16 * ((NTILE + 1) // 2))
                    pool.wait_ge(stored[1], 16 * (NTILE // 2))

        MX = sb("MX", [P, NTILE, T, 2, H])
        t_rows = t_tab.rearrange("n (t w) -> (n t) w", t=T)
        NPAIR = RB // 2
        G2 = 2 * G
        SW = H + T
        kept_rows = dram("kept_rows", [CAP + 1, NPAIR, P, G2 * D])
        kept_scores = dram("kept_scores", [CAP + 1, NPAIR, P, G2 * SW])

        def both_ranks(a, n=G):
            return a.rearrange("p j k w -> p (j k) w") if n == G else a[:, :, 0, :]

        def scores(s, dve, R, g, n, prod, sc, al):
            xa = XA[:, g * G:g * G + n, :].rearrange("p k (t n) -> p k t n", t=T)
            m = 2 * n
            for j in range(2):
                t = s.go(dve.tensor_tensor(prod[:, j * n:(j + 1) * n, :, 0:HK], xa,
                                           R[:, j, 0:n, D + HK:TW].unsqueeze(3).to_broadcast([P, n, T, HK]), ALU.mult))
                yield
            s.need(t)
            t = s.go(dve.tensor_reduce(sc[:, 0:m], prod[:, 0:m, :, 0:HK].rearrange("p k t n -> p k n t"), AX.X, ALU.add))
            yield
            s.need(t)
            t = s.go(dve.tensor_tensor(sc[:, 0:m], sc[:, 0:m], both_ranks(R, n)[:, :, D:D + HK], ALU.add))
            yield
            s.need(t)
            t = s.go(dve.scalar_tensor_tensor(out=sc[:, 0:m], in0=sc[:, 0:m], scalar=0.2, in1=sc[:, 0:m],
                                              op0=ALU.mult, op1=ALU.max))
            yield
            s.need(t)
            t = s.go(dve.tensor_tensor(sc[:, 0:m], sc[:, 0:m], pk[:].unsqueeze(1).to_broadcast([P, m, HK]), ALU.mult))
            yield
            s.need(t)
            t = s.go(dve.tensor_reduce(al[:, 0:m], sc[:, 0:m].rearrange("p k (h c) -> p k h c", h=H), AX.X, ALU.add))
            yield
            s.need(t)

        def pair_memory(c, width):
            pairs, slot, slots_in, rows_in, rows_free, marker = pass_memory(c, width, pairs=True)
            return pairs, [pairs[q // 2][:, q % 2] for q in range(RB)], slot, slots_in, rows_in, rows_free, marker

        with ExitStack() as c1:
            pairs, rows, slot, slots_in, rows_in, rows_free, marker = pair_memory(c1, TW)
            keep = [sb(f"keep{p}", [P, G2, D], F32, c1) for p in range(NPAIR)]
            small = [sb(f"small{p}", [P, G2, SW], F32, c1) for p in range(NPAIR)]
            prod = sb("prod", [P, G2, T, HK], F32, c1)
            sc = sb("sc", [P, G2, HK], F32, c1)
            al = [sb(f"alpha{p}", [P, G2, H], F32, c1) for p in range(NPAIR)]
            pen = [sb(f"pen{p}", [P, G2, T], F32, c1) for p in range(NPAIR)]
            cand = sb("cand", [P, G2, T, H], F32, c1)
            top = sb("top", [P, G, T, H], F32, c1)
            mnew = sb("mnew", [P, G, T, H], F32, c1)
            ex = sb("ex", [P, 3 * G, T, H], F32, c1)
            MAX = sb("MAX", [P, NTILE, T, H], F32, c1)
            DEN = sb("DEN", [P, NTILE, T, H], F32, c1)
            own, exp_in, exp_out, blank, copied = (
                sem(n, c1) for n in ("own", "exp_in", "exp_out", "blank", "copied"))
            kept_out = [sem(f"kept_out{p}", c1) for p in range(NPAIR)]
            with nc.Block() as block:
                @block.sync
                def _(sp):
                    load_slots(sp, slot_typed, slot, slots_in, rows_in)

                @block.gpsimd
                def _(pool):
                    sweep(pool, lambda g, u, n, w, in_: gather_unit(
                        pool, u, n, t_rows, slot, rows, slots_in, rows_in, rows_free, marker))

                @block.scalar
                def _(act):
                    def store(at, p, n=G):
                        for table, mine, width in ((kept_rows, keep, D), (kept_scores, small, SW)):
                            act.dma_start(table[at, p, :, 0:2 * n * width].rearrange("o p n -> (o p) n"),
                                          mine[p][:, 0:2 * n].rearrange("p k w -> p (k w)")).then_inc(kept_out[p], 16)

                    def body(g, u, n, w, in_):
                        at = nc.s_assert_within((u - CAP) * (u < CAP) + CAP, 0, CAP)
                        for p in range(NPAIR):
                            for q in (2 * p, 2 * p + 1):
                                act.wait_ge(rows_in[q], in_)
                            act.wait_ge(kept_out[p], 32 * u + 32)
                            act.activation(keep[p][:, 0:2 * n], both_ranks(pairs[p][:], n)[:, :, 0:D],
                                           ACT.Copy).then_inc(copied, 1)
                            act.wait_ge(exp_in, u * NPAIR + (p + 1))
                            act.activation(ex[:, 0:3 * n], ex[:, 0:3 * n], ACT.Exp).then_inc(exp_out, 1)
                            act.wait_ge(copied, u * NPAIR + (p + 1))
                            store(bass.ds(at, 1), p, n)

                    act.wait_ge(blank, 2 * NPAIR)
                    for p in range(NPAIR):
                        store(slice(CAP, CAP + 1), p)
                    sweep(act, body)
                    units = bounds(act, UB + NGRP, 1, [NGRP], [unit_hi[NGRP]])[0]
                    for p in range(NPAIR):
                        act.wait_ge(kept_out[p], 32 * units + 32)
                        act.sem_inc(marker, 1)

                @block.vector
                def _(dve):
                    s = Steps(dve, own)
                    TT = dve.tensor_tensor
                    for p in range(NPAIR):
                        dve.memset(keep[p][:], 0.0).then_inc(blank, 1)
                        dve.memset(small[p][:], 0.0).then_inc(blank, 1)
                    s.go(dve.memset(MAX[:], NEG))
                    s.go(dve.memset(DEN[:], 0.0))
                    s.need(s.n)
                    dve.wait_ge(blank, 2 * NPAIR)
                    for q in range(RB):
                        dve.sem_inc(rows_free[q], 1)

                    def score(g, u, n, in_, p):
                        R, m = pairs[p][:], 2 * n
                        oh = both_ranks(R, n)[:, :, D + HK:TW]
                        for q in (2 * p, 2 * p + 1):
                            dve.wait_ge(rows_in[q], in_)
                        dve.wait_ge(kept_out[p], 32 * u + 32)
                        s.go(dve.tensor_copy(small[p][:, 0:m, H:SW], oh))
                        s.go(dve.tensor_scalar(pen[p][:, 0:m], oh, -1.0, -NEG, ALU.add, ALU.mult))
                        yield
                        yield from scores(s, dve, R, g, n, prod, sc, al[p])
                        s.go(dve.tensor_copy(small[p][:, 0:m, 0:H], al[p][:, 0:m]))
                        dve.wait_ge(copied, u * NPAIR + (p + 1))
                        dve.sem_inc(rows_free[2 * p], 1)
                        dve.sem_inc(rows_free[2 * p + 1], 1)

                    def add_up(g, u, n, p, side):
                        m = 2 * n
                        oh = small[p][:, 0:m, H:SW].unsqueeze(3).to_broadcast([P, m, T, H])
                        cd, e01, e2 = cand[:, 0:m], ex[:, 0:m], ex[:, m:m + n]
                        M, S = MAX[:, g * G:g * G + n], DEN[:, g * G:g * G + n]
                        tp, mn = top[:, 0:n], mnew[:, 0:n]

                        def link(ins):
                            t = s.go(ins)
                            next(side, None)
                            s.need(t)

                        link(TT(cd, al[p][:, 0:m].unsqueeze(2).to_broadcast([P, m, T, H]), oh, ALU.mult))
                        link(TT(cd, cd, pen[p][:, 0:m].unsqueeze(3).to_broadcast([P, m, T, H]), ALU.add))
                        link(TT(tp, cd[:, 0:n], cd[:, n:m], ALU.max))
                        link(TT(mn, M, tp, ALU.max))
                        s.go(TT(e01[:, 0:n], cd[:, 0:n], mn, ALU.subtract))
                        s.go(TT(e01[:, n:m], cd[:, n:m], mn, ALU.subtract))
                        s.link(TT(e2, M, mn, ALU.subtract))
                        dve.sem_inc(exp_in, 1)
                        link(dve.tensor_copy(M, mn))
                        next(side, None)
                        dve.wait_ge(exp_out, u * NPAIR + (p + 1))
                        s.go(TT(S, S, e2, ALU.mult))
                        link(TT(e01, e01, oh, ALU.mult))
                        link(TT(e01[:, 0:n], e01[:, 0:n], e01[:, n:m], ALU.add))
                        link(TT(S, S, e01[:, 0:n], ALU.add))
                        for _ in side:
                            pass

                    def body(g, u, n, w, in_):
                        s.restart()
                        for _ in score(g, u, n, in_, 0):
                            pass
                        for p in range(NPAIR):
                            add_up(g, u, n, p, score(g, u, n, in_, p + 1) if p + 1 < NPAIR else iter(()))

                    sweep(dve, body)
                    s.restart()
                    s.link(dve.tensor_copy(MX[:, :, :, 0, :], MAX[:]))
                    s.link(dve.tensor_scalar(MAX[:], DEN[:], 0.0, None, ALU.is_equal))
                    s.link(TT(DEN[:], DEN[:], MAX[:], ALU.add))
                    s.link(dve.reciprocal(DEN[:], DEN[:]))
                    s.link(TT(MX[:, :, :, 1, :], DEN[:],
                              imp[:].unsqueeze(1).unsqueeze(3).to_broadcast([P, NTILE, T, H]), ALU.mult))

        def weights(s, dve, oh, al, g, n, prod, sel, wgt, exp_in, exp_out, turn):
            mx = MX[:, g * G:g * G + n].rearrange("p k t a h -> p k t (a h)")
            m = 2 * n
            for j in range(2):
                t = s.go(dve.tensor_tensor(prod[:, j * n:(j + 1) * n, :, 0:2 * H], mx,
                                           oh[:, j * n:(j + 1) * n].unsqueeze(3).to_broadcast([P, n, T, 2 * H]), ALU.mult))
            yield
            s.need(t)
            t = s.go(dve.tensor_reduce(sel[:, 0:m], prod[:, 0:m, :, 0:2 * H].rearrange("p k t n -> p k n t"), AX.X, ALU.add))
            yield
            s.need(t)
            t = s.go(dve.tensor_tensor(wgt[:, 0:m], al, sel[:, 0:m, 0:H], ALU.subtract))
            yield
            s.need(t)
            dve.sem_inc(exp_in, 1)
            yield
            dve.wait_ge(exp_out, turn)
            t = s.go(dve.tensor_tensor(wgt[:, 0:m], wgt[:, 0:m], sel[:, 0:m, H:2 * H], ALU.mult))
            yield
            s.need(t)

        for again in (False, True):
            with ExitStack() as c1:
                if again:
                    pairs, rows, slot, slots_in, rows_in, rows_free, marker = pair_memory(c1, TW)
                    sc = sb("sc", [P, G2, HK], F32, c1)
                    al = sb("al", [P, G2, H], F32, c1)
                else:
                    pairs = [sb(f"kept{p}", [P, G2, D], F32, c1) for p in range(NPAIR)]
                    small = [sb(f"kept_small{p}", [P, G2, SW], F32, c1) for p in range(NPAIR)]
                    kept_in, small_in, kept_free, small_free = (
                        [sem(f"{name}{p}", c1) for p in range(NPAIR)]
                        for name in ("kept_in", "small_in", "kept_free", "small_free"))
                prod = [sb(f"wprod{i}", [P, G2, T, HK], F32, c1) for i in range(2)]
                sel = [sb(f"sel{i}", [P, G2, 2 * H], F32, c1) for i in range(2)]
                wgt = [sb(f"wgt{i}", [P, G2, H], F32, c1) for i in range(2)]
                wrow = [sb(f"wrow{i}", [P, G2, D], F32, c1) for i in range(2)]
                acc = psum("acc", [P, 2, 1024], c1)
                own, exp_in, exp_out, weighted, added, closed, summed = (
                    sem(n, c1) for n in ("own", "exp_in", "exp_out", "weighted", "added", "closed", "summed"))

                if again:
                    parts = [[(CB + g, G)] for g in range(NGRP)]
                    hi = [max(n - CAP, 0) for n in unit_hi]
                else:
                    parts = [[(BB, G), (BB + 1, 1)]] + [[(BB + 1 + g, G)] for g in range(1, NGRP)]
                    hi = [min(n, CAP) for n in (unit_hi[0], *unit_hi[1:2], *unit_hi[1:])]

                def part_bounds(eng):
                    return bounds(eng, parts[0][0][0], len(hi), [0] * len(hi), hi)

                def each_unit(eng, body, after=None, before=None):
                    pb = part_bounds(eng)
                    for g in range(NGRP):
                        if before:
                            before(g)
                        for at, n in parts[g]:
                            at -= parts[0][0][0]
                            with eng.If(pb[at] < pb[at + 1]):
                                with eng.Fori(pb[at], pb[at + 1]) as u:
                                    body(g, u, n)
                        if after:
                            after(g, pb[at + 1])

                with nc.Block() as block:
                    @block.sync
                    def _(sp):
                        if again:
                            last = part_bounds(sp)[-1]
                            with sp.If(0 < last):
                                load_slots(sp, slot_typed, slot, slots_in, rows_in, last, CAP)
                        else:
                            def body(g, u, n):
                                for free, mine, table, there, width in (
                                        (small_free, small, kept_scores, small_in, SW),
                                        (kept_free, pairs, kept_rows, kept_in, D)):
                                    for p in range(NPAIR):
                                        sp.wait_ge(free[p], u + 1)
                                        sp.dma_start(mine[p][:, 0:2 * n].rearrange("p k w -> p (k w)"),
                                                     table[bass.ds(u, 1), p, :, 0:2 * n * width]
                                                     .rearrange("o p n -> (o p) n")
                                                     ).then_inc(there[p], 16)

                            each_unit(sp, body)

                    if again:
                        @block.gpsimd
                        def _(pool):
                            each_unit(pool, lambda g, u, n: gather_unit(pool, u, n, t_rows, slot, rows, slots_in, rows_in,
                                                                     rows_free, marker))

                    @block.scalar
                    def _(act):
                        def body(g, u, n):
                            for p in range(NPAIR):
                                act.wait_ge(exp_in, u * NPAIR + (p + 1))
                                act.activation(wgt[p][:, 0:2 * n], wgt[p][:, 0:2 * n], ACT.Exp).then_inc(exp_out, 1)

                        each_unit(act, body)

                    @block.tensor
                    def _(pe):
                        def clear(g):
                            if g >= 2:
                                pe.wait_ge(summed, g - 1)
                            clear_sums(pe, acc[:, g % 2, :])

                        def body(g, u, n):
                            for p in range(NPAIR):
                                pe.wait_ge(weighted, u * NPAIR + (p + 1))
                                add_rows(pe, acc[:, g % 2, :], wrow[p][:, 0:n], n)
                                add_rows(pe, acc[:, g % 2, :], wrow[p][:, n:2 * n], n).then_inc(added, 1)

                        each_unit(pe, body, before=clear, after=lambda g, units: pe.matmul(
                            acc[:, g % 2, 5 * P:6 * P], ident[:], zeros[:, 0:P], start=True, stop=True,
                            skip_group_check=True).then_inc(closed, 1))

                    @block.vector
                    def _(dve):
                        s = Steps(dve, own)
                        TT = dve.tensor_tensor
                        if again:
                            for q in range(RB):
                                dve.sem_inc(rows_free[q], 1)
                        else:
                            for p in range(NPAIR):
                                dve.sem_inc(small_free[p], 1)
                                dve.sem_inc(kept_free[p], 1)
                        dve.sem_inc(added, NPAIR)

                        def pair(g, u, n, p):
                            m = 2 * n
                            if again:
                                for q in (2 * p, 2 * p + 1):
                                    dve.wait_ge(rows_in[q], (16 * G) * u + 16 * G)
                                for _ in scores(s, dve, pairs[p][:], g, n, prod[p], sc, al):
                                    pass
                                R = both_ranks(pairs[p][:])
                                oh, score = R[:, :, D + HK:TW], al[:]
                            else:
                                dve.wait_ge(small_in[p], 16 * u + 16)
                                R = pairs[p][:]
                                oh, score = small[p][:, 0:m, H:SW], small[p][:, 0:m, 0:H]
                            yield from weights(s, dve, oh, score, g, n, prod[p], sel[p], wgt[p], exp_in, exp_out,
                                               u * NPAIR + (p + 1))
                            if not again:
                                dve.sem_inc(small_free[p], 1)
                                dve.wait_ge(kept_in[p], 16 * u + 16)
                            dve.wait_ge(added, u * NPAIR + (p + 1))
                            s.link(TT(wrow[p][:, 0:m].rearrange("p k (h c) -> p k h c", h=H),
                                      R[:, 0:m, 0:D].rearrange("p k (h c) -> p k h c", h=H),
                                      wgt[p][:, 0:m].unsqueeze(3).to_broadcast([P, m, H, C]), ALU.mult))
                            dve.sem_inc(weighted, 1)
                            if again:
                                dve.sem_inc(rows_free[2 * p], 1)
                                dve.sem_inc(rows_free[2 * p + 1], 1)
                            else:
                                dve.sem_inc(kept_free[p], 1)

                        def body(g, u, n):
                            s.restart()
                            chains = [pair(g, u, n, p) for p in range(NPAIR)]
                            if again:
                                for chain in chains:
                                    for _ in chain:
                                        pass
                            else:
                                for _ in zip_longest(*chains):
                                    pass

                        def take(g, n):
                            s.restart()
                            dve.wait_ge(closed, g + 1)
                            dve.wait_ge(added, n * NPAIR + NPAIR)
                            s.link(TT(RES[:, cols(g), :], RES[:, cols(g), :],
                                      acc[:, g % 2, 0:5 * P].rearrange("p (k d) -> p k d", k=G), ALU.add))
                            dve.sem_inc(summed, 1)

                        each_unit(dve, body, after=take)

        with ExitStack() as c1:
            sq = sb("sq", [P, G, D], F32, c1)
            st = sb("st", [P, 4, G], F32, c1)
            own, std_in, std_out = (sem(n, c1) for n in ("own", "std_in", "std_out"))
            with nc.Block() as block:
                @block.scalar
                def _(act):
                    for g in range(NGRP):
                        roots(act, st, std_in, std_out, g)

                @block.vector
                def _(dve):
                    s = Steps(dve, own)
                    for g in range(NGRP):
                        normalise(s, dve, g, RES, sq, st, std_in, std_out, g)
                        s.link(dve.tensor_copy(X[:, cols(g), :], RES[:, cols(g), :]))

        with ExitStack() as c1:
            Wa = sb("Wa", [P, 2, D], F32, c1)
            Wb = sb("Wb", [P, D], F32, c1)
            b1 = sb("b1", [P, 1], F32, c1)
            b2 = sb("b2", [P, D], F32, c1)
            inT = [sb(f"inT{i}", [P, 2 * D], F32, c1) for i in range(2)]
            hT = [sb(f"hT{i}", [P, D], F32, c1) for i in range(2)]
            sq = sb("sq", [P, G, D], F32, c1)
            st = sb("st", [P, 4, G], F32, c1)
            in_ps = psum("in_ps", [P, 2, 512], c1)
            h_ps = psum("h_ps", [P, 2, 512], c1)
            y_ps = psum("y_ps", [P, 2, 512], c1)
            signals = [sem(n, c1) for n in ("loaded", "own", "turned", "kept", "hidden", "active", "outed", "taken",
                                            "std_in", "std_out", "normed")]
            loaded, own, turned, kept, hidden, active, outed, taken, std_in, std_out, normed = signals
            with nc.Block() as block:
                @block.sync
                def _(sp):
                    for one in signals:
                        sp.sem_clear(one)
            with nc.Block() as block:
                @block.sync
                def _(sp):
                    sp.dma_start(Wa[:], W1m.rearrange("(a i) o -> i a o", a=2)).then_inc(loaded, 16)
                    sp.dma_start(Wb[:], W2m).then_inc(loaded, 16)
                    sp.dma_start(b1[:], b1m.rearrange("(d o) -> d o", o=1)).then_inc(loaded, 16)
                    sp.dma_start(b2[:], b2m.rearrange("(o d) -> o d", o=1).to_broadcast([P, D])).then_inc(loaded, 16)

                @block.tensor
                def _(pe):
                    def turn(t):
                        pe.transpose(in_ps[:, t % 2, 0:D], X[:, t, :], ident[:])
                        pe.transpose(in_ps[:, t % 2, D:2 * D], ATT[:, t, :], ident[:]).then_inc(turned, 1)

                    def first(t):
                        pe.wait_ge(kept, t + 1)
                        pe.matmul(h_ps[:, t % 2, 0:D], Wa[:, 0, :], inT[t % 2][:, 0:D], start=True, stop=False)
                        pe.matmul(h_ps[:, t % 2, 0:D], Wa[:, 1, :], inT[t % 2][:, D:2 * D], start=False,
                                  stop=True).then_inc(hidden, 1)

                    def second(t):
                        pe.wait_ge(active, t + 1)
                        if t >= 2:
                            pe.wait_ge(taken, t - 1)
                        pe.matmul(y_ps[:, t % 2, 0:D], hT[t % 2][:], Wb[:], start=True, stop=True).then_inc(outed, 1)

                    pe.wait_ge(loaded, 64)
                    turn(0)
                    for t in range(NTILE):
                        if t + 1 < NTILE:
                            turn(t + 1)
                        first(t)
                        if t:
                            second(t - 1)
                    second(NTILE - 1)

                @block.scalar
                def _(act):
                    def keep_turned(t):
                        act.wait_ge(turned, t + 1)
                        act.activation(inT[t % 2][:], in_ps[:, t % 2, 0:2 * D], ACT.Copy).then_inc(kept, 1)

                    act.wait_ge(loaded, 64)
                    keep_turned(0)
                    for t in range(NTILE):
                        if t + 1 < NTILE:
                            keep_turned(t + 1)
                        act.wait_ge(hidden, t + 1)
                        act.activation(hT[t % 2][:], h_ps[:, t % 2, 0:D], ACT.Relu, bias=b1[:, 0:1]).then_inc(active, 1)
                        if t >= G and t % G == 0:
                            roots(act, st, std_in, std_out, t // G - 1)
                    roots(act, st, std_in, std_out, NGRP - 1)

                @block.vector
                def _(dve):
                    s = Steps(dve, own)
                    dve.wait_ge(loaded, 64)
                    for g in range(NGRP):
                        for t in range(g * G, g * G + G):
                            s.link(dve.tensor_tensor(RES[:, t, :], X[:, t, :], b2[:], ALU.add))
                            dve.wait_ge(outed, t + 1)
                            s.link(dve.tensor_tensor(RES[:, t, :], RES[:, t, :], y_ps[:, t % 2, 0:D], ALU.add))
                            dve.sem_inc(taken, 1)
                        normalise(s, dve, g, RES, sq, st, std_in, std_out, g)
                        dve.sem_inc(normed, 1)

                @block.gpsimd
                def _(pool):
                    for g in range(NGRP):
                        pool.wait_ge(normed, g + 1)
                        for k in range(G):
                            t = g * G + k
                            pool.indirect_dma_start(out, bass.IndirectOffsetOnAxis(ap=node[:, t, 2:3], axis=0),
                                                    RES[:, t, :], None, bounds_check=N - 1, oob_is_err=False
                                                    ).then_inc(out_stored, 16)
                    pool.wait_ge(out_stored, 16 * NTILE)


_INS = ['x', 'src', 'dst', 'edge_attr_128', 'edge_type_4', 'L2_gnn_W', 'L2_gnn_att_vectors',
        'L2_gnn_confounder_probs', 'L2_gnn_edge_importance', 'L2_gnn_bias', 'L3_gnn_W1', 'L3_gnn_b1',
        'L3_gnn_W2', 'L3_gnn_b2']
_OUTS = [((3125, 128), 'float32')]


def kernel(**inputs):
    import numpy as _np
    import concourse.bacc as _bacc
    from concourse import mybir as _mybir
    from concourse.bass_utils import run_bass_kernel_spmd as _run

    nc = _bacc.Bacc("TRN2", target_bir_lowering=False, num_devices=1)
    arrays, args = {}, []
    for name in _INS:
        a = _np.ascontiguousarray(inputs[name])
        arrays[f"in_{name}_dram"] = a
        args.append(nc.dram_tensor(f"in_{name}_dram", a.shape, _mybir.dt.from_np(a.dtype), kind="ExternalInput").ap())
    for i, (shape, dtype) in enumerate(_OUTS):
        dt = _mybir.dt.from_np(_np.dtype(dtype))
        args.append(nc.dram_tensor(f"out_{i}_dram", shape, dt, kind="ExternalOutput").ap())
    build_program(nc, *args)
    r = _run(nc, [arrays], core_ids=[0])
    got = tuple(r.results[0][f"out_{i}_dram"] for i in range(len(_OUTS)))
    return got[0]
```
